# Optimizing a Trainium2 kernel written in Bass

```python
import numpy as np
import jax
import jax.numpy as jnp

def _softmax(x, axis=-1):
    return jax.nn.softmax(x, axis=axis)
def _gelu(x):
    return jax.nn.gelu(x, approximate=True)
def _silu(x):
    return jax.nn.silu(x)
def _sigmoid(x):
    return jax.nn.sigmoid(x)
def _layernorm(x, axis=-1, eps=1e-5):
    m = jnp.mean(x, axis=axis, keepdims=True)
    v = jnp.var(x, axis=axis, keepdims=True)
    return (x - m) / jnp.sqrt(v + eps)
def _scatter_add(tgt, idx, src, axis=0):
    return tgt.at[idx].add(src)
def _segment_sum(src, seg, n):
    return jax.ops.segment_sum(src, seg, n)

kernel_name = 'mk_conv_preact_d4_conv_nchw96_45f794'

def setup_inputs(seed: int = 0):
    np.random.seed(seed)
    _w = jnp.asarray
    def _rec_inputs():
        import jax
        import jax.numpy as jnp
        _gk = jax.random.key(seed)
        x = 0.0001705 + 1 * jax.random.normal(jax.random.fold_in(_gk, 1), (2, 96, 48, 48), jnp.float32)
        return x
    x = _rec_inputs()
    def _L0_conv_setup():
        import jax, jax.numpy as jnp
        import numpy as np
        B, DM, H, W = (2, 96, 48, 48)
        E = 192
        R, N = (6, 16)

        def conv2d(x, w, b, groups=1, pad=0):
            out = jax.lax.conv_general_dilated(x, w, window_strides=(1, 1), padding=[(pad, pad), (pad, pad)], dimension_numbers=('NCHW', 'OIHW', 'NCHW'), feature_group_count=groups)
            return out + b[None, :, None, None]
        key = jax.random.key(seed)
        ks = jax.random.split(key, 24)
        f = lambda k, shape, s: jax.random.normal(k, shape, jnp.float32) * s
        inp = {'x': jax.random.normal(ks[0], (B, DM, H, W), jnp.float32), 'in_proj_w': f(ks[1], (2 * E, DM), 0.05), 'conv_w': f(ks[2], (E, 1, 3, 3), 0.2), 'conv_b': f(ks[3], (E,), 0.1), 'x_proj_w': f(ks[4], (4, R + 2 * N, E), 0.01), 'dt_proj_w': f(ks[5], (4, E, R), 0.01), 'dt_proj_b': jnp.full((4, E), -9.0) + f(ks[6], (4, E), 0.1), 'A_log': jnp.tile(jnp.log(jnp.arange(1, N + 1, dtype=jnp.float32))[None, None, :], (4, E, 1)), 'Ds': jnp.ones((4, E), jnp.float32), 'ln_g': jnp.ones(E, jnp.float32), 'ln_b': jnp.zeros(E, jnp.float32), 'c1_w': f(ks[7], (2 * E, E, 1, 1), 0.05), 'c1_b': jnp.zeros(2 * E), 'bn1_g': jnp.ones(2 * E), 'bn1_b': jnp.zeros(2 * E), 'bn1_m': jnp.zeros(2 * E), 'bn1_v': jnp.ones(2 * E), 'c2_w': f(ks[8], (2 * E, 1, 3, 3), 0.2), 'c2_b': jnp.zeros(2 * E), 'bn2_g': jnp.ones(2 * E), 'bn2_b': jnp.zeros(2 * E), 'bn2_m': jnp.zeros(2 * E), 'bn2_v': jnp.ones(2 * E), 'c3_w': f(ks[9], (E // 2, 2 * E, 1, 1), 0.05), 'c3_b': jnp.zeros(E // 2), 'se1_w': f(ks[10], (E // 4, E // 2), 0.1), 'se1_b': jnp.zeros(E // 4), 'se2_w': f(ks[11], (E // 2, E // 4), 0.1), 'se2_b': jnp.zeros(E // 2)}
        return inp
    _L0_conv_all = _L0_conv_setup()
    _L0_conv_in = {k: v for k, v in _L0_conv_all.items() if k in ('in_proj_w', 'conv_w', 'conv_b', 'x_proj_w', 'dt_proj_w', 'dt_proj_b', 'A_log', 'Ds', 'ln_g', 'ln_b', 'c1_w', 'c1_b', 'bn1_g', 'bn1_b', 'bn1_m', 'bn1_v', 'c2_w', 'c2_b', 'bn2_g', 'bn2_b', 'bn2_m', 'bn2_v', 'c3_w', 'c3_b', 'se1_w', 'se1_b', 'se2_w', 'se2_b', )}
    del _L0_conv_all

    def _L1_conv_setup():
        import jax, jax.numpy as jnp
        import numpy as np
        N, C, H, W, O = (4, 96, 32, 32, 96)
        K, PAD, SPARSITY = (3, 1, 0.9)
        key = jax.random.key(seed)
        kx, kw, km = jax.random.split(key, 3)
        x = jax.random.normal(kx, (N, C, H, W), dtype=jnp.float32)
        weight = jax.random.normal(kw, (O, C, C), dtype=jnp.float32) * 0.02
        bias = jnp.zeros((O,), dtype=jnp.float32)
        mask = (jax.random.uniform(km, (O, C, C)) > SPARSITY).astype(jnp.float32)
        mask = mask * (1.0 - jnp.eye(C, dtype=jnp.float32))[None, :, :]
        return {'x': x, 'weight': weight, 'bias': bias, 'mask': mask}
    _L1_conv_all = _L1_conv_setup()
    _L1_conv_in = {k: v for k, v in _L1_conv_all.items() if k in ('weight', 'bias', 'mask', )}
    del _L1_conv_all

    def _L2_conv_setup():
        import jax, jax.numpy as jnp
        import numpy as np
        import math
        ALPHA = 0.65
        KSIZE = 9

        def _make_y(size):
            ii = jnp.arange(size, dtype=jnp.float32)
            coords = jnp.stack(jnp.meshgrid(ii, ii, indexing='ij'), axis=-1)
            origin = jnp.array([size // 2, size // 2], dtype=jnp.float32)
            return coords - origin

        def _diffusion_kernel(diff_metric, t=1.0):
            y = _make_y(KSIZE)
            z = jnp.einsum('cij,hwj->chwi', diff_metric, y)
            r2 = jnp.sum(z * z, axis=-1)
            alpha = ALPHA
            teff = t ** (1.0 / alpha)
            c1 = 1.0 / math.gamma(1.0 + 1.0 / alpha)
            c2 = math.sqrt(2.0 * c1)
            val = 3.0 * (-2.0 + (1.0 + 2.0 * alpha) * c2) / ((1.0 + 2.0 * alpha) * (-2.0 * c1 + 3.0 * c2))
            tg = c1 * teff
            gauss = 1.0 / (4.0 * math.pi * tg) * jnp.exp(-r2 / (4.0 * tg))
            tp = c2 * math.sqrt(teff)
            poi = math.gamma(1.5) / math.pi ** 1.5 * tp / jnp.power(tp * tp + r2, 1.5)
            return val * gauss + (1.0 - val) * poi
        key = jax.random.key(seed)
        k1, k2 = jax.random.split(key)
        x = jax.random.normal(k1, (16, 96, 224, 224), dtype=jnp.float32)
        bound = math.sqrt(0.5)
        diff_metric = jax.random.uniform(k2, (96, 2, 2), dtype=jnp.float32, minval=-bound, maxval=bound)
        return {'x': x, 'diff_metric': diff_metric}
    _L2_conv_all = _L2_conv_setup()
    _L2_conv_in = {k: v for k, v in _L2_conv_all.items() if k in ('diff_metric', )}
    del _L2_conv_all

    def _L3_conv_setup():
        import jax, jax.numpy as jnp
        import numpy as np
        import math
        ALPHA_MIN, ALPHA_MAX = (0.1, 0.9)

        def _dis_s_np(N):
            s = np.zeros(N, dtype=np.float64)
            s[1] = 1.0
            s[N - 1] = 1.0
            idx = (np.arange(N)[:, None] - np.arange(N)[None, :]) % N
            S = s[idx] + np.diag(np.fft.fft(s).real)
            r = N // 2
            even = 1 - N % 2
            P = np.zeros((N, N))
            P[0, 0] = 1.0
            for i in range(1, r - even + 1):
                P[i, i] = 1 / math.sqrt(2)
                P[i, N - i] = 1 / math.sqrt(2)
            if even:
                P[r, r] = 1.0
            for i in range(r + 1, N):
                P[i, i] = -1 / math.sqrt(2)
                P[i, N - i] = 1 / math.sqrt(2)
            CS = P @ S @ P.T
            h = N // 2 + 1
            ec, vc = np.linalg.eigh(CS[:h, :h])
            es, vs = np.linalg.eigh(CS[h:, h:])
            vc = vc[:, np.argsort(-ec)]
            vs = vs[:, np.argsort(-es)]
            SC2 = P @ np.vstack([vc, np.zeros((N - h, h))])
            SS2 = P @ np.vstack([np.zeros((h, N - h)), vs])
            if N % 2 == 0:
                E = np.zeros((N, N + 1))
                SS2 = np.hstack([SS2, np.zeros((N, 1))])
                E[:, 0:N + 1:2] = SC2
                E[:, 1:N:2] = SS2
                E = np.delete(E, N - 1, axis=1)
            else:
                E = np.zeros((N, N))
                E[:, 0:N + 1:2] = SC2
                E[:, 1:N:2] = SS2
            return E.astype(np.float32)

        def _frft_mat(Np, alpha):
            Evec = jnp.asarray(_dis_s_np(Np), dtype=jnp.complex64)
            even = 1 - Np % 2
            l = np.concatenate([np.arange(Np - 1, dtype=np.float32), np.array([Np - 1 + even], dtype=np.float32)])
            theta = np.pi / 2 * alpha[:, None] * jnp.asarray(l)[None, :]
            phase = jax.lax.complex(jnp.cos(theta), -jnp.sin(theta))
            return Np ** 0.5 * jnp.einsum('ji,bj,jk->bik', Evec, phase.astype(jnp.complex64), Evec)

        def _frft2d(x, Fh, Fw):
            xc = jnp.fft.fftshift(x, axes=(2, 3)).astype(jnp.complex64)
            out = jnp.einsum('bij,bcjk->bcik', Fh, xc)
            out = jnp.einsum('bcij,bjk->bcik', out, Fw)
            return jnp.fft.fftshift(out, axes=(2, 3))

        def _mlp(v, w1, b1, w2, b2):
            return jax.nn.relu(v @ w1.T + b1) @ w2.T + b2

        def _gate(g, half):
            go, gi = (g[:, :half], g[:, half:])
            return jax.nn.sigmoid(go[:, :, None] * gi[:, None, :])

        def _group_conv(x, w, b, pad):
            N, Cin, H, W = x.shape
            Cout = w.shape[1]
            out = jax.lax.conv_general_dilated(x.reshape(1, N * Cin, H, W), w.reshape(N * Cout, Cin, w.shape[3], w.shape[4]), (1, 1), [(pad, pad), (pad, pad)], dimension_numbers=('NCHW', 'OIHW', 'NCHW'), feature_group_count=N)
            return out.reshape(N, Cout, out.shape[2], out.shape[3]) + b[None, :, None, None]

        def _forward(x, conv0_w, conv0_b, conv05_w, conv05_b, conv1_w, conv1_b, conv2_w, conv2_b, alpha_w1, alpha_b1, alpha_w2, alpha_b2, gfreq_w1, gfreq_b1, gfreq_w2, gfreq_b2, gsp_w1, gsp_b1, gsp_w2, gsp_b2, gfft_w1, gfft_b1, gfft_w2, gfft_b2):
            N, C, H, W = x.shape
            C0 = C // 3
            C1 = C - 2 * C0
            x_0, x_05, x_1 = (x[:, :C0], x[:, C0:C - C0], x[:, C - C0:])
            Y0 = _gate(_mlp(x_0.mean((2, 3)), gsp_w1, gsp_b1, gsp_w2, gsp_b2), C0)
            x_0 = _group_conv(x_0, conv0_w[None] * Y0[..., None, None], conv0_b, 1)
            gap = x_05.mean((2, 3))
            alpha = ALPHA_MIN + (ALPHA_MAX - ALPHA_MIN) * jax.nn.sigmoid(_mlp(gap, alpha_w1, alpha_b1, alpha_w2, alpha_b2))[:, 0]
            Y = _gate(_mlp(gap, gfreq_w1, gfreq_b1, gfreq_w2, gfreq_b2), 2 * C1)
            Fre = _frft2d(x_05, _frft_mat(H, alpha), _frft_mat(W, alpha))
            Mix = jnp.concatenate([Fre.real, Fre.imag], axis=1)
            Mix = _group_conv(Mix, conv05_w[None] * Y[..., None, None], conv05_b, 0)
            Fre_out = jax.lax.complex(Mix[:, :C1], Mix[:, C1:])
            IFRFT = jnp.abs(_frft2d(Fre_out, _frft_mat(H, -alpha), _frft_mat(W, -alpha))) / (H * W)
            Y1 = _gate(_mlp(x_1.mean((2, 3)), gfft_w1, gfft_b1, gfft_w2, gfft_b2), 2 * C0)
            fre = jnp.fft.rfft2(x_1)
            mix = jnp.concatenate([fre.real, fre.imag], axis=1)
            mix = _group_conv(mix, conv1_w[None] * Y1[..., None, None], conv1_b, 0)
            x_1 = jnp.fft.irfft2(jax.lax.complex(mix[:, :C0], mix[:, C0:]), s=(H, W))
            out = jnp.concatenate([x_0, IFRFT, x_1], axis=1)
            out = jax.lax.conv_general_dilated(out, conv2_w, (1, 1), [(1, 1), (1, 1)], dimension_numbers=('NCHW', 'OIHW', 'NCHW')) + conv2_b[None, :, None, None]
            return out
        key = jax.random.key(seed)
        N, C, H, W = (16, 96, 128, 128)
        C0 = C // 3
        C1 = C - 2 * C0
        hid = max(8, C1 // 4)
        ks = jax.random.split(key, 24)

        def rn(k, shape, s=0.05):
            return s * jax.random.normal(k, shape, dtype=jnp.float32)
        return {'x': jax.random.normal(ks[0], (N, C, H, W), dtype=jnp.float32), 'conv0_w': rn(ks[1], (C0, C0, 3, 3)), 'conv0_b': rn(ks[2], (C0,)), 'conv05_w': rn(ks[3], (2 * C1, 2 * C1, 1, 1)), 'conv05_b': rn(ks[4], (2 * C1,)), 'conv1_w': rn(ks[5], (2 * C0, 2 * C0, 1, 1)), 'conv1_b': rn(ks[6], (2 * C0,)), 'conv2_w': rn(ks[7], (C, C, 3, 3)), 'conv2_b': rn(ks[8], (C,)), 'alpha_w1': rn(ks[9], (hid, C1)), 'alpha_b1': rn(ks[10], (hid,)), 'alpha_w2': rn(ks[11], (1, hid), 0.5), 'alpha_b2': jnp.zeros((1,), jnp.float32), 'gfreq_w1': rn(ks[12], (hid, C1)), 'gfreq_b1': rn(ks[13], (hid,)), 'gfreq_w2': rn(ks[14], (4 * C1, hid)), 'gfreq_b2': rn(ks[15], (4 * C1,)), 'gsp_w1': rn(ks[16], (hid, C0)), 'gsp_b1': rn(ks[17], (hid,)), 'gsp_w2': rn(ks[18], (2 * C0, hid)), 'gsp_b2': rn(ks[19], (2 * C0,)), 'gfft_w1': rn(ks[20], (hid, C0)), 'gfft_b1': rn(ks[21], (hid,)), 'gfft_w2': rn(ks[22], (4 * C0, hid)), 'gfft_b2': rn(ks[23], (4 * C0,))}
    _L3_conv_all = _L3_conv_setup()
    _L3_conv_in = {k: v for k, v in _L3_conv_all.items() if k in ('conv0_w', 'conv0_b', 'conv05_w', 'conv05_b', 'conv1_w', 'conv1_b', 'conv2_w', 'conv2_b', 'alpha_w1', 'alpha_b1', 'alpha_w2', 'alpha_b2', 'gfreq_w1', 'gfreq_b1', 'gfreq_w2', 'gfreq_b2', 'gsp_w1', 'gsp_b1', 'gsp_w2', 'gsp_b2', 'gfft_w1', 'gfft_b1', 'gfft_w2', 'gfft_b2', )}
    del _L3_conv_all

    return {
        "x": x,
        "L0_conv_in_proj_w": _L0_conv_in["in_proj_w"],
        "L0_conv_conv_w": _L0_conv_in["conv_w"],
        "L0_conv_conv_b": _L0_conv_in["conv_b"],
        "L0_conv_x_proj_w": _L0_conv_in["x_proj_w"],
        "L0_conv_dt_proj_w": _L0_conv_in["dt_proj_w"],
        "L0_conv_dt_proj_b": _L0_conv_in["dt_proj_b"],
        "L0_conv_A_log": _L0_conv_in["A_log"],
        "L0_conv_Ds": _L0_conv_in["Ds"],
        "L0_conv_ln_g": _L0_conv_in["ln_g"],
        "L0_conv_ln_b": _L0_conv_in["ln_b"],
        "L0_conv_c1_w": _L0_conv_in["c1_w"],
        "L0_conv_c1_b": _L0_conv_in["c1_b"],
        "L0_conv_bn1_g": _L0_conv_in["bn1_g"],
        "L0_conv_bn1_b": _L0_conv_in["bn1_b"],
        "L0_conv_bn1_m": _L0_conv_in["bn1_m"],
        "L0_conv_bn1_v": _L0_conv_in["bn1_v"],
        "L0_conv_c2_w": _L0_conv_in["c2_w"],
        "L0_conv_c2_b": _L0_conv_in["c2_b"],
        "L0_conv_bn2_g": _L0_conv_in["bn2_g"],
        "L0_conv_bn2_b": _L0_conv_in["bn2_b"],
        "L0_conv_bn2_m": _L0_conv_in["bn2_m"],
        "L0_conv_bn2_v": _L0_conv_in["bn2_v"],
        "L0_conv_c3_w": _L0_conv_in["c3_w"],
        "L0_conv_c3_b": _L0_conv_in["c3_b"],
        "L0_conv_se1_w": _L0_conv_in["se1_w"],
        "L0_conv_se1_b": _L0_conv_in["se1_b"],
        "L0_conv_se2_w": _L0_conv_in["se2_w"],
        "L0_conv_se2_b": _L0_conv_in["se2_b"],
        "L1_conv_weight": _L1_conv_in["weight"],
        "L1_conv_bias": _L1_conv_in["bias"],
        "L1_conv_mask": _L1_conv_in["mask"],
        "L2_conv_diff_metric": _L2_conv_in["diff_metric"],
        "L3_conv_conv0_w": _L3_conv_in["conv0_w"],
        "L3_conv_conv0_b": _L3_conv_in["conv0_b"],
        "L3_conv_conv05_w": _L3_conv_in["conv05_w"],
        "L3_conv_conv05_b": _L3_conv_in["conv05_b"],
        "L3_conv_conv1_w": _L3_conv_in["conv1_w"],
        "L3_conv_conv1_b": _L3_conv_in["conv1_b"],
        "L3_conv_conv2_w": _L3_conv_in["conv2_w"],
        "L3_conv_conv2_b": _L3_conv_in["conv2_b"],
        "L3_conv_alpha_w1": _L3_conv_in["alpha_w1"],
        "L3_conv_alpha_b1": _L3_conv_in["alpha_b1"],
        "L3_conv_alpha_w2": _L3_conv_in["alpha_w2"],
        "L3_conv_alpha_b2": _L3_conv_in["alpha_b2"],
        "L3_conv_gfreq_w1": _L3_conv_in["gfreq_w1"],
        "L3_conv_gfreq_b1": _L3_conv_in["gfreq_b1"],
        "L3_conv_gfreq_w2": _L3_conv_in["gfreq_w2"],
        "L3_conv_gfreq_b2": _L3_conv_in["gfreq_b2"],
        "L3_conv_gsp_w1": _L3_conv_in["gsp_w1"],
        "L3_conv_gsp_b1": _L3_conv_in["gsp_b1"],
        "L3_conv_gsp_w2": _L3_conv_in["gsp_w2"],
        "L3_conv_gsp_b2": _L3_conv_in["gsp_b2"],
        "L3_conv_gfft_w1": _L3_conv_in["gfft_w1"],
        "L3_conv_gfft_b1": _L3_conv_in["gfft_b1"],
        "L3_conv_gfft_w2": _L3_conv_in["gfft_w2"],
        "L3_conv_gfft_b2": _L3_conv_in["gfft_b2"],
    }

def reference(x, L0_conv_in_proj_w, L0_conv_conv_w, L0_conv_conv_b, L0_conv_x_proj_w, L0_conv_dt_proj_w, L0_conv_dt_proj_b, L0_conv_A_log, L0_conv_Ds, L0_conv_ln_g, L0_conv_ln_b, L0_conv_c1_w, L0_conv_c1_b, L0_conv_bn1_g, L0_conv_bn1_b, L0_conv_bn1_m, L0_conv_bn1_v, L0_conv_c2_w, L0_conv_c2_b, L0_conv_bn2_g, L0_conv_bn2_b, L0_conv_bn2_m, L0_conv_bn2_v, L0_conv_c3_w, L0_conv_c3_b, L0_conv_se1_w, L0_conv_se1_b, L0_conv_se2_w, L0_conv_se2_b, L1_conv_weight, L1_conv_bias, L1_conv_mask, L2_conv_diff_metric, L3_conv_conv0_w, L3_conv_conv0_b, L3_conv_conv05_w, L3_conv_conv05_b, L3_conv_conv1_w, L3_conv_conv1_b, L3_conv_conv2_w, L3_conv_conv2_b, L3_conv_alpha_w1, L3_conv_alpha_b1, L3_conv_alpha_w2, L3_conv_alpha_b2, L3_conv_gfreq_w1, L3_conv_gfreq_b1, L3_conv_gfreq_w2, L3_conv_gfreq_b2, L3_conv_gsp_w1, L3_conv_gsp_b1, L3_conv_gsp_w2, L3_conv_gsp_b2, L3_conv_gfft_w1, L3_conv_gfft_b1, L3_conv_gfft_w2, L3_conv_gfft_b2):
    import jax
    import jax.numpy as jnp
    def _L0_conv_ref(x, in_proj_w, conv_w, conv_b, x_proj_w, dt_proj_w, dt_proj_b, A_log, Ds, ln_g, ln_b, c1_w, c1_b, bn1_g, bn1_b, bn1_m, bn1_v, c2_w, c2_b, bn2_g, bn2_b, bn2_m, bn2_v, c3_w, c3_b, se1_w, se1_b, se2_w, se2_b):
        import jax, jax.numpy as jnp
        import numpy as np
        B, DM, H, W = (2, 96, 48, 48)
        E = 192
        R, N = (6, 16)

        def conv2d(x, w, b, groups=1, pad=0):
            out = jax.lax.conv_general_dilated(x, w, window_strides=(1, 1), padding=[(pad, pad), (pad, pad)], dimension_numbers=('NCHW', 'OIHW', 'NCHW'), feature_group_count=groups)
            return out + b[None, :, None, None]
        Bs, _, Hs, Ws = x.shape
        L = Hs * Ws
        xz = jnp.einsum('bchw,oc->bohw', x, in_proj_w)
        xi, z = jnp.split(xz, 2, axis=1)
        xi = jax.nn.silu(conv2d(xi, conv_w, conv_b, groups=E, pad=1))
        xf = xi.reshape(Bs, E, L)
        xt = jnp.swapaxes(xi, 2, 3).reshape(Bs, E, L)
        xs = jnp.stack([xf, xf[..., ::-1], xt, xt[..., ::-1]], axis=1)
        dbc = jnp.einsum('bkcl,krc->bkrl', xs, x_proj_w)
        dlt, b, c = (dbc[:, :, :R], dbc[:, :, R:R + N], dbc[:, :, R + N:])
        dlt = jnp.einsum('bkrl,kdr->bkdl', dlt, dt_proj_w) + dt_proj_b[None, :, :, None]
        dlt = jax.nn.softplus(dlt)
        dA = dlt[..., None] * A_log[None, :, :, None, :]
        phi = jnp.exp(-jnp.cumsum(dA, axis=3))
        dbx = dlt[..., None] * jnp.swapaxes(b, 2, 3)[:, :, None] * xs[..., None]
        h = phi * jnp.cumsum(dbx / (phi + 1e-12), axis=3)
        y = jnp.einsum('bkdln,bknl->bkdl', h, c) + Ds[None, :, :, None]
        y1 = y[:, 0]
        y2 = y[:, 1, :, ::-1]
        y3 = jnp.swapaxes(y[:, 2].reshape(Bs, E, Ws, Hs), 2, 3).reshape(Bs, E, L)
        y4 = jnp.swapaxes(y[:, 3, :, ::-1].reshape(Bs, E, Ws, Hs), 2, 3).reshape(Bs, E, L)
        ys = (y1 + y2 + y3 + y4).reshape(Bs, E, Hs, Ws)
        yn = jnp.moveaxis(ys, 1, -1)
        mu = yn.mean(-1, keepdims=True)
        var = yn.var(-1, keepdims=True)
        yn = (yn - mu) / jnp.sqrt(var + 1e-05) * ln_g + ln_b
        u = jnp.moveaxis(yn, -1, 1) * z

        def bn(t, g, bb, m, v):
            return (t - m[None, :, None, None]) / jnp.sqrt(v + 1e-05)[None, :, None, None] * g[None, :, None, None] + bb[None, :, None, None]
        t = jax.nn.relu(bn(conv2d(u, c1_w, c1_b), bn1_g, bn1_b, bn1_m, bn1_v))
        t = jax.nn.relu(bn(conv2d(t, c2_w, c2_b, groups=2 * E, pad=1), bn2_g, bn2_b, bn2_m, bn2_v))
        t = conv2d(t, c3_w, c3_b)
        s = t.mean((2, 3))
        s = jax.nn.relu(s @ se1_w.T + se1_b)
        s = jax.nn.sigmoid(s @ se2_w.T + se2_b)
        return t + t * s[:, :, None, None]

    def _L1_conv_ref(x, weight, bias, mask):
        import jax, jax.numpy as jnp
        import numpy as np
        N, C, H, W, O = (4, 96, 32, 32, 96)
        K, PAD, SPARSITY = (3, 1, 0.9)
        n, c, h, w = x.shape
        s = jax.lax.reduce_window(x, 0.0, jax.lax.add, window_dimensions=(1, 1, K, K), window_strides=(1, 1, 1, 1), padding=((0, 0), (0, 0), (PAD, PAD), (PAD, PAD)))
        p = s / float(K * K)
        ho, wo = (p.shape[2], p.shape[3])
        p = p.reshape(n, c, ho * wo).transpose(0, 2, 1)
        wm = weight * mask
        t = jnp.einsum('nlc,ocd->nlod', p, wm)
        y = jnp.einsum('nlod,nld->nlo', t, p)
        y = y + bias[None, None, :]
        return y.transpose(0, 2, 1).reshape(n, -1, ho, wo)

    def _L2_conv_ref(x, diff_metric):
        import jax, jax.numpy as jnp
        import numpy as np
        import math
        ALPHA = 0.65
        KSIZE = 9

        def _make_y(size):
            ii = jnp.arange(size, dtype=jnp.float32)
            coords = jnp.stack(jnp.meshgrid(ii, ii, indexing='ij'), axis=-1)
            origin = jnp.array([size // 2, size // 2], dtype=jnp.float32)
            return coords - origin

        def _diffusion_kernel(diff_metric, t=1.0):
            y = _make_y(KSIZE)
            z = jnp.einsum('cij,hwj->chwi', diff_metric, y)
            r2 = jnp.sum(z * z, axis=-1)
            alpha = ALPHA
            teff = t ** (1.0 / alpha)
            c1 = 1.0 / math.gamma(1.0 + 1.0 / alpha)
            c2 = math.sqrt(2.0 * c1)
            val = 3.0 * (-2.0 + (1.0 + 2.0 * alpha) * c2) / ((1.0 + 2.0 * alpha) * (-2.0 * c1 + 3.0 * c2))
            tg = c1 * teff
            gauss = 1.0 / (4.0 * math.pi * tg) * jnp.exp(-r2 / (4.0 * tg))
            tp = c2 * math.sqrt(teff)
            poi = math.gamma(1.5) / math.pi ** 1.5 * tp / jnp.power(tp * tp + r2, 1.5)
            return val * gauss + (1.0 - val) * poi
        C = x.shape[1]
        kern = _diffusion_kernel(diff_metric, t=1.0)
        rhs = kern[:, None, :, :]
        return jax.lax.conv_general_dilated(x, rhs, window_strides=(1, 1), padding='SAME', dimension_numbers=('NCHW', 'OIHW', 'NCHW'), feature_group_count=C)

    def _L3_conv_ref(x, conv0_w, conv0_b, conv05_w, conv05_b, conv1_w, conv1_b, conv2_w, conv2_b, alpha_w1, alpha_b1, alpha_w2, alpha_b2, gfreq_w1, gfreq_b1, gfreq_w2, gfreq_b2, gsp_w1, gsp_b1, gsp_w2, gsp_b2, gfft_w1, gfft_b1, gfft_w2, gfft_b2):
        import jax, jax.numpy as jnp
        import numpy as np
        import math
        ALPHA_MIN, ALPHA_MAX = (0.1, 0.9)

        def _dis_s_np(N):
            s = np.zeros(N, dtype=np.float64)
            s[1] = 1.0
            s[N - 1] = 1.0
            idx = (np.arange(N)[:, None] - np.arange(N)[None, :]) % N
            S = s[idx] + np.diag(np.fft.fft(s).real)
            r = N // 2
            even = 1 - N % 2
            P = np.zeros((N, N))
            P[0, 0] = 1.0
            for i in range(1, r - even + 1):
                P[i, i] = 1 / math.sqrt(2)
                P[i, N - i] = 1 / math.sqrt(2)
            if even:
                P[r, r] = 1.0
            for i in range(r + 1, N):
                P[i, i] = -1 / math.sqrt(2)
                P[i, N - i] = 1 / math.sqrt(2)
            CS = P @ S @ P.T
            h = N // 2 + 1
            ec, vc = np.linalg.eigh(CS[:h, :h])
            es, vs = np.linalg.eigh(CS[h:, h:])
            vc = vc[:, np.argsort(-ec)]
            vs = vs[:, np.argsort(-es)]
            SC2 = P @ np.vstack([vc, np.zeros((N - h, h))])
            SS2 = P @ np.vstack([np.zeros((h, N - h)), vs])
            if N % 2 == 0:
                E = np.zeros((N, N + 1))
                SS2 = np.hstack([SS2, np.zeros((N, 1))])
                E[:, 0:N + 1:2] = SC2
                E[:, 1:N:2] = SS2
                E = np.delete(E, N - 1, axis=1)
            else:
                E = np.zeros((N, N))
                E[:, 0:N + 1:2] = SC2
                E[:, 1:N:2] = SS2
            return E.astype(np.float32)

        def _frft_mat(Np, alpha):
            Evec = jnp.asarray(_dis_s_np(Np), dtype=jnp.complex64)
            even = 1 - Np % 2
            l = np.concatenate([np.arange(Np - 1, dtype=np.float32), np.array([Np - 1 + even], dtype=np.float32)])
            theta = np.pi / 2 * alpha[:, None] * jnp.asarray(l)[None, :]
            phase = jax.lax.complex(jnp.cos(theta), -jnp.sin(theta))
            return Np ** 0.5 * jnp.einsum('ji,bj,jk->bik', Evec, phase.astype(jnp.complex64), Evec)

        def _frft2d(x, Fh, Fw):
            xc = jnp.fft.fftshift(x, axes=(2, 3)).astype(jnp.complex64)
            out = jnp.einsum('bij,bcjk->bcik', Fh, xc)
            out = jnp.einsum('bcij,bjk->bcik', out, Fw)
            return jnp.fft.fftshift(out, axes=(2, 3))

        def _mlp(v, w1, b1, w2, b2):
            return jax.nn.relu(v @ w1.T + b1) @ w2.T + b2

        def _gate(g, half):
            go, gi = (g[:, :half], g[:, half:])
            return jax.nn.sigmoid(go[:, :, None] * gi[:, None, :])

        def _group_conv(x, w, b, pad):
            N, Cin, H, W = x.shape
            Cout = w.shape[1]
            out = jax.lax.conv_general_dilated(x.reshape(1, N * Cin, H, W), w.reshape(N * Cout, Cin, w.shape[3], w.shape[4]), (1, 1), [(pad, pad), (pad, pad)], dimension_numbers=('NCHW', 'OIHW', 'NCHW'), feature_group_count=N)
            return out.reshape(N, Cout, out.shape[2], out.shape[3]) + b[None, :, None, None]

        def _forward(x, conv0_w, conv0_b, conv05_w, conv05_b, conv1_w, conv1_b, conv2_w, conv2_b, alpha_w1, alpha_b1, alpha_w2, alpha_b2, gfreq_w1, gfreq_b1, gfreq_w2, gfreq_b2, gsp_w1, gsp_b1, gsp_w2, gsp_b2, gfft_w1, gfft_b1, gfft_w2, gfft_b2):
            N, C, H, W = x.shape
            C0 = C // 3
            C1 = C - 2 * C0
            x_0, x_05, x_1 = (x[:, :C0], x[:, C0:C - C0], x[:, C - C0:])
            Y0 = _gate(_mlp(x_0.mean((2, 3)), gsp_w1, gsp_b1, gsp_w2, gsp_b2), C0)
            x_0 = _group_conv(x_0, conv0_w[None] * Y0[..., None, None], conv0_b, 1)
            gap = x_05.mean((2, 3))
            alpha = ALPHA_MIN + (ALPHA_MAX - ALPHA_MIN) * jax.nn.sigmoid(_mlp(gap, alpha_w1, alpha_b1, alpha_w2, alpha_b2))[:, 0]
            Y = _gate(_mlp(gap, gfreq_w1, gfreq_b1, gfreq_w2, gfreq_b2), 2 * C1)
            Fre = _frft2d(x_05, _frft_mat(H, alpha), _frft_mat(W, alpha))
            Mix = jnp.concatenate([Fre.real, Fre.imag], axis=1)
            Mix = _group_conv(Mix, conv05_w[None] * Y[..., None, None], conv05_b, 0)
            Fre_out = jax.lax.complex(Mix[:, :C1], Mix[:, C1:])
            IFRFT = jnp.abs(_frft2d(Fre_out, _frft_mat(H, -alpha), _frft_mat(W, -alpha))) / (H * W)
            Y1 = _gate(_mlp(x_1.mean((2, 3)), gfft_w1, gfft_b1, gfft_w2, gfft_b2), 2 * C0)
            fre = jnp.fft.rfft2(x_1)
            mix = jnp.concatenate([fre.real, fre.imag], axis=1)
            mix = _group_conv(mix, conv1_w[None] * Y1[..., None, None], conv1_b, 0)
            x_1 = jnp.fft.irfft2(jax.lax.complex(mix[:, :C0], mix[:, C0:]), s=(H, W))
            out = jnp.concatenate([x_0, IFRFT, x_1], axis=1)
            out = jax.lax.conv_general_dilated(out, conv2_w, (1, 1), [(1, 1), (1, 1)], dimension_numbers=('NCHW', 'OIHW', 'NCHW')) + conv2_b[None, :, None, None]
            return out
        return _forward(x, conv0_w, conv0_b, conv05_w, conv05_b, conv1_w, conv1_b, conv2_w, conv2_b, alpha_w1, alpha_b1, alpha_w2, alpha_b2, gfreq_w1, gfreq_b1, gfreq_w2, gfreq_b2, gsp_w1, gsp_b1, gsp_w2, gsp_b2, gfft_w1, gfft_b1, gfft_w2, gfft_b2)

    def _gn(v, G=32, eps=1e-5):
        B_, C_, H_, W_ = v.shape
        g = v.reshape(B_, G, C_ // G, H_, W_)
        m = jnp.mean(g, axis=(2, 3, 4), keepdims=True)
        s = jnp.var(g, axis=(2, 3, 4), keepdims=True)
        return ((g - m) / jnp.sqrt(s + eps)).reshape(v.shape)

    def _ln_c(v, eps=1e-6):
        m = jnp.mean(v, axis=1, keepdims=True)
        s = jnp.var(v, axis=1, keepdims=True)
        return (v - m) / jnp.sqrt(s + eps)

    def _ln_t(v, eps=1e-5):
        m = jnp.mean(v, axis=-1, keepdims=True)
        s = jnp.var(v, axis=-1, keepdims=True)
        return (v - m) / jnp.sqrt(s + eps)

    def _to_tokens(v):
        B_, C_, H_, W_ = v.shape
        return v.reshape(B_, C_, H_ * W_).transpose(0, 2, 1)
    def _from_tokens(t, like):
        B_, C_, H_, W_ = like.shape
        return t.transpose(0, 2, 1).reshape(B_, C_, H_, W_)

    x = x + _L0_conv_ref(_gn(x), L0_conv_in_proj_w, L0_conv_conv_w, L0_conv_conv_b, L0_conv_x_proj_w, L0_conv_dt_proj_w, L0_conv_dt_proj_b, L0_conv_A_log, L0_conv_Ds, L0_conv_ln_g, L0_conv_ln_b, L0_conv_c1_w, L0_conv_c1_b, L0_conv_bn1_g, L0_conv_bn1_b, L0_conv_bn1_m, L0_conv_bn1_v, L0_conv_c2_w, L0_conv_c2_b, L0_conv_bn2_g, L0_conv_bn2_b, L0_conv_bn2_m, L0_conv_bn2_v, L0_conv_c3_w, L0_conv_c3_b, L0_conv_se1_w, L0_conv_se1_b, L0_conv_se2_w, L0_conv_se2_b)
    x = x + _L1_conv_ref(_gn(x), L1_conv_weight, L1_conv_bias, L1_conv_mask)
    x = x + _L2_conv_ref(_gn(x), L2_conv_diff_metric)
    x = x + _L3_conv_ref(_gn(x), L3_conv_conv0_w, L3_conv_conv0_b, L3_conv_conv05_w, L3_conv_conv05_b, L3_conv_conv1_w, L3_conv_conv1_b, L3_conv_conv2_w, L3_conv_conv2_b, L3_conv_alpha_w1, L3_conv_alpha_b1, L3_conv_alpha_w2, L3_conv_alpha_b2, L3_conv_gfreq_w1, L3_conv_gfreq_b1, L3_conv_gfreq_w2, L3_conv_gfreq_b2, L3_conv_gsp_w1, L3_conv_gsp_b1, L3_conv_gsp_w2, L3_conv_gsp_b2, L3_conv_gfft_w1, L3_conv_gfft_b1, L3_conv_gfft_w2, L3_conv_gfft_b2)
    return x


_drawn_inputs = setup_inputs


def setup_inputs(seed=0):
    import zlib

    import numpy as np

    out = dict(_drawn_inputs(seed))
    spreads = {'L0_conv_Ds': (1.0, 0.2),
     'L0_conv_ln_g': (1.0, 0.2),
     'L0_conv_ln_b': (0.0, 0.58),
     'L0_conv_c1_b': (0.0, 0.1),
     'L0_conv_bn1_g': (1.0, 0.2),
     'L0_conv_bn1_b': (0.0, 0.1),
     'L0_conv_bn1_m': (0.0, 0.1),
     'L0_conv_bn1_v': (1.0, 0.2),
     'L0_conv_c2_b': (0.0, 0.1),
     'L0_conv_bn2_g': (1.0, 0.2),
     'L0_conv_bn2_b': (0.0, 0.1),
     'L0_conv_bn2_m': (0.0, 0.1),
     'L0_conv_bn2_v': (1.0, 0.2),
     'L0_conv_c3_b': (0.0, 0.1),
     'L0_conv_se1_b': (0.0, 0.8),
     'L0_conv_se2_b': (0.0, 0.8),
     'L1_conv_bias': (0.0, 0.1)}
    factors = {'L0_conv_conv_w': 8.0,
     'L0_conv_conv_b': 8.0,
     'L0_conv_x_proj_w': 8.0,
     'L0_conv_dt_proj_w': 8.0,
     'L0_conv_dt_proj_b': 8.0,
     'L0_conv_A_log': 8.0,
     'L0_conv_se1_w': 8.0,
     'L0_conv_se2_w': 8.0,
     'L3_conv_conv05_b': 64.0,
     'L3_conv_conv1_b': 64.0,
     'L3_conv_alpha_b1': 4.941,
     'L3_conv_gfreq_w1': 8.0,
     'L3_conv_gfreq_b1': 64.0,
     'L3_conv_gfreq_w2': 64.0,
     'L3_conv_gfreq_b2': 60.492,
     'L3_conv_gsp_w1': 8.0,
     'L3_conv_gsp_b1': 8.0,
     'L3_conv_gsp_w2': 8.0,
     'L3_conv_gsp_b2': 8.0,
     'L3_conv_gfft_w1': 27.816,
     'L3_conv_gfft_b1': 64.0,
     'L3_conv_gfft_w2': 8.0,
     'L3_conv_gfft_b2': 22.922}
    for name, (base, spread) in spreads.items():
        noise = np.random.default_rng([zlib.crc32(name.encode()), seed]).standard_normal(out[name].shape)
        drawn = base * np.exp(spread * noise) if base else spread * noise
        out[name] = jnp.asarray(drawn.astype(out[name].dtype))
    for name, factor in factors.items():
        out[name] = (out[name] * factor).astype(out[name].dtype)
    return out
```

```python
from contextlib import ExitStack
import math

import numpy as np

import concourse.bass as bass
from concourse import mybir

F32 = mybir.dt.float32
BF16 = mybir.dt.bfloat16
I32 = mybir.dt.int32
ALU = mybir.AluOpType
ACT = mybir.ActivationFunctionType
AX = mybir.AxisListType

B, C, H, W = 2, 96, 48, 48
L = H * W
E = 2 * C
T = B * E // 128
R, N = 6, 16
K = 4
CH = 8 * W
NC = L // CH
BANK = 512
SEG = 2 * CH
NSEG = L // SEG
PW = W + 2
LOG_FLOOR = math.log(1e12)
PAIR_ROWS = (C // 2) * C + C // 2
PT = -(-PAIR_ROWS // 128)
TAPS = 9
C3 = C // 3
HID = 8
UH = W // 2 + 1


class Steps:

    def __init__(self, eng, sem):
        self.eng, self.sem, self.n = eng, sem, 0

    def __call__(self, ins):
        self.n += 1
        ins.then_inc(self.sem, 1)
        self.eng.wait_ge(self.sem, self.n)


def space(nc, ctx, tag):
    numbers = []

    def sb(name, shape, dt=F32):
        return ctx.enter_context(nc.sbuf_tensor(f"{tag}_{name}", shape, dt))

    def sem(name):
        s = ctx.enter_context(nc.semaphore(f"{tag}_{name}"))
        numbers.append(s.num)
        return s

    def clear():
        run = []
        for n in sorted(numbers) + [None]:
            if run and n != run[-1] + 1:
                nc.gpsimd.sem_clear(range(run[0], run[-1] + 1))
                run = []
            run.append(n)

    ctx.callback(clear)
    return sb, sem


def by_image(ap):
    return ap.rearrange("p (h w) -> p h w", w=W)


def interior(pad, border=1):
    return pad[:, border:border + H, border:border + W]


def scan_order(ap, k):
    v = ap[:, ::-1] if k % 2 else ap
    return v.rearrange("p (w h) -> p h w", h=H) if k >= 2 else v.rearrange("p (h w) -> p h w", w=W)


def banks(ps, first, count):
    return ps[:, first * BANK:(first + count) * BANK].rearrange("p (c n) -> p c n", n=BANK)[:, :, 0:CH]


def banks_hw(ps, first, count):
    return banks(ps, first, count).rearrange("p c (h w) -> p c h w", w=W)


def rsqrt_newton(step, dve, out, v, t1, t2):
    step(dve.tensor_tensor(t1, out, out, ALU.mult))
    step(dve.tensor_tensor(t2, t1, v, ALU.mult))
    step(dve.tensor_scalar(t1, t2, -0.5, 1.5, ALU.mult, ALU.add))


def group_norm(nc, tag, X, ps, gavg, st, outs, eps=1e-5):
    with ExitStack() as ctx:
        sb, sem = space(nc, ctx, tag)
        bn = sb("bn", [C, B, NC, 6])
        d, sq, var, t1, t2 = (sb(n, [C, B]) for n in ("d", "sq", "var", "t1", "t2"))
        s_dve, s_stat, s_mean, s_spread, s_var, s_inv, s_root = map(
            sem, ("dve", "stat", "mean", "spread", "var", "inv", "root"))
        mv, rstd, shift = st["mv"], st["rstd"], st["shift"]
        block = ctx.enter_context(nc.Block())

        @block.vector
        def _(dve):
            step = Steps(dve, s_dve)
            for b in range(B):
                for c in range(NC):
                    last = dve.bn_stats(bn[:, b, c, :], X[:, b, c * CH:(c + 1) * CH])
                step(last)
                ins = dve.bn_aggr(mv[:, b, :], bn[:, b, :, :].rearrange("p c s -> p (c s)"))
                ins.then_inc(s_stat, 1)
            dve.wait_ge(s_stat, B)
            dve.wait_ge(s_mean, 1)
            step(dve.tensor_tensor(d[:, :], mv[:, :, 0], ps[0:C, 0:B], ALU.subtract))
            step(dve.tensor_tensor(sq[:, :], d[:, :], d[:, :], ALU.mult))
            dve.tensor_tensor(sq[:, :], sq[:, :], mv[:, :, 1], ALU.add).then_inc(s_spread, 1)
            dve.wait_ge(s_var, 1)
            step(dve.tensor_scalar(var[:, :], ps[0:C, BANK:BANK + B], eps, None, ALU.add))
            dve.reciprocal(t1[:, :], var[:, :]).then_inc(s_inv, 1)
            dve.wait_ge(s_root, 1)
            rsqrt_newton(step, dve, rstd[:, :], var[:, :], t1[:, :], t2[:, :])
            step(dve.tensor_tensor(rstd[:, :], rstd[:, :], t1[:, :], ALU.mult))
            step(dve.tensor_scalar(t2[:, :], ps[0:C, 0:B], -1.0, None, ALU.mult))
            step(dve.tensor_tensor(shift[:, :], t2[:, :], rstd[:, :], ALU.mult))
            for b in range(B):
                ins = dve.tensor_scalar(outs[b], by_image(X[:, b, :]), rstd[:, b:b + 1], shift[:, b:b + 1],
                                        ALU.mult, ALU.add)
            step(ins)

        @block.tensor
        def _(pe):
            pe.wait_ge(s_stat, B)
            pe.matmul(ps[0:C, 0:B], gavg[:, :], mv[:, :, 0], start=True, stop=True).then_inc(s_mean, 1)
            pe.wait_ge(s_spread, 1)
            pe.matmul(ps[0:C, BANK:BANK + B], gavg[:, :], sq[:, :], start=True, stop=True).then_inc(s_var, 1)

        @block.scalar
        def _(act):
            act.wait_ge(s_inv, 1)
            act.activation(rstd[:, :], t1[:, :], ACT.Sqrt).then_inc(s_root, 1)


def load(nc, tag, pairs):
    with ExitStack() as ctx:
        _, sem = space(nc, ctx, tag)
        s_in = sem("in")
        block = ctx.enter_context(nc.Block())

        @block.sync
        def _(sp):
            for dst, src in pairs:
                sp.dma_start(dst, src).then_inc(s_in, 16)
            sp.wait_ge(s_in, 16 * len(pairs))




def l0_project(nc, a, X, XG, ps, XI, Z):
    with ExitStack() as ctx:
        sb, sem = space(nc, ctx, "l0p")
        w_in = sb("w_in", [C, 2 * E])
        cw = sb("cw", [128, T, TAPS])
        cb = sb("cb", [128, T])
        pad = sb("pad", [128, T, PW, PW])
        acc = sb("acc", [128, T, L])
        s_in, s_pad, s_mm, s_ev, s_evz, s_tap = map(sem, ("in", "pad", "mm", "ev", "evz", "tap"))
        block = ctx.enter_context(nc.Block())
        parts = [[(0, 128, 0, 0)], [(0, 64, 128, 0), (64, 128, 0, 1)], [(0, 128, 64, 1)]]

        @block.sync
        def _(sp):
            sp.dma_start(w_in[:, :], a["w_in"]).then_inc(s_in, 16)
            sp.dma_start(cw[:, :, :], a["cw"]).then_inc(s_in, 16)
            sp.dma_start(cb[:, :], a["cb"]).then_inc(s_in, 16)
            sp.wait_ge(s_in, 48)

        @block.tensor
        def _(pe):
            pe.wait_ge(s_in, 48)
            for j in range(2 * T):
                half, t = divmod(j, T)
                for c in range(NC):
                    q = j * NC + c
                    if q >= 8:
                        pe.wait_ge(s_ev, q - 7)
                    for lo, hi, w0, b in parts[t]:
                        mm = pe.matmul(ps[lo:hi, (q % 8) * BANK:(q % 8) * BANK + CH],
                                       w_in[:, half * E + w0:half * E + w0 + hi - lo],
                                       XG[:, b, c * CH:(c + 1) * CH], start=True, stop=True)
                    mm.then_inc(s_mm, 1)

        @block.scalar
        def _(act):
            act.wait_ge(s_pad, T)
            for j in range(2 * T):
                half, t = divmod(j, T)
                for c in range(NC):
                    q = j * NC + c
                    act.wait_ge(s_mm, q + 1)
                    src = ps[:, (q % 8) * BANK:(q % 8) * BANK + CH]
                    if half:
                        act.copy(Z[:, t, c * CH:(c + 1) * CH], src).then_inc(s_ev, 1)
                    else:
                        act.copy(pad[:, t, 1 + 8 * c:9 + 8 * c, 1:1 + W],
                                 src.rearrange("p (h w) -> p h w", w=W)).then_inc(s_ev, 1)
            act.wait_ge(s_in, 48)
            for t in range(T):
                act.wait_ge(s_tap, TAPS * (t + 1))
                ins = act.activation(XI[:, t, :], acc[:, t, :], ACT.Silu, bias=cb[:, t:t + 1])
            ins.then_inc(s_evz, 1)
            act.wait_ge(s_evz, 1)

        @block.vector
        def _(dve):
            for t in range(T):
                dve.memset(pad[:, t, :, :], 0.0).then_inc(s_pad, 1)
            dve.wait_ge(s_in, 48)
            for t in range(T):
                dve.wait_ge(s_ev, NC * (t + 1))
                for i in range(TAPS):
                    dy, dx = divmod(i, 3)
                    src = pad[:, t, dy:dy + H, dx:dx + W]
                    dst = by_image(acc[:, t, :])
                    if i == 0:
                        ins = dve.tensor_scalar(dst, src, cw[:, t, 0:1], None, ALU.mult)
                    else:
                        dve.wait_ge(s_tap, TAPS * t + i)
                        ins = dve.scalar_tensor_tensor(dst, src, cw[:, t, i:i + 1], dst, ALU.mult, ALU.add)
                    ins.then_inc(s_tap, 1)


def l0_rows(nc, a, ps, XI, P, d):
    with ExitStack() as ctx:
        sb, sem = space(nc, ctx, "l0r")
        w_bc = sb("w_bc", [128, 2, T, 128])
        w_dt = sb("w_dt", [128, T, K * B * R])
        al = sb("al", [128, K * T, N])
        na = sb("na", [128, K * T, 2 * N])
        bc = sb("bc", [128, 2, L])
        rest = sb("rest", [128, L])
        parts = sb("parts", [128, 2, 3, L], BF16)
        s_in, s_bc, s_bce, s_hi, s_mid, s_lo, s_rest, s_pm, s_pe, s_na, s_out = map(
            sem, "in bc bce hi mid lo rest pm pe na out".split())
        block = ctx.enter_context(nc.Block())

        @block.sync
        def _(sp):
            for dst, src in ((w_bc[:, :, :, :], a["w_bc"]), (w_dt[:, :, :], a["w_dt"]), (al[:, :, :], a["A"])):
                sp.dma_start(dst, src).then_inc(s_in, 16)
            sp.wait_ge(s_na, 2)
            sp.dma_start(d["na"].rearrange("g p n -> p g n"), na[:, :, :]).then_inc(s_out, 16)
            for m in range(2):
                for i, s_part in enumerate((s_hi, s_mid, s_lo)):
                    sp.wait_ge(s_part, m + 1)
                    for r in range(4):
                        k, s = 2 * m + r // 2, r % 2
                        sp.dma_start(d["bc"][k, s, i * B * N:(i + 1) * B * N, :],
                                     parts[32 * r:32 * r + 32, m, i, :]).then_inc(s_out, 16)
            sp.wait_ge(s_out, 16 * 25)

        @block.tensor
        def _(pe):
            pe.wait_ge(s_in, 48)
            for m in range(2):
                if m:
                    pe.wait_ge(s_bce, 2)
                for c in range(NC):
                    for t in range(T):
                        mm = pe.matmul(ps[:, c * BANK:c * BANK + CH], w_bc[:, m, t, :],
                                       XI[:, t, c * CH:(c + 1) * CH], start=(t == 0), stop=(t == T - 1))
                mm.then_inc(s_bc, 1)
            pe.wait_ge(s_bce, 4)
            for c in range(NC):
                for t in range(T):
                    mm = pe.matmul(ps[0:K * B * R, c * BANK:c * BANK + CH], w_dt[:, t, :],
                                   XI[:, t, c * CH:(c + 1) * CH], start=(t == 0), stop=(t == T - 1))
            mm.then_inc(s_pm, 1)

        @block.scalar
        def _(act):
            act.wait_ge(s_in, 48)
            act.mul(na[:, :, 0:N], al[:, :, :], -1.0).then_inc(s_na, 1)
            act.mul(na[:, :, N:2 * N], al[:, :, :], -0.5).then_inc(s_na, 1)
            for m in range(2):
                act.wait_ge(s_bc, m + 1)
                for r in range(2):
                    k = 2 * m + r
                    for c in range(NC):
                        ins = act.copy(scan_order(bc[:, m, :], k)[64 * r:64 * r + 64, 8 * c:8 * c + 8, :],
                                       ps[64 * r:64 * r + 64, c * BANK:c * BANK + CH]
                                       .rearrange("p (h w) -> p h w", w=W))
                    ins.then_inc(s_bce, 1)
                act.wait_ge(s_bce, 2 * m + 2)
                act.copy(parts[:, m, 0, :], bc[:, m, :]).then_inc(s_hi, 1)
                act.wait_ge(s_rest, m + 1)
                act.copy(parts[:, m, 1, :], rest[:, :]).then_inc(s_mid, 1)
            act.wait_ge(s_pm, 1)
            act.copy(P[:, :].rearrange("p (c n) -> p c n", n=CH), banks(ps, 0, NC)[0:K * B * R]).then_inc(s_pe, 1)

        @block.vector
        def _(dve):
            for m in range(2):
                dve.wait_ge(s_hi, m + 1)
                if m:
                    dve.wait_ge(s_lo, m)
                dve.tensor_tensor(rest[:, :], bc[:, m, :], parts[:, m, 0, :], ALU.subtract).then_inc(s_rest, 1)
                dve.wait_ge(s_mid, m + 1)
                dve.wait_ge(s_rest, m + 1)
                dve.tensor_tensor(parts[:, m, 2, :], rest[:, :], parts[:, m, 1, :], ALU.subtract).then_inc(s_lo, 1)


def l0_steps(nc, a, ps, XI, P, d):
    with ExitStack() as ctx:
        sb, sem = space(nc, ctx, "l0s")
        w_up = sb("w_up", [K * B * R, K * T, 128])
        dtb = sb("dtb", [128, T, K])
        x0, e, ln, wm, dl, vv = (sb(n, [128, 2, L]) for n in ("x0", "e", "ln", "wm", "dl", "vv"))
        s_in, s_up, s_x0, s_ab, s_e, s_ln, s_wm, s_c, s_min, s_dl, s_vv = map(
            sem, "in up x0 ab e ln wm c min dl vv".split())
        s_store = [sem(f"store{i}") for i in range(2)]
        G = K * T
        block = ctx.enter_context(nc.Block())

        @block.sync
        def _(sp):
            sp.dma_start(w_up[:, :, :], a["w_up"]).then_inc(s_in, 16)
            sp.dma_start(dtb[:, :, :], a["dtb"]).then_inc(s_in, 16)
            for g in range(G):
                sp.wait_ge(s_dl, g + 1)
                sp.dma_start(d["dlt"][g], dl[:, g % 2, :]).then_inc(s_store[g % 2], 16)
                sp.wait_ge(s_vv, g + 1)
                sp.dma_start(d["v"][g], vv[:, g % 2, :]).then_inc(s_store[g % 2], 16)
            for i in range(2):
                sp.wait_ge(s_store[i], 32 * (G // 2))

        @block.tensor
        def _(pe):
            pe.wait_ge(s_in, 32)
            for g in range(G):
                for half in range(2):
                    q = 2 * g + half
                    if q >= 2:
                        pe.wait_ge(s_x0, q - 1)
                    for c in range(3 * half, 3 * half + 3):
                        mm = pe.matmul(ps[:, c * BANK:c * BANK + CH], w_up[:, g, :],
                                       P[:, c * CH:(c + 1) * CH], start=True, stop=True)
                    mm.then_inc(s_up, 1)

        @block.scalar
        def _(act):
            act.wait_ge(s_in, 32)
            for g in range(G):
                t, k, i = g // K, g % K, g % 2
                if g >= 2:
                    act.wait_ge(s_dl, g - 1)
                for half in range(2):
                    act.wait_ge(s_up, 2 * g + half + 1)
                    for c in range(3 * half, 3 * half + 3):
                        ins = act.activation(scan_order(x0[:, i, :], k)[:, 8 * c:8 * c + 8, :],
                                             ps[:, c * BANK:c * BANK + CH].rearrange("p (h w) -> p h w", w=W),
                                             ACT.Identity, bias=dtb[:, t, k:k + 1])
                    ins.then_inc(s_x0, 1)
                act.wait_ge(s_x0, 2 * g + 2)
                act.activation(e[:, i, :], x0[:, i, :], ACT.Abs).then_inc(s_ab, 1)
                act.wait_ge(s_ab, g + 1)
                act.activation(e[:, i, :], e[:, i, :], ACT.Exp, scale=-1.0).then_inc(s_e, 1)
                act.wait_ge(s_e, g + 1)
                act.activation(ln[:, i, :], e[:, i, :], ACT.Ln, bias=1.0).then_inc(s_ln, 1)

        @block.vector
        def _(dve):
            for g in range(G):
                t, k, i = g // K, g % K, g % 2
                dve.wait_ge(s_e, g + 1)
                dve.tensor_scalar(wm[:, i, :], e[:, i, :], 1.0, -1.0, ALU.add, ALU.add).then_inc(s_wm, 1)
                dve.wait_ge(s_c, g + 1)
                dve.wait_ge(s_ln, g + 1)
                dve.tensor_tensor(ln[:, i, :], ln[:, i, :], wm[:, i, :], ALU.add).then_inc(s_min, 1)
                dve.wait_ge(s_min, 2 * g + 1)
                dve.tensor_tensor(ln[:, i, :], ln[:, i, :], e[:, i, :], ALU.min).then_inc(s_min, 1)
                dve.wait_ge(s_min, 2 * g + 2)
                if g >= 2:
                    dve.wait_ge(s_store[i], 32 * (g // 2))
                dve.scalar_tensor_tensor(dl[:, i, :], x0[:, i, :], 0.0, ln[:, i, :], ALU.max, ALU.add
                                         ).then_inc(s_dl, 1)
                dve.wait_ge(s_dl, g + 1)
                dve.tensor_tensor(scan_order(vv[:, i, :], k), by_image(XI[:, t, :]), scan_order(dl[:, i, :], k),
                                  ALU.mult).then_inc(s_vv, 1)

        @block.gpsimd
        def _(pool):
            for g in range(G):
                i = g % 2
                pool.wait_ge(s_wm, g + 1)
                pool.tensor_tensor(wm[:, i, :], e[:, i, :], wm[:, i, :], ALU.subtract).then_inc(s_c, 1)


def l0_scan(nc, a, ps, ident, d):
    with ExitStack() as ctx:
        sb, sem = space(nc, ctx, "l0c")
        NA = 4
        dlt, v, S, y = (sb(n, [128, 2, SEG]) for n in ("dlt", "v", "S", "y"))
        Bp, Cp = (sb(n, [3 * B * N, 2, SEG], BF16) for n in ("Bp", "Cp"))
        sel = sb("sel", [3 * B * N, 2, N * 128], BF16)
        na = sb("na", [128, 2, 2 * N])
        da = sb("da", [128, NA, SEG])
        r = sb("r", [128, NA, SEG])
        h = sb("h", [128, 2, SEG])
        hc = sb("hc", [128, 2, SEG])
        carry = sb("carry", [128, N])
        credit = sb("credit", [128, 8])
        floor = sb("floor", [128, 1])
        s_in = [sem(f"in{i}") for i in range(2)]
        s_yout = [sem(f"yout{i}") for i in range(2)]
        s_scan, s_ub, s_hc, s_y, s_evac = map(sem, ("scan", "ub", "hc", "y", "evac"))
        s_a, s_tanh, s_r, s_w, s_b, s_c, s_S, s_car, s_init = map(
            sem, ("a", "tanh", "r", "w", "b", "c", "S", "car", "init"))
        PB, PC, PY = 0, 2, 4
        block = ctx.enter_context(nc.Block())
        U = 2 * NSEG
        J = U * N
        NLOAD = 6

        def nest(eng):
            return eng.Fori(0, T), eng.Fori(0, K // 2)

        @block.sync
        def _(sp):
            lt, lq = nest(sp)
            with lt as t, lq as q:
                for u in range(U):
                    g = t * (2 * U) + q * U + u
                    kt = t * K + q * 2 + u // NSEG
                    c0 = (u % NSEG) * SEG
                    i = u % 2
                    k32 = (q * 2 + u // NSEG) * (2 * B * N)
                    sp.wait_ge(s_evac, g + 1)
                    sp.dma_start(dlt[:, i, :], d["dlt"][kt, :, c0:c0 + SEG]).then_inc(s_in[i], 16)
                    sp.dma_start(v[:, i, :], d["v"][kt, :, c0:c0 + SEG]).then_inc(s_in[i], 16)
                    sp.dma_start(na[:, i, :], d["na"][kt]).then_inc(s_in[i], 16)
                    sp.dma_start(Bp[:, i, :], d["bc"][q * 2 + u // NSEG, 0, :, c0:c0 + SEG]).then_inc(s_in[i], 16)
                    sp.dma_start(Cp[:, i, :], d["bc"][q * 2 + u // NSEG, 1, :, c0:c0 + SEG]).then_inc(s_in[i], 16)
                    sp.dma_start(sel[:, i, :], a["sel"][t]).then_inc(s_in[i], 16)
            for i in range(2):
                sp.wait_ge(s_in[i], 16 * NLOAD * K * T * NSEG // 2)

        @block.tensor
        def _(pe):
            lt, lq = nest(pe)
            with lt as t, lq as q:
                base = t * (2 * J) + q * J
                segs = t * (2 * U) + q * U

                def spread(rows, first, j, done):
                    i, n = (j // N) % 2, j % N
                    for c in range(2):
                        mm = pe.matmul(ps[:, (first + c) * BANK:(first + c) * BANK + CH],
                                       sel[:, i, n * 128:(n + 1) * 128], rows[:, i, c * CH:(c + 1) * CH],
                                       start=True, stop=True)
                    mm.then_inc(done, 1)

                def b_rows(j):
                    if j % N == 0:
                        pe.wait_ge(s_in[(j // N) % 2],
                                   (t * U + q * (U // 2) + j // N // 2 + 1) * (16 * NLOAD))
                    pe.wait_ge(s_ub, base + j + NA)
                    spread(Bp, PB, j, s_b)

                def add_y(j):
                    u, n = j // N, j % N
                    if n == 0:
                        pe.wait_ge(s_evac, segs + u + 1)
                    pe.wait_ge(s_hc, base + j + 2)
                    for c in range(2):
                        o = (PY + 2 * (u % 2) + c) * BANK
                        mm = pe.matmul(ps[:, o:o + CH], ident[:, :], hc[:, j % 2, c * CH:(c + 1) * CH],
                                       start=(n == 0), stop=(n == N - 1))
                    mm.then_inc(s_y, 1)

                b_rows(0)
                for j in range(J):
                    if j + 1 < J:
                        b_rows(j + 1)
                    pe.wait_ge(s_hc, base + j + 1)
                    spread(Cp, PC, j, s_c)
                    if j:
                        add_y(j - 1)
                add_y(J - 1)

        @block.vector
        def _(dve):
            dve.memset(floor[:, :], 0.5 * LOG_FLOOR).then_inc(s_init, 1)
            dve.memset(credit[:, 0:1], 0.0).then_inc(s_scan, NA)
            dve.memset(credit[:, 1:2], 0.0).then_inc(s_ub, NA)
            dve.memset(credit[:, 2:3], 0.0).then_inc(s_hc, 1)
            dve.memset(credit[:, 3:4], 0.0).then_inc(s_y, 2)
            dve.memset(credit[:, 4:5], 0.0).then_inc(s_evac, 2)
            dve.memset(credit[:, 5:6], 0.0).then_inc(s_yout[0], 16)
            dve.memset(credit[:, 6:7], 0.0).then_inc(s_yout[1], 16)
            lt, lq = nest(dve)
            with lt as t, lq as q:
                base = t * (2 * J) + q * J
                segs = t * (2 * U) + q * U
                loads = t * U + q * (U // 2)

                def cumsum(u):
                    i = u % 2
                    dve.wait_ge(s_in[i], (loads + u // 2 + 1) * (16 * NLOAD))
                    if u % NSEG:
                        dve.wait_ge(s_S, segs + u)
                        init = S[:, 1 - i, SEG - 1:SEG]
                    else:
                        init = 0.0
                    dve.tensor_tensor_scan(S[:, i, :], dlt[:, i, :], dlt[:, i, :], init, ALU.add, ALU.bypass
                                           ).then_inc(s_S, 1)

                def times_c(j):
                    u, n = j // N, j % N
                    dve.wait_ge(s_scan, base + j + NA + 1)
                    dve.tensor_copy(carry[:, n:n + 1], h[:, j % 2, SEG - 1:SEG]).then_inc(s_car, 1)
                    dve.wait_ge(s_c, base + j + 1)
                    dve.wait_ge(s_y, base + j + 1)
                    dve.tensor_tensor(hc[:, j % 2, :].rearrange("p (c n) -> p c n", n=CH), banks(ps, PC, 2),
                                      h[:, j % 2, :].rearrange("p (c n) -> p c n", n=CH), ALU.mult).then_inc(s_hc, 1)

                cumsum(0)
                for j in range(J):
                    u, n = j // N, j % N
                    dve.wait_ge(s_w, base + j + 1)
                    dve.wait_ge(s_b, base + j + 1)
                    rj = r[:, j % NA, :]
                    dve.tensor_tensor(rj.rearrange("p (c n) -> p c n", n=CH), banks(ps, PB, 2),
                                      rj.rearrange("p (c n) -> p c n", n=CH), ALU.mult).then_inc(s_ub, 1)
                    if j:
                        times_c(j - 1)
                    if n == N // 2 and u + 1 < U:
                        cumsum(u + 1)
                    dve.wait_ge(s_a, base + j + 1)
                    dve.wait_ge(s_ub, base + j + NA + 1)
                    if u % NSEG:
                        dve.wait_ge(s_car, base + (j - N) + 1)
                        init = carry[:, n:n + 1]
                    else:
                        init = 0.0
                    dve.tensor_tensor_scan(h[:, j % 2, :], da[:, j % NA, :], rj, init, ALU.mult, ALU.add
                                           ).then_inc(s_scan, 1)
                times_c(J - 1)

        @block.gpsimd
        def _(pool):
            lt, lq = nest(pool)
            with lt as t, lq as q:
                base = t * (2 * J) + q * J
                for j in range(J):
                    if j % N == 0:
                        pool.wait_ge(s_in[(j // N) % 2], (t * U + q * (U // 2) + j // N // 2 + 1) * (16 * NLOAD))
                    pool.wait_ge(s_r, base + j + 1)
                    pool.tensor_tensor(r[:, j % NA, :], r[:, j % NA, :], v[:, (j // N) % 2, :], ALU.mult
                                       ).then_inc(s_w, 1)

        @block.scalar
        def _(act):
            act.wait_ge(s_init, 1)
            lt, lq = nest(act)
            with lt as t, lq as q:
                base = t * (2 * J) + q * J
                segs = t * (2 * U) + q * U

                def store(u):
                    i = u % 2
                    act.wait_ge(s_y, base + (u + 1) * N + 2)
                    act.wait_ge(s_yout[i], (t * U + q * (U // 2) + u // 2 + 1) * 16)
                    act.activation(y[:, i, :].rearrange("p (c n) -> p c n", n=CH), banks(ps, PY + 2 * i, 2),
                                   ACT.Copy, scale=0.5).then_inc(s_evac, 1)
                    act.wait_ge(s_evac, segs + u + 3)
                    kt = t * K + q * 2 + u // NSEG
                    c0 = (u % NSEG) * SEG
                    act.dma_start(d["y"][kt, :, c0:c0 + SEG], y[:, i, :]).then_inc(s_yout[i], 16)

                for j in range(J):
                    u, n, i = j // N, j % N, (j // N) % 2
                    if n == 0:
                        act.wait_ge(s_in[i], (t * U + q * (U // 2) + u // 2 + 1) * (16 * NLOAD))
                        act.wait_ge(s_S, segs + u + 1)
                    act.wait_ge(s_scan, base + j + 1)
                    act.activation(r[:, j % NA, :], S[:, i, :], ACT.Tanh, bias=floor[:, :],
                                   scale=na[:, i, N + n:N + n + 1]).then_inc(s_tanh, 1)
                    act.activation(da[:, j % NA, :], dlt[:, i, :], ACT.Exp,
                                   scale=na[:, i, n:n + 1]).then_inc(s_a, 1)
                    act.wait_ge(s_tanh, base + j + 1)
                    act.activation(r[:, j % NA, :], r[:, j % NA, :], ACT.Identity, bias=1.0).then_inc(s_r, 1)
                    if n == 3 and u:
                        store(u - 1)
                store(U - 1)
            for i in range(2):
                act.wait_ge(s_yout[i], 16 * (K * T * NSEG // 2 + 1))


def l0_norm(nc, a, ps, Z, Y, d):
    with ExitStack() as ctx:
        sb, sem = space(nc, ctx, "l0n")
        yk = sb("yk", [128, 3, L])
        Ds = sb("Ds", [128, T, K])
        dsum, eps = sb("dsum", [128, T]), sb("eps", [128, 1])
        gb = sb("gb", [128, T, 2])
        avg = sb("avg", [128, 7, 128])
        sq = sb("sq", [128, T, L])
        iv = sb("iv", [128, T, L])
        s_in, s_dve, s_mean, s_yc, s_sq, s_var, s_inv, s_root, s_n, s_aff, s_add = map(
            sem, "in dve mean yc sq var inv root n aff add".split())
        s_y = sem("y")
        s_k = [sem(f"k{i}") for i in range(3)]
        mix = [[(0, 0), (1, 1)], [(0, 2), (1, 3), (2, 4)], [(1, 5), (2, 6)]]
        adds = [(t, k) for t in range(T) for k in range(1, K)]
        block = ctx.enter_context(nc.Block())

        @block.sync
        def _(sp):
            for dst, src in ((Ds[:, :, :], a["Ds"]), (gb[:, :, :], a["gb"]), (avg[:, :, :], a["avg"])):
                sp.dma_start(dst, src).then_inc(s_in, 16)
            for t in range(T):
                sp.dma_start(Y[:, t, :], d["y"][t * K]).then_inc(s_y, 16)
            for j, (t, k) in enumerate(adds):
                if j >= 3:
                    sp.wait_ge(s_add, j - 2)
                sp.dma_start(yk[:, j % 3, :], d["y"][t * K + k]).then_inc(s_k[j % 3], 16)

        @block.tensor
        def _(pe):
            pe.wait_ge(s_in, 48)
            pe.wait_ge(s_add, len(adds))
            for base, src, s_src, s_done, s_free in ((0, Y, s_add, s_mean, s_yc), (0, sq, s_sq, s_var, s_inv)):
                for q in range(T * NC):
                    t, c = divmod(q, NC)
                    if q >= 8:
                        pe.wait_ge(s_free, q - 7)
                    elif s_src is s_sq:
                        pe.wait_ge(s_sq, T)
                    o = (q % 8) * BANK
                    for m, (f, blk) in enumerate(mix[t]):
                        mm = pe.matmul(ps[:, o:o + CH], avg[:, blk, :], src[:, f, c * CH:(c + 1) * CH],
                                       start=(m == 0), stop=(m == len(mix[t]) - 1))
                    mm.then_inc(s_done, 1)

        @block.scalar
        def _(act):
            for t in range(T):
                act.wait_ge(s_yc, NC * (t + 1))
                act.activation(sq[:, t, :], iv[:, t, :], ACT.Square).then_inc(s_sq, 1)
            act.wait_ge(s_in, 48)
            for t in range(T):
                act.wait_ge(s_inv, NC * (t + 1))
                act.activation(yk[:, t, :], yk[:, t, :], ACT.Sqrt).then_inc(s_root, 1)
            for t in range(T):
                act.wait_ge(s_n, t + 1)
                act.activation(yk[:, t, :], yk[:, t, :], ACT.Identity, scale=gb[:, t, 0:1],
                               bias=gb[:, t, 1:2]).then_inc(s_aff, 1)

        @block.vector
        def _(dve):
            step = Steps(dve, s_dve)
            dve.wait_ge(s_in, 48)
            step(dve.tensor_reduce(dsum[:, :], Ds[:, :, :], AX.X, ALU.add))
            dve.wait_ge(s_y, 16 * T)
            for j, (t, k) in enumerate(adds):
                dve.wait_ge(s_k[j % 3], 16 * (j // 3 + 1))
                if j:
                    dve.wait_ge(s_add, j)
                dst = by_image(Y[:, t, :])
                src = scan_order(yk[:, j % 3, :], k)
                if k == 1:
                    ins = dve.scalar_tensor_tensor(dst, src, dsum[:, t:t + 1], dst, ALU.add, ALU.add)
                else:
                    ins = dve.tensor_tensor(dst, src, dst, ALU.add)
                ins.then_inc(s_add, 1)
            for q in range(T * NC):
                t, c = divmod(q, NC)
                dve.wait_ge(s_mean, q + 1)
                o = (q % 8) * BANK
                cs = slice(c * CH, (c + 1) * CH)
                dve.tensor_tensor(iv[:, t, cs], Y[:, t, cs], ps[:, o:o + CH], ALU.subtract).then_inc(s_yc, 1)
            for q in range(T * NC):
                t, c = divmod(q, NC)
                dve.wait_ge(s_var, q + 1)
                o = (q % 8) * BANK
                cs = slice(c * CH, (c + 1) * CH)
                dve.tensor_scalar(Y[:, t, cs], ps[:, o:o + CH], 1e-5, None, ALU.add).then_inc(s_dve, 1)
                step.n += 1
                dve.wait_ge(s_dve, step.n)
                dve.reciprocal(yk[:, t, cs], Y[:, t, cs]).then_inc(s_inv, 1)
            for t in range(T):
                dve.wait_ge(s_root, t + 1)
                dve.wait_ge(s_yc, T * NC)
                dve.tensor_tensor(yk[:, t, :], yk[:, t, :], iv[:, t, :], ALU.mult).then_inc(s_n, 1)
            for t in range(T):
                dve.wait_ge(s_aff, t + 1)
                step(dve.tensor_tensor(Y[:, t, :], yk[:, t, :], Z[:, t, :], ALU.mult))


def l0_ffn(nc, a, ps, X, U):
    OT = 2 * E // 128
    with ExitStack() as ctx:
        sb, sem = space(nc, ctx, "l0f")
        c1 = sb("c1", [128, T, 2 * E])
        c3 = sb("c3", [128, OT, C])
        pr = sb("pr", [128, OT, 10])
        c2 = sb("c2", [128, OT, TAPS])
        c3b = sb("c3b", [C, 1])
        se1, se2 = sb("se1", [C, C // 2]), sb("se2", [C // 2, C])
        seb = sb("seb", [C, 2])
        sc = sb("sc", [128, 2, OT])
        bi = sb("bi", [128, 2, OT])
        t1, t2 = sb("t1", [128, 2, OT]), sb("t2", [128, 2, OT])
        pad = sb("pad", [128, 2, PW, PW])
        acc = sb("acc", [128, 2, L])
        t3 = sb("t3", [128, OT, L])
        to = sb("to", [C, B, L])
        m, s1, s2 = sb("m", [C, B, NC]), sb("s1", [C // 2, B]), sb("s2", [C, B])
        mean = sb("mean", [C, B])
        (s_in, s_dve, s_inv, s_root, s_bn, s_pad, s_c1, s_ev, s_tap, s_t3, s_c3, s_o, s_m, s_h, s_s1, s_g, s_e, s_t3p
         ) = map(sem, "in dve inv root bn pad c1 ev tap t3 c3 o m h s1 g e t3p".split())
        NIN = 8
        block = ctx.enter_context(nc.Block())

        @block.sync
        def _(sp):
            for dst, src in ((c1[:, :, :], a["c1"]), (c3[:, :, :], a["c3"]), (pr[:, :, :], a["ffn"]),
                             (c2[:, :, :], a["c2"]), (c3b[:, :], a["c3b"]), (se1[:, :], a["se1"]),
                             (se2[:, :], a["se2"]), (seb[:, :], a["seb"])):
                sp.dma_start(dst, src).then_inc(s_in, 16)
            sp.wait_ge(s_in, 16 * NIN)

        feeds = [[(0, 128, 0), (0, 64, 1)], [(64, 128, 1), (0, 128, 2)]]
        tiles = [(b, ot) for b in range(B) for ot in range(OT)]

        @block.tensor
        def _(pe):
            pe.wait_ge(s_in, 16 * NIN)

            def c1_tile(j):
                b, ot = tiles[j]
                for c in range(NC):
                    if j:
                        pe.wait_ge(s_ev, NC * (j - 1) + c + 1)
                    for f, (lo, hi, t) in enumerate(feeds[b]):
                        mm = pe.matmul(ps[:, c * BANK:c * BANK + CH], c1[lo:hi, t, ot * 128:(ot + 1) * 128],
                                       U[lo:hi, t, c * CH:(c + 1) * CH], start=(f == 0), stop=(f == 1))
                    mm.then_inc(s_c1, 1)

            def c3_image(b):
                pe.wait_ge(s_t3, OT * (b + 1))
                for c in range(NC):
                    q = b * NC + c
                    if q >= 2:
                        pe.wait_ge(s_o, q - 1)
                    o = (6 + q % 2) * BANK
                    for ot in range(OT):
                        mm = pe.matmul(ps[0:C, o:o + CH], c3[:, ot, :], t3[:, ot, c * CH:(c + 1) * CH],
                                       start=(ot == 0), stop=(ot == OT - 1))
                    mm.then_inc(s_c3, 1)

            for j in range(OT + 1):
                c1_tile(j)
            c3_image(0)
            for j in range(OT + 1, 2 * OT):
                c1_tile(j)
            c3_image(1)
            pe.wait_ge(s_m, 1)
            pe.matmul(ps[0:C // 2, 0:B], se1[:, :], mean[:, :], start=True, stop=True).then_inc(s_h, 1)
            pe.wait_ge(s_s1, 1)
            pe.matmul(ps[0:C, BANK:BANK + B], se2[:, :], s1[:, :], start=True, stop=True).then_inc(s_g, 1)

        @block.scalar
        def _(act):
            act.wait_ge(s_inv, 1)
            act.activation(sc[:, :, :], t1[:, :, :], ACT.Sqrt).then_inc(s_root, 1)
            act.wait_ge(s_bn, 1)
            act.wait_ge(s_pad, 2)

            def evacuate(j):
                b, ot = tiles[j]
                if j >= 2:
                    act.wait_ge(s_tap, TAPS * (j - 1))
                for c in range(NC):
                    act.wait_ge(s_c1, NC * j + c + 1)
                    act.activation(pad[:, j % 2, 1 + 8 * c:9 + 8 * c, 1:1 + W],
                                   ps[:, c * BANK:c * BANK + CH].rearrange("p (h w) -> p h w", w=W), ACT.Relu,
                                   scale=sc[:, 0, ot:ot + 1], bias=bi[:, 0, ot:ot + 1]).then_inc(s_ev, 1)

            def finish(j):
                b, ot = tiles[j]
                act.wait_ge(s_tap, TAPS * (j + 1))
                if b:
                    act.wait_ge(s_c3, NC)
                act.activation(t3[:, ot, :], acc[:, j % 2, :], ACT.Relu, scale=sc[:, 1, ot:ot + 1],
                               bias=bi[:, 1, ot:ot + 1]).then_inc(s_t3, 1)

            def out(b):
                for c in range(NC):
                    q = b * NC + c
                    act.wait_ge(s_c3, q + 1)
                    o = (6 + q % 2) * BANK
                    act.activation(to[:, b, c * CH:(c + 1) * CH], ps[0:C, o:o + CH], ACT.Identity,
                                   bias=c3b[:, :], accum_out=m[:, b, c:c + 1]).then_inc(s_o, 1)

            evacuate(0)
            for j in range(2 * OT):
                if j == OT:
                    out(0)
                if j + 1 < 2 * OT:
                    evacuate(j + 1)
                finish(j)
            out(1)
            act.wait_ge(s_h, 1)
            act.activation(s1[:, :], ps[0:C // 2, 0:B], ACT.Relu, bias=seb[0:C // 2, 0:1]).then_inc(s_s1, 1)
            act.wait_ge(s_g, 1)
            act.activation(s2[:, :], ps[0:C, BANK:BANK + B], ACT.Sigmoid, bias=seb[:, 1:2]).then_inc(s_e, 1)

        @block.vector
        def _(dve):
            step = Steps(dve, s_dve)
            for i in range(2):
                dve.memset(pad[:, i, :, :], 0.0).then_inc(s_pad, 1)
            dve.wait_ge(s_in, 16 * NIN)
            p = pr[:, :, :].rearrange("p o (h q) -> p h o q", h=2)
            step(dve.tensor_scalar(t2[:, :, :], p[:, :, :, 4], 1e-5, None, ALU.add))
            dve.reciprocal(t1[:, :, :], t2[:, :, :]).then_inc(s_inv, 1)
            dve.wait_ge(s_root, 1)
            step(dve.tensor_tensor(t1[:, :, :], sc[:, :, :], sc[:, :, :], ALU.mult))
            step(dve.tensor_tensor(t1[:, :, :], t1[:, :, :], t2[:, :, :], ALU.mult))
            step(dve.tensor_scalar(t1[:, :, :], t1[:, :, :], -0.5, 1.5, ALU.mult, ALU.add))
            step(dve.tensor_tensor(sc[:, :, :], sc[:, :, :], t1[:, :, :], ALU.mult))
            step(dve.tensor_tensor(sc[:, :, :], sc[:, :, :], p[:, :, :, 1], ALU.mult))
            step(dve.tensor_tensor(t1[:, :, :], p[:, :, :, 0], p[:, :, :, 3], ALU.subtract))
            step(dve.tensor_tensor(t1[:, :, :], t1[:, :, :], sc[:, :, :], ALU.mult))
            dve.tensor_tensor(bi[:, :, :], t1[:, :, :], p[:, :, :, 2], ALU.add).then_inc(s_bn, 1)
            for j, (b, ot) in enumerate(tiles):
                dve.wait_ge(s_ev, NC * (j + 1))
                if j >= 2:
                    dve.wait_ge(s_t3, j - 1)
                dst = by_image(acc[:, j % 2, :])
                for i in range(TAPS):
                    dy, dx = divmod(i, 3)
                    src = pad[:, j % 2, dy:dy + H, dx:dx + W]
                    if i == 0:
                        ins = dve.tensor_scalar(dst, src, c2[:, ot, 0:1], None, ALU.mult)
                    else:
                        dve.wait_ge(s_tap, TAPS * j + i)
                        ins = dve.scalar_tensor_tensor(dst, src, c2[:, ot, i:i + 1], dst, ALU.mult, ALU.add)
                    ins.then_inc(s_tap, 1)
            dve.wait_ge(s_o, B * NC)
            step(dve.tensor_reduce(mean[:, :], m[:, :, :], AX.X, ALU.add))
            dve.tensor_scalar(mean[:, :], mean[:, :], 1.0 / L, None, ALU.mult).then_inc(s_m, 1)
            dve.wait_ge(s_e, 1)
            for b in range(B):
                step(dve.scalar_tensor_tensor(to[:, b, :], to[:, b, :], s2[:, b:b + 1], to[:, b, :], ALU.mult, ALU.add))
                step(dve.tensor_tensor(X[:, b, :], to[:, b, :], X[:, b, :], ALU.add))




def l1_pairs(nc, a, ps, X, pad, d):
    with ExitStack() as ctx:
        sb, sem = space(nc, ctx, "l1")
        wa = sb("wa", [128, PT, C])
        bias = sb("bias", [C, 1])
        s_w, s_edge, s_sum, s_sump, s_p, s_pd, s_wd, s_wp = map(sem, "w edge sum sump p pd wd wp".split())
        s_wt = sem("wt")
        with ExitStack() as early:
            sb1, _ = space(nc, early, "l1e")
            rows, p = sb1("rows", [C, B, PW, W]), sb1("p", [C, B, L])
            wb, ma, mb = (sb1(n, [128, PT, C]) for n in ("wb", "ma", "mb"))
            block = early.enter_context(nc.Block())

            @block.sync
            def _(sp):
                for dst, src in ((wa, "wa"), (wb, "wb"), (ma, "ma"), (mb, "mb")):
                    sp.dma_start(dst[:, :, :], a[src]).then_inc(s_w, 16)
                sp.dma_start(bias[:, :], a["l1b"]).then_inc(s_w, 16)
                for b in range(B):
                    sp.wait_ge(s_p, b + 1)
                    for i in range(2):
                        sp.dma_start(d["pd"][i * C:(i + 1) * C, b, :], p[:, b, :]).then_inc(s_pd, 16)
                sp.wait_ge(s_pd, 64)

            def box(step, eng, b):
                step(eng.tensor_tensor(rows[:, b, :, :], pad[:, b, :, 0:W], pad[:, b, :, 1:1 + W], ALU.add))
                step(eng.tensor_tensor(rows[:, b, :, :], rows[:, b, :, :], pad[:, b, :, 2:2 + W], ALU.add))
                step(eng.tensor_tensor(by_image(p[:, b, :]), rows[:, b, 0:H, :], rows[:, b, 1:1 + H, :], ALU.add))
                step(eng.tensor_tensor(by_image(p[:, b, :]), by_image(p[:, b, :]), rows[:, b, 2:2 + H, :], ALU.add))

            @block.vector
            def _(dve):
                for b in range(B):
                    dve.memset(pad[:, b, 0:PW:PW - 1, :], 0.0)
                    dve.memset(pad[:, b, 1:1 + H, 0:PW:PW - 1], 0.0).then_inc(s_edge, 1)
                dve.wait_ge(s_edge, 2)
                step = Steps(dve, s_sum)
                box(step, dve, 0)
                dve.wait_ge(s_w, 80)
                dve.tensor_tensor(wb[:, :, :], wb[:, :, :], mb[:, :, :], ALU.mult).then_inc(s_wd, 1)
                dve.wait_ge(s_wd, 1)
                dve.wait_ge(s_wp, 1)
                dve.tensor_tensor(wa[:, 1:, :], wa[:, 1:, :], wb[:, 1:, :], ALU.add)
                dve.tensor_tensor(wa[C:128, 0, :], wa[C:128, 0, :], wb[C:128, 0, :], ALU.add).then_inc(s_wt, 1)
                dve.wait_ge(s_wt, 1)

            @block.gpsimd
            def _(pool):
                pool.wait_ge(s_edge, 2)
                step = Steps(pool, s_sump)
                box(step, pool, 1)
                pool.wait_ge(s_w, 80)
                pool.tensor_tensor(wa[:, :, :], wa[:, :, :], ma[:, :, :], ALU.mult).then_inc(s_wp, 1)

            @block.scalar
            def _(act):
                for b, s in enumerate((s_sum, s_sump)):
                    act.wait_ge(s, 4)
                    act.mul(p[:, b, :], p[:, b, :], 1.0 / 9.0).then_inc(s_p, 1)

        base = sb("base", [128, 3, L])
        other = sb("other", [128, 3, L])
        prod = sb("prod", [128, 3, L])
        s_base, s_prod, s_used, s_out = map(sem, "base prod used out".split())
        s_slot = [sem(f"slot{i}") for i in range(3)]
        reads = []
        for i in range(PT):
            lo, hi, part = 128 * i, min(128 * i + 128, PAIR_ROWS), []
            while lo < hi:
                end = min(hi, (lo // C + 1) * C)
                part.append((lo - 128 * i, end - lo, lo % C + lo // C))
                lo = end
            reads.append(part)
        height = [sum(n for _, n, _ in part) for part in reads]
        nslot = [sum(len(reads[i]) for i in range(s, PT, 3)) for s in range(3)]
        upto = [sum(len(reads[j]) for j in range(i % 3, i + 1, 3)) for i in range(PT)]
        with nc.Block() as block:

            @block.sync
            def _(sp):
                with sp.Fori(0, B) as b:
                    sp.wait_ge(s_out, b + 1)
                    for j in range(3):
                        d0 = 128 * j % C
                        sp.dma_start(base[:, j, :], d["pd"][d0:d0 + 128, b, :]).then_inc(s_base, 16)
                    for i in range(PT):
                        if i >= 3:
                            sp.wait_ge(s_prod, b * PT + i - 2)
                        for lo, n, src in reads[i]:
                            sp.dma_start(other[lo:lo + n, i % 3, :], d["pd"][src:src + n, b, :]
                                         ).then_inc(s_slot[i % 3], 16)

            @block.vector
            def _(dve):
                dve.memset(prod[0:1, 0, 0:1], 0.0).then_inc(s_out, 1)
                dve.wait_ge(s_out, 1)
                with dve.Fori(0, B) as b:
                    dve.wait_ge(s_base, (b + 1) * 48)
                    for i in range(PT):
                        s, n = i % 3, height[i]
                        dve.wait_ge(s_slot[s], b * (16 * nslot[s]) + 16 * upto[i])
                        if i >= 3:
                            dve.wait_ge(s_used, b * PT + i - 2)
                        dve.tensor_tensor(prod[0:n, s, :], base[0:n, s, :], other[0:n, s, :], ALU.mult
                                          ).then_inc(s_prod, 1)
                    dve.wait_ge(s_used, b * PT + PT)
                    xb = X[:, b, :].rearrange("p (c n) -> p c n", n=CH)
                    dve.scalar_tensor_tensor(xb, banks(ps, 0, NC)[0:C], bias[:, :], xb, ALU.add, ALU.add
                                             ).then_inc(s_out, 1)
                dve.wait_ge(s_out, B + 1)

            @block.tensor
            def _(pe):
                with pe.Fori(0, B) as b:
                    pe.wait_ge(s_out, b + 1)
                    for i in range(PT):
                        pe.wait_ge(s_prod, b * PT + i + 1)
                        for c in range(NC):
                            mm = pe.matmul(ps[0:C, c * BANK:c * BANK + CH], wa[0:height[i], i, :],
                                           prod[0:height[i], i % 3, c * CH:(c + 1) * CH],
                                           start=(i == 0), stop=(i == PT - 1))
                        mm.then_inc(s_used, 1)



KS = 9
RAD = KS // 2
DW = W + 2 * RAD
PE_TAPS = 32


def l2_diffuse(nc, a, ps, X, pad, ident):
    al = 0.65
    c1 = 1.0 / math.gamma(1.0 + 1.0 / al)
    c2 = math.sqrt(2.0 * c1)
    val = 3.0 * (-2.0 + (1.0 + 2.0 * al) * c2) / ((1.0 + 2.0 * al) * (-2.0 * c1 + 3.0 * c2))
    gauss_k = val / (4.0 * math.pi * c1)
    poi_k = (1.0 - val) * math.gamma(1.5) / math.pi ** 1.5 * c2
    NT = KS * KS
    dve_taps = list(range(NT - PE_TAPS))
    pe_taps = list(range(NT - PE_TAPS, NT))
    with ExitStack() as ctx:
        sb, sem = space(nc, ctx, "l2")
        yg = sb("yg", [C, 2, NT])
        dm = sb("dm", [C, 4])
        z, z2 = sb("z", [C, 2, NT]), sb("z2", [C, 2, NT])
        r2, q, ex, root, t = (sb(n, [C, NT]) for n in ("r2", "q", "ex", "root", "t"))
        kern = sb("kern", [C, NT])
        diag = sb("diag", [C, PE_TAPS, C])
        acc = sb("acc", [C, B, L])
        s_in, s_edge, s_dve, s_r2, s_q, s_ex, s_root, s_kern, s_diag, s_tap, s_pe, s_end = map(
            sem, "in edge dve r2 q ex root kern diag tap pe end".split())
        block = ctx.enter_context(nc.Block())

        def finish(dve, b):
            dve.wait_ge(s_pe, b + 1)
            xb = X[:, b, :].rearrange("p (c n) -> p c n", n=CH)
            dve.tensor_tensor(xb, banks(ps, 0, NC)[0:C], xb, ALU.add).then_inc(s_end, 1)

        @block.sync
        def _(sp):
            sp.dma_start(yg[:, :, :], a["grid"]).then_inc(s_in, 16)
            sp.dma_start(dm[:, :], a["dm"]).then_inc(s_in, 16)
            sp.wait_ge(s_in, 32)

        @block.gpsimd
        def _(pool):
            for b in range(B):
                for lo, hi in ((0, RAD), (RAD + H, DW)):
                    pool.memset(pad[:, b, lo:hi, :], 0.0)
                    ins = pool.memset(pad[:, b, RAD:RAD + H, lo:hi], 0.0)
                ins.then_inc(s_edge, 1)

        @block.scalar
        def _(act):
            act.wait_ge(s_r2, 1)
            act.activation(ex[:, :], r2[:, :], ACT.Exp, scale=-1.0 / (4.0 * c1)).then_inc(s_ex, 1)
            act.wait_ge(s_q, 1)
            act.activation(root[:, :], q[:, :], ACT.Sqrt).then_inc(s_root, 1)
            act.wait_ge(s_kern, 1)
            for i, tap in enumerate(pe_taps):
                act.activation(diag[:, i, :], ident[0:C, 0:C], ACT.Copy, scale=kern[:, tap:tap + 1]
                               ).then_inc(s_diag, 1)

        @block.vector
        def _(dve):
            dve.wait_ge(s_in, 32)
            step = Steps(dve, s_dve)
            for i in range(2):
                step(dve.tensor_scalar(z[:, i, :], yg[:, 0, :], dm[:, 2 * i:2 * i + 1], None, ALU.mult))
                step(dve.scalar_tensor_tensor(z[:, i, :], yg[:, 1, :], dm[:, 2 * i + 1:2 * i + 2], z[:, i, :],
                                              ALU.mult, ALU.add))
            step(dve.tensor_tensor(z2[:, :, :], z[:, :, :], z[:, :, :], ALU.mult))
            dve.tensor_tensor(r2[:, :], z2[:, 0, :], z2[:, 1, :], ALU.add).then_inc(s_r2, 1)
            dve.wait_ge(s_r2, 1)
            dve.tensor_scalar(q[:, :], r2[:, :], c2 * c2, None, ALU.add).then_inc(s_q, 1)
            dve.wait_ge(s_root, 1)
            step(dve.reciprocal(t[:, :], root[:, :]))
            step(dve.tensor_tensor(t[:, :], t[:, :], q[:, :], ALU.mult))
            step(dve.tensor_tensor(root[:, :], root[:, :], t[:, :], ALU.add))
            step(dve.tensor_tensor(t[:, :], root[:, :], q[:, :], ALU.mult))
            step(dve.reciprocal(root[:, :], t[:, :]))
            step(dve.tensor_scalar(root[:, :], root[:, :], 2.0 * poi_k, None, ALU.mult))
            dve.wait_ge(s_ex, 1)
            dve.scalar_tensor_tensor(kern[:, :], ex[:, :], gauss_k, root[:, :], ALU.mult, ALU.add).then_inc(s_kern, 1)
            dve.wait_ge(s_kern, 1)
            dve.wait_ge(s_edge, B)
            count = 0
            for i, tap in enumerate(dve_taps):
                dy, dx = divmod(tap, KS)
                for b in range(B):
                    src = pad[:, b, dy:dy + H, dx:dx + W]
                    dst = by_image(acc[:, b, :])
                    if i == 0:
                        ins = dve.tensor_scalar(dst, src, kern[:, tap:tap + 1], None, ALU.mult)
                    else:
                        dve.wait_ge(s_tap, count - 1)
                        ins = dve.scalar_tensor_tensor(dst, src, kern[:, tap:tap + 1], dst, ALU.mult, ALU.add)
                    ins.then_inc(s_tap, 1)
                    count += 1
                if i == len(dve_taps) // 2:
                    finish(dve, 0)
            dve.wait_ge(s_tap, count)
            finish(dve, 1)
            dve.wait_ge(s_end, 2)
            for b in range(B):
                ins = dve.tensor_tensor(X[:, b, :], acc[:, b, :], X[:, b, :], ALU.add)
            ins.then_inc(s_end, 1)
            dve.wait_ge(s_end, 2 + 1)

        @block.tensor
        def _(pe):
            pe.wait_ge(s_edge, B)
            pe.wait_ge(s_diag, PE_TAPS)
            for b in range(B):
                if b:
                    pe.wait_ge(s_end, b)
                for i, tap in enumerate(pe_taps):
                    dy, dx = divmod(tap, KS)
                    for c in range(NC):
                        mm = pe.matmul(ps[0:C, c * BANK:c * BANK + CH], diag[:, i, :],
                                       pad[:, b, dy + 8 * c:dy + 8 * c + 8, dx:dx + W],
                                       start=(i == 0), stop=(i == PE_TAPS - 1))
                mm.then_inc(s_pe, 1)



HC = 4 * HID
O_SP, O_AL, O_FR, O_FF = 0, 2 * C3, 2 * C3 + 1, 2 * C3 + 1 + 4 * C3
GO = O_FF + 4 * C3
BC = B * C3
FJ = 10
FCH = [(j, min(j + FJ, H)) for j in range(0, H, FJ)]


def l3_gates(nc, a, ps, st, wg, bw, w0g, ph, d, XG):
    with ExitStack() as ctx:
        sb, sem = space(nc, ctx, "l3g")
        gap = sb("gap", [C, B])
        w1, b1 = sb("w1", [C, HC]), sb("b1", [HC, 1])
        w2, b2 = sb("w2", [HC, GO]), sb("b2", [1, GO])
        one = sb("one", [1, C3])
        hid = sb("hid", [HC, B])
        row = sb("row", [1, B, GO])
        wt = sb("wt", [BC, 2, 2, 2 * C3])
        w0 = sb("w0", [3 * C3, B, 3, C3])
        gate = sb("gate", [BC, 2, 2, 2 * C3])
        gate0 = sb("gate0", [3 * C3, B, C3])
        lv = sb("lv", [BC, H])
        al = sb("al", [BC, 1])
        turns, fr = sb("turns", [BC, 2, H]), sb("fr", [BC, 2, H])
        whole = sb("whole", [BC, 2, H], I32)
        cs = sb("cs", [BC, 2, H])
        t1, t2 = sb("t1", [BC, H, H]), sb("t2", [BC, H, H])
        (s_in, s_dve, s_gap, s_hid, s_hs, s_row, s_rs, s_gate, s_gs, s_al, s_als, s_w, s_fr, s_cs, s_pool, s_x, s_ex
         ) = map(sem, "in dve gap hid hs row rs gate gs al als w fr cs pool x ex".split())
        NIN = 8
        block = ctx.enter_context(nc.Block())

        @block.sync
        def _(sp):
            sp.dma_start(d["g"].rearrange("c b l -> c (b l)"), XG[C3:C, :, :].rearrange("c b l -> c (b l)")
                         ).then_inc(s_x, 16)
            for dst, src in ((w1[:, :], "w1"), (b1[:, :], "b1"), (w2[:, :], "w2"), (b2[:, :], "b2"),
                             (wt[:, :, :, :], "wt"), (w0[:, :, :, :], "w0"), (lv[:, :], "lv"),
                             (bw[:, :, :, :], "bw")):
                sp.dma_start(dst, a[src]).then_inc(s_in, 16)
            sp.wait_ge(s_x, 16)
            sp.wait_ge(s_in, 16 * NIN)

        @block.tensor
        def _(pe):
            pe.wait_ge(s_in, 16 * NIN)
            pe.wait_ge(s_gap, 1)
            pe.matmul(ps[0:HC, 0:B], w1[:, :], gap[:, :], start=True, stop=True).then_inc(s_hid, 1)
            pe.wait_ge(s_hs, 1)
            for b in range(B):
                pe.matmul(ps[0:1, (1 + b) * BANK:(1 + b) * BANK + GO], hid[:, b:b + 1], w2[:, :],
                          start=True, stop=False)
                mm = pe.matmul(ps[0:1, (1 + b) * BANK:(1 + b) * BANK + GO], one[:, 0:1], b2[:, :],
                               start=False, stop=True)
            mm.then_inc(s_row, 1)
            pe.wait_ge(s_rs, 1)
            for b in range(B):
                for f, o in enumerate((O_FR, O_FF)):
                    for p in range(2):
                        mm = pe.matmul(ps[C3 * b:C3 * b + C3, (3 + 2 * f + p) * BANK:(3 + 2 * f + p) * BANK + 2 * C3],
                                       row[:, b, o + 2 * C3 + p * C3:o + 2 * C3 + (p + 1) * C3],
                                       row[:, b, o:o + 2 * C3], start=True, stop=True)
            for b in range(B):
                for i in range(3):
                    pe.matmul(ps[C3 * i:C3 * i + C3, (7 * b) * BANK:(7 * b) * BANK + C3],
                              row[:, b, O_SP + C3:O_SP + 2 * C3], row[:, b, O_SP:O_SP + C3], start=True, stop=True)
            for b in range(B):
                mm = pe.matmul(ps[C3 * b:C3 * b + C3, BANK:BANK + 1], one[:, :], row[:, b, O_AL:O_AL + 1],
                               start=True, stop=True)
            mm.then_inc(s_gate, 1)

        @block.scalar
        def _(act):
            act.wait_ge(s_in, 16 * NIN)
            act.wait_ge(s_hid, 1)
            act.activation(hid[:, :], ps[0:HC, 0:B], ACT.Relu, bias=b1[:, :]).then_inc(s_hs, 1)
            act.wait_ge(s_row, 1)
            act.copy(row[:, :, :], ps[0:1, BANK:3 * BANK].rearrange("p (b n) -> p b n", b=B)[:, :, 0:GO]
                     ).then_inc(s_rs, 1)
            act.wait_ge(s_gate, 1)
            act.activation(al[:, :], ps[0:BC, BANK:BANK + 1], ACT.Sigmoid).then_inc(s_als, 1)
            act.activation(gate[:, :, :, :].rearrange("p f i o -> p (f i) o"),
                           ps[0:BC, 3 * BANK:7 * BANK].rearrange("p (q n) -> p q n", n=BANK)[:, :, 0:2 * C3],
                           ACT.Sigmoid).then_inc(s_gs, 1)
            for b in range(B):
                act.activation(gate0[:, b, :], ps[0:3 * C3, 7 * b * BANK:7 * b * BANK + C3], ACT.Sigmoid
                               ).then_inc(s_gs, 1)
            act.wait_ge(s_fr, 1)
            act.activation(cs[:, :, :], fr[:, :, :], ACT.Sin, scale=2.0 * math.pi * (1.0 - 1e-7)).then_inc(s_cs, 1)

        @block.vector
        def _(dve):
            step = Steps(dve, s_dve)
            step(dve.memset(one[:, :], 1.0))
            step(dve.tensor_tensor(gap[:, :], st["mv"][:, :, 0], st["rstd"][:, :], ALU.mult))
            dve.tensor_tensor(gap[:, :], gap[:, :], st["shift"][:, :], ALU.add).then_inc(s_gap, 1)
            step(dve.memset(wg[:, :, :, :, :], 0.0))
            dve.wait_ge(s_als, 1)
            step(dve.tensor_scalar(al[:, :], al[:, :], 0.8, 0.1, ALU.mult, ALU.add))
            step(dve.tensor_scalar(turns[:, 0, :], lv[:, :], al[:, 0:1], 0.25, ALU.mult, ALU.mult))
            step(dve.tensor_scalar(turns[:, 1, :], turns[:, 0, :], 0.25, None, ALU.add))
            step(dve.tensor_copy(whole[:, :, :], turns[:, :, :]))
            step(dve.tensor_copy(fr[:, :, :], whole[:, :, :]))
            step(dve.tensor_tensor(turns[:, :, :], turns[:, :, :], fr[:, :, :], ALU.subtract))
            step(dve.tensor_scalar(fr[:, :, :], turns[:, :, :], 0.5, None, ALU.is_gt))
            dve.tensor_tensor(fr[:, :, :], turns[:, :, :], fr[:, :, :], ALU.subtract).then_inc(s_fr, 1)
            dve.wait_ge(s_gs, 3)
            dve.wait_ge(s_in, 16 * NIN)
            for f in range(2):
                for b in range(B):
                    rows = slice(C3 * b, C3 * b + C3)
                    dst = wg[rows, f, :, :, rows]
                    step(dve.tensor_tensor(dst, gate[rows, f, :, :].rearrange("p i (q o) -> p i q o", q=2),
                                           wt[rows, f, :, :].rearrange("p i (q o) -> p i q o", q=2), ALU.mult))
            for b in range(B):
                for i in range(3):
                    ins = dve.tensor_tensor(w0g[:, b, i, :], gate0[:, b, :], w0[:, b, i, :], ALU.mult)
            step(ins)
            dve.wait_ge(s_cs, 1)
            sj = [cs[:, i, :].unsqueeze(2).to_broadcast([BC, H, H]) for i in range(2)]
            sk = [cs[:, i, :].unsqueeze(1).to_broadcast([BC, H, H]) for i in range(2)]
            step(dve.tensor_tensor(t1[:, :, :], sj[1], sk[1], ALU.mult))
            step(dve.tensor_tensor(t2[:, :, :], sj[0], sk[0], ALU.mult))
            step(dve.tensor_tensor(ph[:, 0, :, :], t1[:, :, :], t2[:, :, :], ALU.subtract))
            step(dve.tensor_tensor(t1[:, :, :], sj[0], sk[1], ALU.mult))
            step(dve.tensor_tensor(t2[:, :, :], sj[1], sk[0], ALU.mult))
            step(dve.tensor_tensor(ph[:, 1, :, :], t1[:, :, :], t2[:, :, :], ALU.add))


def l3_forward(nc, a, ps, wg, bw, ph, d):
    with ExitStack() as ctx:
        sb, sem = space(nc, ctx, "l3f")
        xh = sb("xh", [H, 2, BC, W])
        ef = sb("ef", [H, H])
        fh, fw = sb("fh", [H, 2 * H]), sb("fw", [H, 2, 2 * UH])
        e11 = sb("e11", [1, H * H])
        ones = sb("ones", [1, BANK])
        A1 = sb("A1", [W, BC, H])
        Xh, Zr, Zi = (sb(n, [BC, H, H]) for n in ("Xh", "Zr", "Zi"))
        Fz = sb("Fz", [BC, H, 2, UH])
        Mz = sb("Mz", [BC, H, 2, UH])
        M = sb("M", [BC, 2, H, H])
        share = sb("share", [BC, 2 * BC * H])
        A2 = share[0:W, :].rearrange("p (c i h) -> p c i h", i=2, h=H)
        V = share[:, 0:2 * H * H].rearrange("p (i j k) -> p i j k", i=2, j=H)
        s_in, s_one, s_mm, s_ev, s_z, s_m, s_dve, s_v, s_out = map(sem, "in one mm ev z m dve v out".split())
        NIN = 4 + 2 * B
        block = ctx.enter_context(nc.Block())

        @block.sync
        def _(sp):
            for dst, src in ((ef[:, :], "ef"), (fh[:, :], "fh"), (fw[:, :, :], "fw"), (e11[:, :], "e11")):
                sp.dma_start(dst, a[src]).then_inc(s_in, 16)
            for f in range(2):
                for b in range(B):
                    sp.dma_start(xh[:, f, C3 * b:C3 * b + C3, :],
                                 d["g"][C3 * f:C3 * f + C3, b, :].rearrange("c (h w) -> h c w", w=W)
                                 ).then_inc(s_in, 16)
            sp.wait_ge(s_m, 1)
            sp.dma_start(d["M"].rearrange("p u i k -> p (u i k)"), Mz[:, :, :, :].rearrange("p u i k -> p (u i k)")
                         ).then_inc(s_out, 16)
            sp.wait_ge(s_v, 2)
            sp.dma_start(d["V"].rearrange("p i j k -> p (i j k)"), V[:, :, :, :].rearrange("p i j k -> p (i j k)")
                         ).then_inc(s_out, 16)
            sp.wait_ge(s_out, 32)

        def rows_jobs():
            n = BANK // (2 * H)
            for c in range(0, BC, n):
                cc = range(c, min(c + n, BC))
                yield ([(xh[:, 1, i, :], fh[:, :], (i - c) * 2 * H, 2 * H, True, True) for i in cc], W,
                       A2[:, c:c + len(cc), :, :].rearrange("p c i h -> p (c i h)"), None)
            n = BANK // H
            for c in range(0, BC, n):
                cc = range(c, min(c + n, BC))
                yield ([(xh[:, 0, i, :], ef[:, :], (i - c) * H, H, True, True) for i in cc], W,
                       A1[:, c:c + len(cc), :].rearrange("p c h -> p (c h)"), None)

        def cols_jobs():
            for lo, hi in FCH:
                mms = []
                for u in range(lo, hi):
                    mms.append((A2[:, :, 0, u], fw[:, 0, :], (u - lo) * 2 * UH, 2 * UH, True, False))
                    mms.append((A2[:, :, 1, u], fw[:, 1, :], (u - lo) * 2 * UH, 2 * UH, False, True))
                yield mms, BC, Fz[:, lo:hi, :, :].rearrange("p u i k -> p (u i k)"), None
            for lo, hi in FCH:
                yield ([(A1[:, :, j], ef[:, :], (j - lo) * H, H, True, True) for j in range(lo, hi)], BC,
                       Xh[:, lo:hi, :].rearrange("p j k -> p (j k)"), float(H))

        def mix_jobs():
            for lo, hi in FCH:
                for q in range(2):
                    o = (hi - lo) * UH
                    yield ([(wg[:, 1, 0, q, :], Fz[:, lo:hi, 0, :], 0, o, True, False),
                            (wg[:, 1, 1, q, :], Fz[:, lo:hi, 1, :], 0, o, False, False),
                            (bw[:, 1, q, :], ones[:, 0:o], 0, o, False, True)], BC, Mz[:, lo:hi, q, :], None)

        def frac_jobs():
            for lo, hi in FCH:
                for q in range(2):
                    o = (hi - lo) * H
                    yield ([(wg[:, 0, 0, q, :], Zr[:, lo:hi, :].rearrange("p j k -> p (j k)"), 0, o, True, False),
                            (wg[:, 0, 1, q, :], Zi[:, lo:hi, :].rearrange("p j k -> p (j k)"), 0, o, False, False),
                            (bw[:, 0, q, :], e11[:, lo * H:hi * H], 0, o, False, True)], BC,
                           M[:, q, lo:hi, :].rearrange("p j k -> p (j k)"), None)

        phases = [list(g()) for g in (rows_jobs, cols_jobs, mix_jobs, frac_jobs)]

        @block.tensor
        def _(pe):
            pe.wait_ge(s_in, 16 * NIN)
            pe.wait_ge(s_one, 1)
            q = 0
            for i, jobs in enumerate(phases):
                if i:
                    pe.wait_ge(s_ev, q)
                if i == 3:
                    pe.wait_ge(s_z, 2)
                for mms, rows, _, _ in jobs:
                    if q >= 8:
                        pe.wait_ge(s_ev, q - 7)
                    for lhsT, rhs, at, n, start, stop in mms:
                        mm = pe.matmul(ps[0:rows, (q % 8) * BANK + at:(q % 8) * BANK + at + n], lhsT, rhs,
                                       start=start, stop=stop)
                    mm.then_inc(s_mm, 1)
                    q += 1

        @block.scalar
        def _(act):
            q = 0
            for i, jobs in enumerate(phases):
                for mms, rows, dst, scale in jobs:
                    act.wait_ge(s_mm, q + 1)
                    n = mms[-1][2] + mms[-1][3]
                    src = ps[0:rows, (q % 8) * BANK:(q % 8) * BANK + n]
                    if len(dst.shape) == 3:
                        src = src.rearrange("p (u k) -> p u k", k=UH)
                    if scale:
                        act.mul(dst, src, scale).then_inc(s_ev, 1)
                    else:
                        act.copy(dst, src).then_inc(s_ev, 1)
                    q += 1
                if i == 2:
                    act.wait_ge(s_ev, q)
                    act.copy(ones[:, 0:1], ones[:, 0:1]).then_inc(s_m, 1)

        @block.vector
        def _(dve):
            step = Steps(dve, s_dve)
            dve.memset(ones[:, :], 1.0).then_inc(s_one, 1)
            dve.wait_ge(s_ev, len(phases[0]) + len(phases[1]))
            dve.tensor_tensor(Zr[:, :, :], Xh[:, :, :], ph[:, 0, :, :], ALU.mult).then_inc(s_z, 1)
            dve.scalar_tensor_tensor(Zi[:, :, :], Xh[:, :, :], -1.0, ph[:, 1, :, :], ALU.mult, ALU.mult
                                     ).then_inc(s_z, 1)
            dve.wait_ge(s_ev, sum(map(len, phases)))
            for q, t in enumerate((Zr, Zi)):
                step(dve.tensor_tensor(V[:, q, :, :], M[:, q, :, :], ph[:, 0, :, :], ALU.mult))
                step(dve.tensor_tensor(t[:, :, :], M[:, 1 - q, :, :], ph[:, 1, :, :], ALU.mult))
            dve.tensor_tensor(V[:, 0, :, :], V[:, 0, :, :], Zr[:, :, :], ALU.subtract).then_inc(s_v, 1)
            dve.tensor_tensor(V[:, 1, :, :], V[:, 1, :, :], Zi[:, :, :], ALU.add).then_inc(s_v, 1)


def l3_inverse(nc, a, ps, d):
    with ExitStack() as ctx:
        sb, sem = space(nc, ctx, "l3i")
        Vj = sb("Vj", [H, BC, 2, H])
        Mu = sb("Mu", [H, BC, 2 * UH])
        ei = sb("ei", [H, H])
        ih, iw = sb("ih", [H, 2 * H]), sb("iw", [2 * UH, 2, W])
        A3 = sb("A3", [W, BC, 2, H])
        A4 = sb("A4", [2 * UH, BC, 2, H])
        O = sb("O", [H, BC, 2, W])
        P2, F = sb("P2", [H, BC, W]), sb("F", [H, BC, W])
        s_in, s_mm, s_ev, s_sum, s_root, s_out = map(sem, "in mm ev sum root out".split())
        NIN = 3 + 1 + 2
        block = ctx.enter_context(nc.Block())

        def jobs(kind):
            n = BANK // (2 * H)
            m = BANK // H
            if kind == 0:
                for c in range(0, BC, n):
                    cc = range(c, min(c + n, BC))
                    yield ([(Mu[:, i, :], ih[:, :], (i - c) * 2 * H, 2 * H, True, True) for i in cc], 2 * UH,
                           A4[:, c:c + len(cc), :, :].rearrange("p c i h -> p (c i h)"), ACT.Copy)
            if kind == 1:
                for c in range(0, BC, m):
                    cc = range(c, min(c + m, BC))
                    mms = []
                    for i in cc:
                        for q in range(2):
                            mms.append((A4[:, i, q, :], iw[:, q, :], (i - c) * W, W, q == 0, q == 1))
                    yield mms, H, F[:, c:c + len(cc), :].rearrange("p c w -> p (c w)"), ACT.Copy
            if kind == 2:
                for c in range(0, 2 * BC, m):
                    cc = range(c, min(c + m, 2 * BC))
                    yield ([(Vj[:, i // 2, i % 2, :], ei[:, :], (i - c) * H, H, True, True) for i in cc], H,
                           A3[:, :, :, :].rearrange("p c i h -> p (c i) h")[:, c:c + len(cc), :]
                           .rearrange("p c h -> p (c h)"), ACT.Copy)
            if kind == 3:
                for c in range(0, 2 * BC, m):
                    cc = range(c, min(c + m, 2 * BC))
                    yield ([(A3[:, i // 2, i % 2, :], ei[:, :], (i - c) * H, H, True, True) for i in cc], H,
                           O[:, :, :, :].rearrange("p c i h -> p (c i) h")[:, c:c + len(cc), :]
                           .rearrange("p c h -> p (c h)"), ACT.Square)

        phases = [list(jobs(i)) for i in range(4)]
        n_fft = len(phases[0]) + len(phases[1])

        @block.sync
        def _(sp):
            for dst, src in ((ei[:, :], "ei"), (ih[:, :], "ih"), (iw[:, :, :], "iw")):
                sp.dma_start(dst, a[src]).then_inc(s_in, 16)
            sp.dma_start(Mu[:, :, :], d["M"].rearrange("p u i k -> u p (i k)")).then_inc(s_in, 16)
            for i in range(2):
                sp.dma_start(Vj[:, :, i, :], d["V"][:, i, :, :].rearrange("p j k -> j p k")).then_inc(s_in, 16)
            sp.wait_ge(s_in, 16 * NIN)
            sp.wait_ge(s_ev, n_fft)
            sp.dma_start(d["o"][1], F[:, :, :]).then_inc(s_out, 16)
            sp.wait_ge(s_root, 1)
            sp.dma_start(d["o"][0], P2[:, :, :]).then_inc(s_out, 16)
            sp.wait_ge(s_out, 32)

        @block.tensor
        def _(pe):
            pe.wait_ge(s_in, 16 * NIN)
            q = 0
            for i, job in enumerate(phases):
                if i % 2:
                    pe.wait_ge(s_ev, q)
                for mms, rows, _, _ in job:
                    if q >= 8:
                        pe.wait_ge(s_ev, q - 7)
                    for lhsT, rhs, at, n, start, stop in mms:
                        mm = pe.matmul(ps[0:rows, (q % 8) * BANK + at:(q % 8) * BANK + at + n], lhsT, rhs,
                                       start=start, stop=stop)
                    mm.then_inc(s_mm, 1)
                    q += 1

        @block.scalar
        def _(act):
            q = 0
            for job in phases:
                for mms, rows, dst, fn in job:
                    act.wait_ge(s_mm, q + 1)
                    n = mms[-1][2] + mms[-1][3]
                    act.activation(dst, ps[0:rows, (q % 8) * BANK:(q % 8) * BANK + n], fn).then_inc(s_ev, 1)
                    q += 1
            act.wait_ge(s_sum, 1)
            act.activation(P2[:, :, :], P2[:, :, :], ACT.Sqrt, scale=1.0 / (H * W)).then_inc(s_root, 1)

        @block.vector
        def _(dve):
            dve.wait_ge(s_ev, sum(map(len, phases)))
            dve.tensor_tensor(P2[:, :, :], O[:, :, 0, :], O[:, :, 1, :], ALU.add).then_inc(s_sum, 1)


def l3_convs(nc, a, ps, X, G0, w0g, d):
    with ExitStack() as ctx:
        sb, sem = space(nc, ctx, "l3v")
        cat = sb("cat", [C, B, PW, PW])
        w2 = sb("w2", [C, TAPS, C])
        b0, b2 = sb("b0", [C3, 1]), sb("b2", [C, 1])
        s_in, s_edge, s_c0, s_e0, s_cat, s_c2, s_x = map(sem, "in edge c0 e0 cat c2 x".split())
        block = ctx.enter_context(nc.Block())

        @block.sync
        def _(sp):
            sp.dma_start(w2[:, :, :], a["cw2"]).then_inc(s_in, 16)
            sp.dma_start(b0[:, :], a["cb0"]).then_inc(s_in, 16)
            sp.dma_start(b2[:, :], a["cb2"]).then_inc(s_in, 16)
            sp.wait_ge(s_edge, 1)
            for f in range(2):
                for b in range(B):
                    sp.dma_start(interior(cat[C3 * (1 + f):C3 * (2 + f), b, :, :]),
                                 d["o"][f, :, C3 * b:C3 * b + C3, :].rearrange("h c w -> c h w")
                                 ).then_inc(s_cat, 16)
            sp.wait_ge(s_in, 48)
            sp.wait_ge(s_cat, 64)

        @block.gpsimd
        def _(pool):
            pool.memset(cat[:, :, :, :], 0.0).then_inc(s_edge, 1)

        @block.tensor
        def _(pe):
            q = 0
            for b in range(B):
                for c in range(NC):
                    if q >= 8:
                        pe.wait_ge(s_e0, q - 7)
                    for i in range(3):
                        mm = pe.matmul(ps[0:C3, (q % 8) * BANK:(q % 8) * BANK + CH], w0g[:, b, i, :],
                                       G0[:, b, i + 8 * c:i + 8 * c + 8, 0:W], start=(i == 0), stop=(i == 2))
                    mm.then_inc(s_c0, 1)
                    q += 1
            pe.wait_ge(s_in, 48)
            pe.wait_ge(s_cat, 64)
            pe.wait_ge(s_e0, B * NC)
            for q in range(B * NC):
                b, c = divmod(q, NC)
                if q >= 8:
                    pe.wait_ge(s_x, q - 7)
                for i in range(TAPS):
                    dy, dx = divmod(i, 3)
                    mm = pe.matmul(ps[0:C, (q % 8) * BANK:(q % 8) * BANK + CH], w2[:, i, :],
                                   cat[:, b, dy + 8 * c:dy + 8 * c + 8, dx:dx + W], start=(i == 0),
                                   stop=(i == TAPS - 1))
                mm.then_inc(s_c2, 1)

        @block.scalar
        def _(act):
            act.wait_ge(s_edge, 1)
            act.wait_ge(s_in, 48)
            for q in range(B * NC):
                b, c = divmod(q, NC)
                act.wait_ge(s_c0, q + 1)
                act.activation(cat[0:C3, b, 1 + 8 * c:9 + 8 * c, 1:1 + W],
                               ps[0:C3, (q % 8) * BANK:(q % 8) * BANK + CH].rearrange("p (h w) -> p h w", w=W),
                               ACT.Identity, bias=b0[:, :]).then_inc(s_e0, 1)

        @block.vector
        def _(dve):
            dve.wait_ge(s_in, 48)
            for q in range(B * NC):
                b, c = divmod(q, NC)
                dve.wait_ge(s_c2, q + 1)
                xs = X[:, b, c * CH:(c + 1) * CH]
                dve.scalar_tensor_tensor(xs, ps[0:C, (q % 8) * BANK:(q % 8) * BANK + CH], b2[:, :], xs,
                                         ALU.add, ALU.add).then_inc(s_x, 1)


def l3_spread(nc, XG, G0):
    with ExitStack() as ctx:
        _, sem = space(nc, ctx, "l3s")
        s_zero, s_copy = sem("zero"), sem("copy")
        block = ctx.enter_context(nc.Block())

        @block.vector
        def _(dve):
            dve.memset(G0[:, :, :, :], 0.0).then_inc(s_zero, 1)

        @block.sync
        def _(sp):
            sp.wait_ge(s_zero, 1)
            for i in range(3):
                lo, hi = max(0, i - 1), W + min(0, i - 1)
                for b in range(B):
                    sp.dma_start(G0[C3 * i:C3 * i + C3, b, 1:1 + H, lo + 1 - i:hi + 1 - i],
                                 by_image(XG[0:C3, b, :])[:, :, lo:hi]).then_inc(s_copy, 16)
            sp.wait_ge(s_copy, 96)


def l3(nc, a, ps, X, gavg, ident, st):
    d = {"g": nc.dram_tensor("g3", (2 * C3, B, L), F32).ap(), "V": nc.dram_tensor("V", (BC, 2, H, H), F32).ap(),
         "M": nc.dram_tensor("M", (BC, H, 2, UH), F32).ap(), "o": nc.dram_tensor("o3", (2, H, BC, W), F32).ap()}
    with ExitStack() as ctx:
        sb, _ = space(nc, ctx, "l3")
        w0g = sb("w0g", [3 * C3, B, 3, C3])
        G0 = sb("G0", [3 * C3, B, PW, W])
        with ExitStack() as spectral:
            sb1, _ = space(nc, spectral, "l3w")
            wg = sb1("wg", [BC, 2, 2, 2, BC])
            bw = sb1("bw", [1, 2, 2, BC])
            ph = sb1("ph", [BC, 2, H, H])
            with ExitStack() as early:
                XG = space(nc, early, "l3x")[0]("XG", [C, B, L])
                group_norm(nc, "gn3", X, ps, gavg, st, [by_image(XG[:, b, :]) for b in range(B)])
                l3_spread(nc, XG, G0)
                l3_gates(nc, a, ps, st, wg, bw, w0g, ph, d, XG)
            l3_forward(nc, a, ps, wg, bw, ph, d)
        l3_inverse(nc, a, ps, d)
        l3_convs(nc, a, ps, X, G0, w0g, d)




def program(nc, a, x, out, layers=(0, 1, 2, 3)):
    with ExitStack() as ctx:
        sb, _ = space(nc, ctx, "net")
        ps = ctx.enter_context(nc.psum_tensor("ps", [128, 8 * BANK], F32))
        X = sb("X", [C, B, L])
        gavg = sb("gavg", [C, C])
        ident = sb("ident", [128, 128])
        st = {"mv": sb("mv", [C, B, 2]), "rstd": sb("rstd", [C, B]), "shift": sb("shift", [C, B])}
        load(nc, "x", [(X[:, :, :], x.rearrange("b c h w -> c b (h w)")), (gavg[:, :], a["gavg"]),
                       (ident[:, :], a["ident"])])
        if 0 in layers:
            d = {"dlt": nc.dram_tensor("dlt", (K * T, 128, L), F32).ap(), "v": nc.dram_tensor("v", (K * T, 128, L), F32).ap(),
                 "y": nc.dram_tensor("y", (K * T, 128, L), F32).ap(), "na": nc.dram_tensor("na", (K * T, 128, 2 * N), F32).ap(),
                 "bc": nc.dram_tensor("bc", (K, 2, 3 * B * N, L), BF16).ap()}
            with ExitStack() as l0:
                sb0, _ = space(nc, l0, "l0")
                Z = sb0("Z", [128, T, L])
                with ExitStack() as early:
                    sb1, _ = space(nc, early, "l0e")
                    XI = sb1("XI", [128, T, L])
                    with ExitStack() as first:
                        XG = space(nc, first, "l0x")[0]("XG", [C, B, L])
                        group_norm(nc, "gn0", X, ps, gavg, st, [by_image(XG[:, b, :]) for b in range(B)])
                        l0_project(nc, a, X, XG, ps, XI, Z)
                    P = sb1("P", [K * B * R, L])
                    l0_rows(nc, a, ps, XI, P, d)
                    l0_steps(nc, a, ps, XI, P, d)
                l0_scan(nc, a, ps, ident, d)
                Y = sb0("Y", [128, T, L])
                l0_norm(nc, a, ps, Z, Y, d)
                l0_ffn(nc, a, ps, X, Y)
        if 1 in layers:
            with ExitStack() as l1:
                pad = space(nc, l1, "l1g")[0]("pad", [C, B, PW, PW])
                group_norm(nc, "gn1", X, ps, gavg, st, [interior(pad[:, b, :, :]) for b in range(B)])
                d = {"pd": nc.dram_tensor("pd", (2 * C, B, L), F32).ap()}
                l1_pairs(nc, a, ps, X, pad, d)
        if 2 in layers:
            with ExitStack() as l2:
                pad = space(nc, l2, "l2g")[0]("pad", [C, B, DW, DW])
                group_norm(nc, "gn2", X, ps, gavg, st, [interior(pad[:, b, :, :], RAD) for b in range(B)])
                l2_diffuse(nc, a, ps, X, pad, ident)
        if 3 in layers:
            l3(nc, a, ps, X, gavg, ident, st)
        load(nc, "out", [(out.rearrange("b c h w -> c b (h w)"), X[:, :, :])])


def row_tiles(x):
    x = np.concatenate([x] * B, axis=0)
    return np.ascontiguousarray(np.moveaxis(x.reshape(T, 128, *x.shape[1:]), 0, 1))


def layout(v):
    f = np.float32
    a = {}
    c = np.arange(C)
    a["gavg"] = ((c[:, None] // 3 == c[None, :] // 3) / 3).astype(f)
    a["ident"] = np.eye(128, dtype=f)
    p = "L0_conv_"
    a["w_in"] = np.ascontiguousarray(v[p + "in_proj_w"].T)
    a["cw"] = row_tiles(v[p + "conv_w"].reshape(E, TAPS))
    a["cb"] = row_tiles(v[p + "conv_b"])
    image = (np.arange(B * E) // E).reshape(T, 128)
    xp, dp = v[p + "x_proj_w"], v[p + "dt_proj_w"]
    w_bc = np.zeros((128, 2, T, 128), f)
    w_dt = np.zeros((128, T, K, B, R), f)
    w_up = np.zeros((K, B, R, T, K, 128), f)
    xe = row_tiles(np.ascontiguousarray(np.transpose(xp, (2, 0, 1))))
    de = row_tiles(np.ascontiguousarray(np.transpose(dp, (1, 0, 2))))
    for t in range(T):
        for b in range(B):
            rows = image[t] == b
            for k in range(K):
                w_dt[rows, t, k, b] = xe[rows, t, k, 0:R]
                w_up[k, b][:, t, k, rows] = de[rows, t, k].T
                for s in range(2):
                    o = 64 * (k % 2) + 32 * s + N * b
                    w_bc[rows, k // 2, t, o:o + N] = xe[rows, t, k, R + N * s:R + N * (s + 1)]
    a["w_bc"], a["w_dt"] = w_bc, w_dt.reshape(128, T, K * B * R)
    a["w_up"] = w_up.reshape(K * B * R, T * K, 128)
    a["dtb"] = row_tiles(np.ascontiguousarray(v[p + "dt_proj_b"].T))
    a["A"] = row_tiles(np.ascontiguousarray(np.transpose(v[p + "A_log"], (1, 0, 2)))).reshape(128, T * K, N)
    sel = np.zeros((T, 3, B, N, N, 128), f)
    for t in range(T):
        for b in range(B):
            for n in range(N):
                sel[t, :, b, n, n, image[t] == b] = 1
    a["sel"] = sel.reshape(T, 3 * B * N, N * 128).astype(mybir.dt.np(BF16))
    a["Ds"] = row_tiles(np.ascontiguousarray(v[p + "Ds"].T))
    a["gb"] = row_tiles(np.stack([v[p + "ln_g"], v[p + "ln_b"]], 1))
    avg = np.zeros((128, 7, 128), f)
    for i, (src, dst) in enumerate(((0, 0), (1, 0), (0, 1), (1, 1), (2, 1), (1, 2), (2, 2))):
        avg[:, i] = (image[src][:, None] == image[dst][None, :]) / E
    a["avg"] = avg
    a["c1"] = row_tiles(np.ascontiguousarray(v[p + "c1_w"].reshape(2 * E, E).T))
    per = lambda x: np.ascontiguousarray(np.moveaxis(x.reshape(2 * E // 128, 128, -1), 0, 1))
    a["c3"] = per(v[p + "c3_w"].reshape(C, 2 * E).T)
    a["c2"] = per(v[p + "c2_w"].reshape(2 * E, TAPS))
    a["ffn"] = per(np.stack([v[p + n] for n in ("c1_b", "bn1_g", "bn1_b", "bn1_m", "bn1_v",
                                                "c2_b", "bn2_g", "bn2_b", "bn2_m", "bn2_v")], 1))
    a["c3b"] = v[p + "c3_b"].reshape(C, 1)
    a["se1"] = np.ascontiguousarray(v[p + "se1_w"].T)
    a["se2"] = np.ascontiguousarray(v[p + "se2_w"].T)
    seb = np.zeros((C, 2), f)
    seb[0:C // 2, 0], seb[:, 1] = v[p + "se1_b"], v[p + "se2_b"]
    a["seb"] = seb
    i = np.arange(PT * 128)
    ci, cj = i % C, (i % C + i // C) % C
    keep = i < PAIR_ROWS
    for name, key in (("w", "weight"), ("m", "mask")):
        src = v["L1_conv_" + key]
        for n, (p0, p1) in (("a", (ci, cj)), ("b", (cj, ci))):
            g = np.where(keep[:, None], src[:, p0, p1].T, f(0))
            a[name + n] = np.ascontiguousarray(np.moveaxis(g.reshape(PT, 128, C), 0, 1))
    a["l1b"] = v["L1_conv_bias"].reshape(C, 1)
    yy = np.stack(np.divmod(np.arange(KS * KS), KS)) - RAD
    a["grid"] = np.ascontiguousarray(np.broadcast_to(yy.astype(f), (C, 2, KS * KS)))
    a["dm"] = v["L2_conv_diff_metric"].reshape(C, 4)
    layout3(v, a)
    return {k: np.ascontiguousarray(x) for k, x in a.items()}


def transform_basis(n):
    s = np.zeros(n)
    s[1] = s[n - 1] = 1.0
    idx = (np.arange(n)[:, None] - np.arange(n)[None, :]) % n
    S = s[idx] + np.diag(np.fft.fft(s).real)
    r, even = n // 2, 1 - n % 2
    P = np.zeros((n, n))
    P[0, 0] = 1.0
    for i in range(1, r - even + 1):
        P[i, i] = P[i, n - i] = 1 / math.sqrt(2)
    if even:
        P[r, r] = 1.0
    for i in range(r + 1, n):
        P[i, i], P[i, n - i] = -1 / math.sqrt(2), 1 / math.sqrt(2)
    CS = P @ S @ P.T
    h = n // 2 + 1
    ec, vc = np.linalg.eigh(CS[:h, :h])
    es, vs = np.linalg.eigh(CS[h:, h:])
    vc, vs = vc[:, np.argsort(-ec)], vs[:, np.argsort(-es)]
    c2, s2 = P @ np.vstack([vc, np.zeros((n - h, h))]), P @ np.vstack([np.zeros((h, n - h)), vs])
    e = np.zeros((n, n + 1))
    e[:, 0:n + 1:2] = c2
    e[:, 1:n:2] = np.hstack([s2, np.zeros((n, 1))])[:, 0:len(range(1, n, 2))]
    return np.delete(e, n - 1, axis=1)


def layout3(v, a):
    f = np.float32
    p = "L3_conv_"
    w1, b1 = np.zeros((C, HC), f), np.zeros((HC, 1), f)
    w2, b2 = np.zeros((HC, GO), f), np.zeros((1, GO), f)
    for i, (name, c0, o, n) in enumerate((("gsp", 0, O_SP, 2 * C3), ("alpha", C3, O_AL, 1),
                                          ("gfreq", C3, O_FR, 4 * C3), ("gfft", 2 * C3, O_FF, 4 * C3))):
        h = slice(i * HID, (i + 1) * HID)
        w1[c0:c0 + C3, h] = v[p + name + "_w1"].T
        b1[h, 0] = v[p + name + "_b1"]
        w2[h, o:o + n] = v[p + name + "_w2"].T
        b2[0, o:o + n] = v[p + name + "_b2"]
    a["w1"], a["b1"], a["w2"], a["b2"] = w1, b1, w2, b2
    wt = np.zeros((B, C3, 2, 2, 2 * C3), f)
    bw = np.zeros((1, 2, 2, B, C3), f)
    for i, name in enumerate(("conv05", "conv1")):
        wt[:, :, i] = v[p + name + "_w"].reshape(2 * C3, 2, C3).transpose(2, 1, 0)
        bw[:, i] = v[p + name + "_b"].reshape(2, 1, C3)
    a["wt"], a["bw"] = wt.reshape(BC, 2, 2, 2 * C3), bw.reshape(1, 2, 2, BC)
    w0 = v[p + "conv0_w"].transpose(3, 1, 2, 0).reshape(3 * C3, 1, 3, C3)
    a["w0"] = np.repeat(w0, B, axis=1)
    a["cw2"] = v[p + "conv2_w"].transpose(1, 2, 3, 0).reshape(C, TAPS, C)
    a["cb0"], a["cb2"] = v[p + "conv0_b"].reshape(C3, 1), v[p + "conv2_b"].reshape(C, 1)
    lv = np.arange(H)
    lv[-1] = H
    a["lv"] = np.broadcast_to(lv.astype(f), (BC, H))
    e = np.roll(transform_basis(H).astype(f).astype(np.float64), H // 2, axis=1)
    a["ef"], a["ei"] = e.T.astype(f), e.astype(f)
    a["e11"] = np.outer(e.sum(1), e.sum(1)).reshape(1, H * H).astype(f)
    i, k = np.arange(H), np.arange(UH)
    full, half = 2 * np.pi * np.outer(i, i) / H, 2 * np.pi * np.outer(i, k) / W
    a["fh"] = np.concatenate([np.cos(full), -np.sin(full)], 1).astype(f)
    a["fw"] = np.stack([np.concatenate([np.cos(half), -np.sin(half)], 1),
                        np.concatenate([np.sin(half), np.cos(half)], 1)], 1).astype(f)
    a["ih"] = np.concatenate([np.cos(full), np.sin(full)], 1).astype(f)
    wk = np.where((k == 0) | (k == W // 2), 1.0, 2.0)[:, None] / (H * W)
    c, s = wk * np.cos(half.T), wk * np.sin(half.T)
    a["iw"] = np.stack([np.concatenate([c, -s]), np.concatenate([-s, -c])], 1).astype(f)


_OUT = (B, C, H, W)


def kernel(**inputs):
    import concourse.bacc as bacc
    from concourse.bass_utils import run_bass_kernel_spmd

    v = {k: np.asarray(x) for k, x in inputs.items()}
    arrays = layout(v)
    nc = bacc.Bacc("TRN2", target_bir_lowering=False, num_devices=1)
    a, sent = {}, {}
    for name, arr in arrays.items():
        sent[f"in_{name}"] = arr
        a[name] = nc.dram_tensor(f"in_{name}", arr.shape, mybir.dt.from_np(arr.dtype), kind="ExternalInput").ap()
    sent["in_x"] = np.ascontiguousarray(v["x"])
    x = nc.dram_tensor("in_x", _OUT, F32, kind="ExternalInput").ap()
    out = nc.dram_tensor("out_0", _OUT, F32, kind="ExternalOutput").ap()
    program(nc, a, x, out)
    r = run_bass_kernel_spmd(nc, [sent], core_ids=[0])
    return r.results[0]["out_0"]
```

```python
from contextlib import ExitStack
import math

import numpy as np

import concourse.bass as bass
from concourse import mybir

F32 = mybir.dt.float32
BF16 = mybir.dt.bfloat16
I32 = mybir.dt.int32
ALU = mybir.AluOpType
ACT = mybir.ActivationFunctionType
AX = mybir.AxisListType

B, C, H, W = 2, 96, 48, 48
L = H * W
E = 2 * C
T = B * E // 128
R, N = 6, 16
K = 4
CH = 8 * W
NC = L // CH
BANK = 512
SEG = 2 * CH
NSEG = L // SEG
PW = W + 2
LOG_FLOOR = math.log(1e12)
PAIR_ROWS = (C // 2) * C + C // 2
PT = -(-PAIR_ROWS // 128)
TAPS = 9
C3 = C // 3
HID = 8
UH = W // 2 + 1


class Steps:

    def __init__(self, eng, sem):
        self.eng, self.sem, self.n = eng, sem, 0

    def __call__(self, ins):
        self.n += 1
        ins.then_inc(self.sem, 1)
        self.eng.wait_ge(self.sem, self.n)


def space(nc, ctx, tag):
    numbers = []

    def sb(name, shape, dt=F32):
        return ctx.enter_context(nc.sbuf_tensor(f"{tag}_{name}", shape, dt))

    def sem(name):
        s = ctx.enter_context(nc.semaphore(f"{tag}_{name}"))
        numbers.append(s.num)
        return s

    def clear():
        run = []
        for n in sorted(numbers) + [None]:
            if run and n != run[-1] + 1:
                nc.gpsimd.sem_clear(range(run[0], run[-1] + 1))
                run = []
            run.append(n)

    ctx.callback(clear)
    return sb, sem


def by_image(ap):
    return ap.rearrange("p (h w) -> p h w", w=W)


def interior(pad, border=1):
    return pad[:, border:border + H, border:border + W]


def scan_order(ap, k):
    v = ap[:, ::-1] if k % 2 else ap
    return v.rearrange("p (w h) -> p h w", h=H) if k >= 2 else v.rearrange("p (h w) -> p h w", w=W)


def banks(ps, first, count):
    return ps[:, first * BANK:(first + count) * BANK].rearrange("p (c n) -> p c n", n=BANK)[:, :, 0:CH]


def banks_hw(ps, first, count):
    return banks(ps, first, count).rearrange("p c (h w) -> p c h w", w=W)


def rsqrt_newton(step, dve, out, v, t1, t2):
    step(dve.tensor_tensor(t1, out, out, ALU.mult))
    step(dve.tensor_tensor(t2, t1, v, ALU.mult))
    step(dve.tensor_scalar(t1, t2, -0.5, 1.5, ALU.mult, ALU.add))


def group_norm(nc, tag, X, ps, gavg, st, outs, eps=1e-5):
    with ExitStack() as ctx:
        sb, sem = space(nc, ctx, tag)
        bn = sb("bn", [C, B, NC, 6])
        d, sq, var, t1, t2 = (sb(n, [C, B]) for n in ("d", "sq", "var", "t1", "t2"))
        s_dve, s_stat, s_mean, s_spread, s_var, s_inv, s_root = map(
            sem, ("dve", "stat", "mean", "spread", "var", "inv", "root"))
        mv, rstd, shift = st["mv"], st["rstd"], st["shift"]
        block = ctx.enter_context(nc.Block())

        @block.vector
        def _(dve):
            step = Steps(dve, s_dve)
            for b in range(B):
                for c in range(NC):
                    last = dve.bn_stats(bn[:, b, c, :], X[:, b, c * CH:(c + 1) * CH])
                step(last)
                ins = dve.bn_aggr(mv[:, b, :], bn[:, b, :, :].rearrange("p c s -> p (c s)"))
                ins.then_inc(s_stat, 1)
            dve.wait_ge(s_stat, B)
            dve.wait_ge(s_mean, 1)
            step(dve.tensor_tensor(d[:, :], mv[:, :, 0], ps[0:C, 0:B], ALU.subtract))
            step(dve.tensor_tensor(sq[:, :], d[:, :], d[:, :], ALU.mult))
            dve.tensor_tensor(sq[:, :], sq[:, :], mv[:, :, 1], ALU.add).then_inc(s_spread, 1)
            dve.wait_ge(s_var, 1)
            step(dve.tensor_scalar(var[:, :], ps[0:C, BANK:BANK + B], eps, None, ALU.add))
            dve.reciprocal(t1[:, :], var[:, :]).then_inc(s_inv, 1)
            dve.wait_ge(s_root, 1)
            rsqrt_newton(step, dve, rstd[:, :], var[:, :], t1[:, :], t2[:, :])
            step(dve.tensor_tensor(rstd[:, :], rstd[:, :], t1[:, :], ALU.mult))
            step(dve.tensor_scalar(t2[:, :], ps[0:C, 0:B], -1.0, None, ALU.mult))
            step(dve.tensor_tensor(shift[:, :], t2[:, :], rstd[:, :], ALU.mult))
            for b in range(B):
                ins = dve.tensor_scalar(outs[b], by_image(X[:, b, :]), rstd[:, b:b + 1], shift[:, b:b + 1],
                                        ALU.mult, ALU.add)
            step(ins)

        @block.tensor
        def _(pe):
            pe.wait_ge(s_stat, B)
            pe.matmul(ps[0:C, 0:B], gavg[:, :], mv[:, :, 0], start=True, stop=True).then_inc(s_mean, 1)
            pe.wait_ge(s_spread, 1)
            pe.matmul(ps[0:C, BANK:BANK + B], gavg[:, :], sq[:, :], start=True, stop=True).then_inc(s_var, 1)

        @block.scalar
        def _(act):
            act.wait_ge(s_inv, 1)
            act.activation(rstd[:, :], t1[:, :], ACT.Sqrt).then_inc(s_root, 1)


def load(nc, tag, pairs):
    with ExitStack() as ctx:
        _, sem = space(nc, ctx, tag)
        s_in = sem("in")
        block = ctx.enter_context(nc.Block())

        @block.sync
        def _(sp):
            for dst, src in pairs:
                sp.dma_start(dst, src).then_inc(s_in, 16)
            sp.wait_ge(s_in, 16 * len(pairs))




def l0_project(nc, a, X, XG, ps, XI, Z):
    with ExitStack() as ctx:
        sb, sem = space(nc, ctx, "l0p")
        w_in = sb("w_in", [C, 2 * E])
        cw = sb("cw", [128, T, TAPS])
        cb = sb("cb", [128, T])
        pad = sb("pad", [128, T, PW, PW])
        acc = sb("acc", [128, T, L])
        s_in, s_pad, s_mm, s_ev, s_evz, s_tap = map(sem, ("in", "pad", "mm", "ev", "evz", "tap"))
        block = ctx.enter_context(nc.Block())
        parts = [[(0, 128, 0, 0)], [(0, 64, 128, 0), (64, 128, 0, 1)], [(0, 128, 64, 1)]]

        @block.sync
        def _(sp):
            sp.dma_start(w_in[:, :], a["w_in"]).then_inc(s_in, 16)
            sp.dma_start(cw[:, :, :], a["cw"]).then_inc(s_in, 16)
            sp.dma_start(cb[:, :], a["cb"]).then_inc(s_in, 16)
            sp.wait_ge(s_in, 48)

        @block.tensor
        def _(pe):
            pe.wait_ge(s_in, 48)
            for j in range(2 * T):
                half, t = divmod(j, T)
                for c in range(NC):
                    q = j * NC + c
                    if q >= 8:
                        pe.wait_ge(s_ev, q - 7)
                    for lo, hi, w0, b in parts[t]:
                        mm = pe.matmul(ps[lo:hi, (q % 8) * BANK:(q % 8) * BANK + CH],
                                       w_in[:, half * E + w0:half * E + w0 + hi - lo],
                                       XG[:, b, c * CH:(c + 1) * CH], start=True, stop=True)
                    mm.then_inc(s_mm, 1)

        @block.scalar
        def _(act):
            act.wait_ge(s_pad, T)
            for j in range(2 * T):
                half, t = divmod(j, T)
                for c in range(NC):
                    q = j * NC + c
                    act.wait_ge(s_mm, q + 1)
                    src = ps[:, (q % 8) * BANK:(q % 8) * BANK + CH]
                    if half:
                        act.copy(Z[:, t, c * CH:(c + 1) * CH], src).then_inc(s_ev, 1)
                    else:
                        act.copy(pad[:, t, 1 + 8 * c:9 + 8 * c, 1:1 + W],
                                 src.rearrange("p (h w) -> p h w", w=W)).then_inc(s_ev, 1)
            act.wait_ge(s_in, 48)
            for t in range(T):
                act.wait_ge(s_tap, TAPS * (t + 1))
                ins = act.activation(XI[:, t, :], acc[:, t, :], ACT.Silu, bias=cb[:, t:t + 1])
            ins.then_inc(s_evz, 1)
            act.wait_ge(s_evz, 1)

        @block.vector
        def _(dve):
            for t in range(T):
                dve.memset(pad[:, t, :, :], 0.0).then_inc(s_pad, 1)
            dve.wait_ge(s_in, 48)
            for t in range(T):
                dve.wait_ge(s_ev, NC * (t + 1))
                for i in range(TAPS):
                    dy, dx = divmod(i, 3)
                    src = pad[:, t, dy:dy + H, dx:dx + W]
                    dst = by_image(acc[:, t, :])
                    if i == 0:
                        ins = dve.tensor_scalar(dst, src, cw[:, t, 0:1], None, ALU.mult)
                    else:
                        dve.wait_ge(s_tap, TAPS * t + i)
                        ins = dve.scalar_tensor_tensor(dst, src, cw[:, t, i:i + 1], dst, ALU.mult, ALU.add)
                    ins.then_inc(s_tap, 1)


def l0_rows(nc, a, ps, XI, P, d):
    with ExitStack() as ctx:
        sb, sem = space(nc, ctx, "l0r")
        w_bc = sb("w_bc", [128, 2, T, 128])
        w_dt = sb("w_dt", [128, T, K * B * R])
        al = sb("al", [128, K * T, N])
        na = sb("na", [128, K * T, 2 * N])
        bc = sb("bc", [128, 2, L])
        rest = sb("rest", [128, L])
        parts = sb("parts", [128, 2, 3, L], BF16)
        wa, wb, mask = (sb(n, [128, PT, C]) for n in ("wa", "wb", "mask"))
        s_wa, s_wb, s_ma, s_mb, s_pair, s_wout = map(sem, "wa wb ma mb pair wout".split())
        s_in, s_bc, s_bce, s_hi, s_mid, s_lo, s_rest, s_pm, s_pe, s_na, s_out = map(
            sem, "in bc bce hi mid lo rest pm pe na out".split())
        block = ctx.enter_context(nc.Block())

        @block.sync
        def _(sp):
            for dst, src in ((w_bc[:, :, :, :], a["w_bc"]), (w_dt[:, :, :], a["w_dt"]), (al[:, :, :], a["A"])):
                sp.dma_start(dst, src).then_inc(s_in, 16)
            for dst, src, s_done in ((wa, "wa", s_wa), (mask, "ma", s_ma), (wb, "wb", s_wb)):
                sp.dma_start(dst[:, :, :], a[src]).then_inc(s_done, 16)
            sp.wait_ge(s_na, 2)
            sp.dma_start(d["na"].rearrange("g p n -> p g n"), na[:, :, :]).then_inc(s_out, 16)
            sp.wait_ge(s_pair, 1)
            sp.dma_start(mask[:, :, :], a["mb"]).then_inc(s_mb, 16)
            for m in range(2):
                for i, s_part in enumerate((s_hi, s_mid, s_lo)):
                    sp.wait_ge(s_part, m + 1)
                    for r in range(4):
                        k, s = 2 * m + r // 2, r % 2
                        sp.dma_start(d["bc"][k, s, i * B * N:(i + 1) * B * N, :],
                                     parts[32 * r:32 * r + 32, m, i, :]).then_inc(s_out, 16)
            sp.wait_ge(s_pair, 4)
            sp.dma_start(d["pairs"], wa[:, :, :]).then_inc(s_wout, 16)
            sp.wait_ge(s_out, 16 * 25)
            sp.wait_ge(s_wout, 16)

        @block.gpsimd
        def _(pool):
            pool.wait_ge(s_wa, 16)
            pool.wait_ge(s_ma, 16)
            pool.tensor_tensor(wa[:, :, :], wa[:, :, :], mask[:, :, :], ALU.mult).then_inc(s_pair, 1)
            pool.wait_ge(s_wb, 16)
            pool.wait_ge(s_mb, 16)
            pool.tensor_tensor(wb[:, :, :], wb[:, :, :], mask[:, :, :], ALU.mult).then_inc(s_pair, 1)
            pool.wait_ge(s_pair, 2)
            pool.tensor_tensor(wa[:, 1:, :], wa[:, 1:, :], wb[:, 1:, :], ALU.add).then_inc(s_pair, 1)
            pool.wait_ge(s_pair, 3)
            pool.tensor_tensor(wa[C:128, 0, :], wa[C:128, 0, :], wb[C:128, 0, :], ALU.add).then_inc(s_pair, 1)

        @block.tensor
        def _(pe):
            pe.wait_ge(s_in, 48)
            for m in range(2):
                if m:
                    pe.wait_ge(s_bce, 2)
                for c in range(NC):
                    for t in range(T):
                        mm = pe.matmul(ps[:, c * BANK:c * BANK + CH], w_bc[:, m, t, :],
                                       XI[:, t, c * CH:(c + 1) * CH], start=(t == 0), stop=(t == T - 1))
                mm.then_inc(s_bc, 1)
            pe.wait_ge(s_bce, 4)
            for c in range(NC):
                for t in range(T):
                    mm = pe.matmul(ps[0:K * B * R, c * BANK:c * BANK + CH], w_dt[:, t, :],
                                   XI[:, t, c * CH:(c + 1) * CH], start=(t == 0), stop=(t == T - 1))
            mm.then_inc(s_pm, 1)

        @block.scalar
        def _(act):
            act.wait_ge(s_in, 48)
            act.mul(na[:, :, 0:N], al[:, :, :], -1.0).then_inc(s_na, 1)
            act.mul(na[:, :, N:2 * N], al[:, :, :], -0.5).then_inc(s_na, 1)
            for m in range(2):
                act.wait_ge(s_bc, m + 1)
                for r in range(2):
                    k = 2 * m + r
                    for c in range(NC):
                        ins = act.copy(scan_order(bc[:, m, :], k)[64 * r:64 * r + 64, 8 * c:8 * c + 8, :],
                                       ps[64 * r:64 * r + 64, c * BANK:c * BANK + CH]
                                       .rearrange("p (h w) -> p h w", w=W))
                    ins.then_inc(s_bce, 1)
                act.wait_ge(s_bce, 2 * m + 2)
                act.copy(parts[:, m, 0, :], bc[:, m, :]).then_inc(s_hi, 1)
                act.wait_ge(s_rest, m + 1)
                act.copy(parts[:, m, 1, :], rest[:, :]).then_inc(s_mid, 1)
            act.wait_ge(s_pm, 1)
            act.copy(P[:, :].rearrange("p (c n) -> p c n", n=CH), banks(ps, 0, NC)[0:K * B * R]).then_inc(s_pe, 1)

        @block.vector
        def _(dve):
            for m in range(2):
                dve.wait_ge(s_hi, m + 1)
                if m:
                    dve.wait_ge(s_lo, m)
                dve.tensor_tensor(rest[:, :], bc[:, m, :], parts[:, m, 0, :], ALU.subtract).then_inc(s_rest, 1)
                dve.wait_ge(s_mid, m + 1)
                dve.wait_ge(s_rest, m + 1)
                dve.tensor_tensor(parts[:, m, 2, :], rest[:, :], parts[:, m, 1, :], ALU.subtract).then_inc(s_lo, 1)


def l0_steps(nc, a, ps, XI, P, d):
    with ExitStack() as ctx:
        sb, sem = space(nc, ctx, "l0s")
        w_up = sb("w_up", [K * B * R, K * T, 128])
        dtb = sb("dtb", [128, T, K])
        x0, e, ln, wm, dl, vv = (sb(n, [128, 2, L]) for n in ("x0", "e", "ln", "wm", "dl", "vv"))
        s_in, s_up, s_x0, s_ab, s_e, s_ln, s_wm, s_c, s_min, s_dl, s_vv = map(
            sem, "in up x0 ab e ln wm c min dl vv".split())
        s_store = [sem(f"store{i}") for i in range(2)]
        G = K * T
        block = ctx.enter_context(nc.Block())

        @block.sync
        def _(sp):
            sp.dma_start(w_up[:, :, :], a["w_up"]).then_inc(s_in, 16)
            sp.dma_start(dtb[:, :, :], a["dtb"]).then_inc(s_in, 16)
            for g in range(G):
                sp.wait_ge(s_dl, g + 1)
                sp.dma_start(d["dlt"][g], dl[:, g % 2, :]).then_inc(s_store[g % 2], 16)
                sp.wait_ge(s_vv, g + 1)
                sp.dma_start(d["v"][g], vv[:, g % 2, :]).then_inc(s_store[g % 2], 16)
            for i in range(2):
                sp.wait_ge(s_store[i], 32 * (G // 2))

        @block.tensor
        def _(pe):
            pe.wait_ge(s_in, 32)
            for g in range(G):
                for half in range(2):
                    q = 2 * g + half
                    if q >= 2:
                        pe.wait_ge(s_x0, q - 1)
                    for c in range(3 * half, 3 * half + 3):
                        mm = pe.matmul(ps[:, c * BANK:c * BANK + CH], w_up[:, g, :],
                                       P[:, c * CH:(c + 1) * CH], start=True, stop=True)
                    mm.then_inc(s_up, 1)

        @block.scalar
        def _(act):
            act.wait_ge(s_in, 32)
            for g in range(G):
                t, k, i = g // K, g % K, g % 2
                if g >= 2:
                    act.wait_ge(s_dl, g - 1)
                for half in range(2):
                    act.wait_ge(s_up, 2 * g + half + 1)
                    for c in range(3 * half, 3 * half + 3):
                        ins = act.activation(scan_order(x0[:, i, :], k)[:, 8 * c:8 * c + 8, :],
                                             ps[:, c * BANK:c * BANK + CH].rearrange("p (h w) -> p h w", w=W),
                                             ACT.Identity, bias=dtb[:, t, k:k + 1])
                    ins.then_inc(s_x0, 1)
                act.wait_ge(s_x0, 2 * g + 2)
                act.activation(e[:, i, :], x0[:, i, :], ACT.Abs).then_inc(s_ab, 1)
                act.wait_ge(s_ab, g + 1)
                act.activation(e[:, i, :], e[:, i, :], ACT.Exp, scale=-1.0).then_inc(s_e, 1)
                act.wait_ge(s_e, g + 1)
                act.activation(ln[:, i, :], e[:, i, :], ACT.Ln, bias=1.0).then_inc(s_ln, 1)

        @block.vector
        def _(dve):
            for g in range(G):
                t, k, i = g // K, g % K, g % 2
                dve.wait_ge(s_e, g + 1)
                dve.tensor_scalar(wm[:, i, :], e[:, i, :], 1.0, -1.0, ALU.add, ALU.add).then_inc(s_wm, 1)
                dve.wait_ge(s_c, g + 1)
                dve.wait_ge(s_ln, g + 1)
                dve.tensor_tensor(ln[:, i, :], ln[:, i, :], wm[:, i, :], ALU.add).then_inc(s_min, 1)
                dve.wait_ge(s_min, 2 * g + 1)
                dve.tensor_tensor(ln[:, i, :], ln[:, i, :], e[:, i, :], ALU.min).then_inc(s_min, 1)
                dve.wait_ge(s_min, 2 * g + 2)
                if g >= 2:
                    dve.wait_ge(s_store[i], 32 * (g // 2))
                dve.scalar_tensor_tensor(dl[:, i, :], x0[:, i, :], 0.0, ln[:, i, :], ALU.max, ALU.add
                                         ).then_inc(s_dl, 1)
                dve.wait_ge(s_dl, g + 1)
                dve.tensor_tensor(scan_order(vv[:, i, :], k), by_image(XI[:, t, :]), scan_order(dl[:, i, :], k),
                                  ALU.mult).then_inc(s_vv, 1)

        @block.gpsimd
        def _(pool):
            for g in range(G):
                i = g % 2
                pool.wait_ge(s_wm, g + 1)
                pool.tensor_tensor(wm[:, i, :], e[:, i, :], wm[:, i, :], ALU.subtract).then_inc(s_c, 1)


def l0_scan(nc, a, ps, ident, d):
    with ExitStack() as ctx:
        sb, sem = space(nc, ctx, "l0c")
        NR, NDA, NHV, NHP = 6, 4, 4, 2
        SPAN = 6
        AHEAD = 3
        dlt, v, S, y = (sb(n, [128, 2, SEG]) for n in ("dlt", "v", "S", "y"))
        Bp, Cp = (sb(n, [3 * B * N, 2, SEG], BF16) for n in ("Bp", "Cp"))
        sel = sb("sel", [3 * B * N, 2, N * 128], BF16)
        na = sb("na", [128, 2, 2 * N])
        da = sb("da", [128, NDA, SEG])
        r = sb("r", [128, NR, SEG])
        h = sb("h", [128, N, SEG])
        hcv = sb("hcv", [128, NHV, SEG])
        hcp = sb("hcp", [128, NHP, SEG])
        cs = sb("cs", [128, NHP, SEG])
        credit = sb("credit", [128, 8])
        floor = sb("floor", [128, 1])
        s_in = [sem(f"in{i}") for i in range(2)]
        s_sel = [sem(f"sel{i}") for i in range(2)]
        s_yout = [sem(f"yout{i}") for i in range(2)]
        s_scan, s_ub, s_hv, s_hp, s_cc, s_y, s_evac = map(sem, ("scan", "ub", "hv", "hp", "cc", "y", "evac"))
        s_a, s_tanh, s_w, s_b, s_c, s_S, s_init = map(sem, ("a", "tanh", "w", "b", "c", "S", "init"))
        HP0 = 6
        PB, PC, PY = 0, 2, 4
        block = ctx.enter_context(nc.Block())
        U = 2 * NSEG
        J = U * N
        NLOAD = 5

        def nest(eng):
            return eng.Fori(0, T), eng.Fori(0, K // 2)

        def by_pool(j):
            return j % 3 == 2

        def dve_steps(j):
            return 2 * (j // 3) + j % 3

        def chunks(ap):
            return ap.rearrange("p (c n) -> p c n", n=CH)

        @block.sync
        def _(sp):
            lt, lq = nest(sp)
            with lt as t, lq as q:
                for u in range(U):
                    g = t * (2 * U) + q * U + u
                    kt = t * K + q * 2 + u // NSEG
                    c0 = (u % NSEG) * SEG
                    i = u % 2
                    sp.wait_ge(s_evac, g + 1)
                    sp.dma_start(dlt[:, i, :], d["dlt"][kt, :, c0:c0 + SEG]).then_inc(s_in[i], 16)
                    sp.dma_start(na[:, i, :], d["na"][kt]).then_inc(s_in[i], 16)
                    sp.dma_start(Bp[:, i, :], d["bc"][q * 2 + u // NSEG, 0, :, c0:c0 + SEG]).then_inc(s_in[i], 16)
                    if u < 2:
                        sp.dma_start(sel[:, i, :], a["sel"][t]).then_inc(s_sel[i], 16)
                    sp.dma_start(v[:, i, :], d["v"][kt, :, c0:c0 + SEG]).then_inc(s_in[i], 16)
                    sp.dma_start(Cp[:, i, :], d["bc"][q * 2 + u // NSEG, 1, :, c0:c0 + SEG]).then_inc(s_in[i], 16)
            for i in range(2):
                sp.wait_ge(s_in[i], 16 * NLOAD * K * T * NSEG // 2)
                sp.wait_ge(s_sel[i], 16 * 2 * T)

        @block.tensor
        def _(pe):
            lt, lq = nest(pe)
            with lt as t, lq as q:
                base = t * (2 * J) + q * J
                vbase = t * (2 * dve_steps(J)) + q * dve_steps(J)
                pbase = t * (2 * J // 3) + q * (J // 3)
                segs = t * (2 * U) + q * U

                def spread(rows, first, j, done):
                    i, n = (j // N) % 2, j % N
                    for c in range(2):
                        mm = pe.matmul(ps[:, (first + c) * BANK:(first + c) * BANK + CH],
                                       sel[:, i, n * 128:(n + 1) * 128], rows[:, i, c * CH:(c + 1) * CH],
                                       start=True, stop=True)
                    mm.then_inc(done, 1)

                def b_rows(j):
                    u = j // N
                    if j % N == 0:
                        pe.wait_ge(s_in[u % 2], (t * U + q * (U // 2) + u // 2 + 1) * (16 * NLOAD))
                        if u < 2:
                            pe.wait_ge(s_sel[u], (t * 2 + q + 1) * 16)
                    pe.wait_ge(s_ub, base + j + 1)
                    spread(Bp, PB, j, s_b)

                def c_rows(j):
                    if j % 3 == 0:
                        pe.wait_ge(s_cc, pbase + j // 3 + 1)
                    else:
                        pe.wait_ge(s_hv, vbase + dve_steps(j))
                    spread(Cp, PC, j, s_c)

                def add_y(j):
                    u, n = j // N, j % N
                    if n == 0:
                        pe.wait_ge(s_evac, segs + u + 1)
                    if by_pool(j):
                        pe.wait_ge(s_hp, pbase + j // 3 + 1 + HP0)
                        hc = hcp[:, (j // 3) % NHP, :]
                    else:
                        pe.wait_ge(s_hv, vbase + dve_steps(j) + 1)
                        hc = hcv[:, dve_steps(j) % NHV, :]
                    for c in range(2):
                        o = (PY + 2 * (u % 2) + c) * BANK
                        mm = pe.matmul(ps[:, o:o + CH], ident[:, :], hc[:, c * CH:(c + 1) * CH],
                                       start=(n == 0), stop=(n == N - 1))
                    mm.then_inc(s_y, 1)

                for j in range(AHEAD + 1):
                    b_rows(j)
                for j in range(J + 3):
                    if j < J:
                        c_rows(j)
                    if j + AHEAD + 1 < J:
                        b_rows(j + AHEAD + 1)
                    if j >= 3:
                        add_y(j - 3)

        @block.vector
        def _(dve):
            dve.memset(floor[:, :], 0.5 * LOG_FLOOR).then_inc(s_init, 1)
            for i, (s, n) in enumerate(((s_scan, NR), (s_ub, 1), (s_cc, 1), (s_hp, HP0), (s_y, SPAN), (s_evac, 2),
                                        (s_yout[0], 16), (s_yout[1], 16))):
                dve.memset(credit[:, i:i + 1], 0.0).then_inc(s, n)
            lt, lq = nest(dve)
            with lt as t, lq as q:
                base = t * (2 * J) + q * J
                pbase = t * (2 * J // 3) + q * (J // 3)
                segs = t * (2 * U) + q * U
                loads = t * U + q * (U // 2)

                def cumsum(u):
                    i = u % 2
                    dve.wait_ge(s_in[i], (loads + u // 2 + 1) * (16 * NLOAD))
                    if u % NSEG:
                        dve.wait_ge(s_S, segs + u)
                        init = S[:, 1 - i, SEG - 1:SEG]
                    else:
                        init = 0.0
                    dve.tensor_tensor_scan(S[:, i, :], dlt[:, i, :], dlt[:, i, :], init, ALU.add, ALU.bypass
                                           ).then_inc(s_S, 1)

                def b_r(j):
                    dve.wait_ge(s_tanh, base + j + 1)
                    dve.wait_ge(s_b, base + j + 1)
                    rj = chunks(r[:, j % NR, :])
                    dve.scalar_tensor_tensor(rj, rj, 1.0, banks(ps, PB, 2), ALU.add, ALU.mult).then_inc(s_ub, 1)

                def times_c(j):
                    dve.wait_ge(s_scan, base + j + NR + 1)
                    dve.wait_ge(s_c, base + j + 1)
                    dve.wait_ge(s_y, base + j + 1)
                    dve.tensor_tensor(chunks(hcv[:, dve_steps(j) % NHV, :]), banks(ps, PC, 2), chunks(h[:, j % N, :]),
                                      ALU.mult).then_inc(s_hv, 1)

                cumsum(0)
                for j in range(AHEAD):
                    b_r(j)
                for j in range(J):
                    u, n = j // N, j % N
                    if j + AHEAD < J:
                        b_r(j + AHEAD)
                    if j and not by_pool(j - 1):
                        times_c(j - 1)
                    if n == 10 and u + 1 < U:
                        cumsum(u + 1)
                    dve.wait_ge(s_a, base + j + 1)
                    dve.wait_ge(s_w, base + j + 1)
                    if j % 3 == 0:
                        dve.wait_ge(s_hp, pbase + j // 3 + 1)
                    if u % NSEG:
                        dve.wait_ge(s_scan, base + j - N + 1 + NR)
                        init = h[:, n, SEG - 1:SEG]
                    else:
                        init = 0.0
                    dve.tensor_tensor_scan(h[:, n, :], da[:, j % NDA, :], r[:, j % NR, :], init, ALU.mult, ALU.add
                                           ).then_inc(s_scan, 1)
                assert by_pool(J - 1)

        @block.gpsimd
        def _(pool):
            lt, lq = nest(pool)
            with lt as t, lq as q:
                base = t * (2 * J) + q * J
                pbase = t * (2 * J // 3) + q * (J // 3)
                for j in range(J + AHEAD + 1):
                    if j < J:
                        if j % N == 0:
                            pool.wait_ge(s_in[(j // N) % 2], (t * U + q * (U // 2) + j // N // 2 + 1) * (16 * NLOAD))
                        pool.wait_ge(s_ub, base + j + 2)
                        pool.tensor_tensor(r[:, j % NR, :], r[:, j % NR, :], v[:, (j // N) % 2, :], ALU.mult
                                           ).then_inc(s_w, 1)
                    e = j - AHEAD - 1
                    if e >= 0 and by_pool(e):
                        pool.wait_ge(s_scan, base + e + NR + 1)
                        pool.wait_ge(s_cc, pbase + e // 3 + 2)
                        pool.wait_ge(s_y, base + e + 1)
                        pool.tensor_tensor(hcp[:, (e // 3) % NHP, :], cs[:, (e // 3) % NHP, :], h[:, e % N, :],
                                           ALU.mult).then_inc(s_hp, 1)

        @block.scalar
        def _(act):
            act.wait_ge(s_init, 1)
            lt, lq = nest(act)
            with lt as t, lq as q:
                base = t * (2 * J) + q * J
                pbase = t * (2 * J // 3) + q * (J // 3)
                segs = t * (2 * U) + q * U

                def store(u):
                    i = u % 2
                    act.wait_ge(s_y, base + (u + 1) * N + SPAN)
                    act.wait_ge(s_yout[i], (t * U + q * (U // 2) + u // 2 + 1) * 16)
                    act.activation(chunks(y[:, i, :]), banks(ps, PY + 2 * i, 2), ACT.Copy, scale=0.5).then_inc(s_evac, 1)
                    act.wait_ge(s_evac, segs + u + 3)
                    kt = t * K + q * 2 + u // NSEG
                    c0 = (u % NSEG) * SEG
                    act.dma_start(d["y"][kt, :, c0:c0 + SEG], y[:, i, :]).then_inc(s_yout[i], 16)

                for j in range(J + 6):
                    u, n, i = j // N, j % N, (j // N) % 2
                    if j < J:
                        if n == 0:
                            act.wait_ge(s_in[i], (t * U + q * (U // 2) + u // 2 + 1) * (16 * NLOAD))
                            act.wait_ge(s_S, segs + u + 1)
                        act.wait_ge(s_scan, base + j + 1)
                        act.activation(r[:, j % NR, :], S[:, i, :], ACT.Tanh, bias=floor[:, :],
                                       scale=na[:, i, N + n:N + n + 1]).then_inc(s_tanh, 1)
                    e = j - 2
                    if 0 <= e < J:
                        ie, ne = (e // N) % 2, e % N
                        act.wait_ge(s_scan, base + e + 1 + NR - NDA)
                        act.activation(da[:, e % NDA, :], dlt[:, ie, :], ACT.Exp,
                                       scale=na[:, ie, ne:ne + 1]).then_inc(s_a, 1)
                    e = j - 5
                    if 0 <= e < J and by_pool(e):
                        act.wait_ge(s_c, base + e + 1)
                        act.wait_ge(s_hp, pbase + e // 3 + 1 + HP0 - NHP)
                        act.copy(chunks(cs[:, (e // 3) % NHP, :]), banks(ps, PC, 2)).then_inc(s_cc, 1)
                    if n == 8 and 0 < u < U:
                        store(u - 1)
                store(U - 1)
            for i in range(2):
                act.wait_ge(s_yout[i], 16 * (K * T * NSEG // 2 + 1))


def l0_norm(nc, a, ps, Z, Y, d):
    with ExitStack() as ctx:
        sb, sem = space(nc, ctx, "l0n")
        yk = sb("yk", [128, 3, L])
        Ds = sb("Ds", [128, T, K])
        dsum, eps = sb("dsum", [128, T]), sb("eps", [128, 1])
        gb = sb("gb", [128, T, 2])
        avg = sb("avg", [128, 7, 128])
        sq = sb("sq", [128, T, L])
        iv = sb("iv", [128, T, L])
        s_in, s_dve, s_mean, s_yc, s_sq, s_var, s_inv, s_root, s_n, s_aff, s_add = map(
            sem, "in dve mean yc sq var inv root n aff add".split())
        s_y = sem("y")
        s_k = [sem(f"k{i}") for i in range(3)]
        mix = [[(0, 0), (1, 1)], [(0, 2), (1, 3), (2, 4)], [(1, 5), (2, 6)]]
        adds = [(t, k) for t in range(T) for k in range(1, K)]
        block = ctx.enter_context(nc.Block())

        @block.sync
        def _(sp):
            for dst, src in ((Ds[:, :, :], a["Ds"]), (gb[:, :, :], a["gb"]), (avg[:, :, :], a["avg"])):
                sp.dma_start(dst, src).then_inc(s_in, 16)
            for t in range(T):
                sp.dma_start(Y[:, t, :], d["y"][t * K]).then_inc(s_y, 16)
            for j, (t, k) in enumerate(adds):
                if j >= 3:
                    sp.wait_ge(s_add, j - 2)
                sp.dma_start(yk[:, j % 3, :], d["y"][t * K + k]).then_inc(s_k[j % 3], 16)

        @block.tensor
        def _(pe):
            pe.wait_ge(s_in, 48)
            pe.wait_ge(s_add, len(adds))
            for base, src, s_src, s_done, s_free in ((0, Y, s_add, s_mean, s_yc), (0, sq, s_sq, s_var, s_inv)):
                for q in range(T * NC):
                    t, c = divmod(q, NC)
                    if q >= 8:
                        pe.wait_ge(s_free, q - 7)
                    elif s_src is s_sq:
                        pe.wait_ge(s_sq, T)
                    o = (q % 8) * BANK
                    for m, (f, blk) in enumerate(mix[t]):
                        mm = pe.matmul(ps[:, o:o + CH], avg[:, blk, :], src[:, f, c * CH:(c + 1) * CH],
                                       start=(m == 0), stop=(m == len(mix[t]) - 1))
                    mm.then_inc(s_done, 1)

        @block.scalar
        def _(act):
            for t in range(T):
                act.wait_ge(s_yc, NC * (t + 1))
                act.activation(sq[:, t, :], iv[:, t, :], ACT.Square).then_inc(s_sq, 1)
            act.wait_ge(s_in, 48)
            for t in range(T):
                act.wait_ge(s_inv, NC * (t + 1))
                act.activation(yk[:, t, :], yk[:, t, :], ACT.Sqrt).then_inc(s_root, 1)
            for t in range(T):
                act.wait_ge(s_n, t + 1)
                act.activation(yk[:, t, :], yk[:, t, :], ACT.Identity, scale=gb[:, t, 0:1],
                               bias=gb[:, t, 1:2]).then_inc(s_aff, 1)

        @block.vector
        def _(dve):
            step = Steps(dve, s_dve)
            dve.wait_ge(s_in, 48)
            step(dve.tensor_reduce(dsum[:, :], Ds[:, :, :], AX.X, ALU.add))
            dve.wait_ge(s_y, 16 * T)
            for j, (t, k) in enumerate(adds):
                dve.wait_ge(s_k[j % 3], 16 * (j // 3 + 1))
                if j:
                    dve.wait_ge(s_add, j)
                dst = by_image(Y[:, t, :])
                src = scan_order(yk[:, j % 3, :], k)
                if k == 1:
                    ins = dve.scalar_tensor_tensor(dst, src, dsum[:, t:t + 1], dst, ALU.add, ALU.add)
                else:
                    ins = dve.tensor_tensor(dst, src, dst, ALU.add)
                ins.then_inc(s_add, 1)
            for q in range(T * NC):
                t, c = divmod(q, NC)
                dve.wait_ge(s_mean, q + 1)
                o = (q % 8) * BANK
                cs = slice(c * CH, (c + 1) * CH)
                dve.tensor_tensor(iv[:, t, cs], Y[:, t, cs], ps[:, o:o + CH], ALU.subtract).then_inc(s_yc, 1)
            for q in range(T * NC):
                t, c = divmod(q, NC)
                dve.wait_ge(s_var, q + 1)
                o = (q % 8) * BANK
                cs = slice(c * CH, (c + 1) * CH)
                dve.tensor_scalar(Y[:, t, cs], ps[:, o:o + CH], 1e-5, None, ALU.add).then_inc(s_dve, 1)
                step.n += 1
                dve.wait_ge(s_dve, step.n)
                dve.reciprocal(yk[:, t, cs], Y[:, t, cs]).then_inc(s_inv, 1)
            for t in range(T):
                dve.wait_ge(s_root, t + 1)
                dve.wait_ge(s_yc, T * NC)
                dve.tensor_tensor(yk[:, t, :], yk[:, t, :], iv[:, t, :], ALU.mult).then_inc(s_n, 1)
            for t in range(T):
                dve.wait_ge(s_aff, t + 1)
                step(dve.tensor_tensor(Y[:, t, :], yk[:, t, :], Z[:, t, :], ALU.mult))


def l0_ffn(nc, a, ps, X, U):
    OT = 2 * E // 128
    with ExitStack() as ctx:
        sb, sem = space(nc, ctx, "l0f")
        c1 = sb("c1", [128, T, 2 * E])
        c3 = sb("c3", [128, OT, C])
        pr = sb("pr", [128, OT, 10])
        c2 = sb("c2", [128, OT, TAPS])
        c3b = sb("c3b", [C, 1])
        se1, se2 = sb("se1", [C, C // 2]), sb("se2", [C // 2, C])
        seb = sb("seb", [C, 2])
        sc = sb("sc", [128, 2, OT])
        bi = sb("bi", [128, 2, OT])
        t1, t2 = sb("t1", [128, 2, OT]), sb("t2", [128, 2, OT])
        pad = sb("pad", [128, 2, PW, PW])
        acc = sb("acc", [128, 2, L])
        t3 = sb("t3", [128, OT, L])
        to = sb("to", [C, B, L])
        m, s1, s2 = sb("m", [C, B, NC]), sb("s1", [C // 2, B]), sb("s2", [C, B])
        mean = sb("mean", [C, B])
        (s_in, s_dve, s_inv, s_root, s_bn, s_pad, s_c1, s_ev, s_tap, s_t3, s_c3, s_o, s_m, s_h, s_s1, s_g, s_e, s_t3p
         ) = map(sem, "in dve inv root bn pad c1 ev tap t3 c3 o m h s1 g e t3p".split())
        NIN = 8
        block = ctx.enter_context(nc.Block())

        @block.sync
        def _(sp):
            for dst, src in ((c1[:, :, :], a["c1"]), (c3[:, :, :], a["c3"]), (pr[:, :, :], a["ffn"]),
                             (c2[:, :, :], a["c2"]), (c3b[:, :], a["c3b"]), (se1[:, :], a["se1"]),
                             (se2[:, :], a["se2"]), (seb[:, :], a["seb"])):
                sp.dma_start(dst, src).then_inc(s_in, 16)
            sp.wait_ge(s_in, 16 * NIN)

        feeds = [[(0, 128, 0), (0, 64, 1)], [(64, 128, 1), (0, 128, 2)]]
        tiles = [(b, ot) for b in range(B) for ot in range(OT)]

        @block.tensor
        def _(pe):
            pe.wait_ge(s_in, 16 * NIN)

            def c1_tile(j):
                b, ot = tiles[j]
                for c in range(NC):
                    if j:
                        pe.wait_ge(s_ev, NC * (j - 1) + c + 1)
                    for f, (lo, hi, t) in enumerate(feeds[b]):
                        mm = pe.matmul(ps[:, c * BANK:c * BANK + CH], c1[lo:hi, t, ot * 128:(ot + 1) * 128],
                                       U[lo:hi, t, c * CH:(c + 1) * CH], start=(f == 0), stop=(f == 1))
                    mm.then_inc(s_c1, 1)

            def c3_image(b):
                pe.wait_ge(s_t3, OT * (b + 1))
                for c in range(NC):
                    q = b * NC + c
                    if q >= 2:
                        pe.wait_ge(s_o, q - 1)
                    o = (6 + q % 2) * BANK
                    for ot in range(OT):
                        mm = pe.matmul(ps[0:C, o:o + CH], c3[:, ot, :], t3[:, ot, c * CH:(c + 1) * CH],
                                       start=(ot == 0), stop=(ot == OT - 1))
                    mm.then_inc(s_c3, 1)

            for j in range(OT + 1):
                c1_tile(j)
            c3_image(0)
            for j in range(OT + 1, 2 * OT):
                c1_tile(j)
            c3_image(1)
            pe.wait_ge(s_m, 1)
            pe.matmul(ps[0:C // 2, 0:B], se1[:, :], mean[:, :], start=True, stop=True).then_inc(s_h, 1)
            pe.wait_ge(s_s1, 1)
            pe.matmul(ps[0:C, BANK:BANK + B], se2[:, :], s1[:, :], start=True, stop=True).then_inc(s_g, 1)

        @block.scalar
        def _(act):
            act.wait_ge(s_inv, 1)
            act.activation(sc[:, :, :], t1[:, :, :], ACT.Sqrt).then_inc(s_root, 1)
            act.wait_ge(s_bn, 1)
            act.wait_ge(s_pad, 2)

            def evacuate(j):
                b, ot = tiles[j]
                if j >= 2:
                    act.wait_ge(s_tap, TAPS * (j - 1))
                for c in range(NC):
                    act.wait_ge(s_c1, NC * j + c + 1)
                    act.activation(pad[:, j % 2, 1 + 8 * c:9 + 8 * c, 1:1 + W],
                                   ps[:, c * BANK:c * BANK + CH].rearrange("p (h w) -> p h w", w=W), ACT.Relu,
                                   scale=sc[:, 0, ot:ot + 1], bias=bi[:, 0, ot:ot + 1]).then_inc(s_ev, 1)

            def finish(j):
                b, ot = tiles[j]
                act.wait_ge(s_tap, TAPS * (j + 1))
                if b:
                    act.wait_ge(s_c3, NC)
                act.activation(t3[:, ot, :], acc[:, j % 2, :], ACT.Relu, scale=sc[:, 1, ot:ot + 1],
                               bias=bi[:, 1, ot:ot + 1]).then_inc(s_t3, 1)

            def out(b):
                for c in range(NC):
                    q = b * NC + c
                    act.wait_ge(s_c3, q + 1)
                    o = (6 + q % 2) * BANK
                    act.activation(to[:, b, c * CH:(c + 1) * CH], ps[0:C, o:o + CH], ACT.Identity,
                                   bias=c3b[:, :], accum_out=m[:, b, c:c + 1]).then_inc(s_o, 1)

            evacuate(0)
            for j in range(2 * OT):
                if j == OT:
                    out(0)
                if j + 1 < 2 * OT:
                    evacuate(j + 1)
                finish(j)
            out(1)
            act.wait_ge(s_h, 1)
            act.activation(s1[:, :], ps[0:C // 2, 0:B], ACT.Relu, bias=seb[0:C // 2, 0:1]).then_inc(s_s1, 1)
            act.wait_ge(s_g, 1)
            act.activation(s2[:, :], ps[0:C, BANK:BANK + B], ACT.Sigmoid, bias=seb[:, 1:2]).then_inc(s_e, 1)

        @block.vector
        def _(dve):
            step = Steps(dve, s_dve)
            for i in range(2):
                dve.memset(pad[:, i, :, :], 0.0).then_inc(s_pad, 1)
            dve.wait_ge(s_in, 16 * NIN)
            p = pr[:, :, :].rearrange("p o (h q) -> p h o q", h=2)
            step(dve.tensor_scalar(t2[:, :, :], p[:, :, :, 4], 1e-5, None, ALU.add))
            dve.reciprocal(t1[:, :, :], t2[:, :, :]).then_inc(s_inv, 1)
            dve.wait_ge(s_root, 1)
            step(dve.tensor_tensor(t1[:, :, :], sc[:, :, :], sc[:, :, :], ALU.mult))
            step(dve.tensor_tensor(t1[:, :, :], t1[:, :, :], t2[:, :, :], ALU.mult))
            step(dve.tensor_scalar(t1[:, :, :], t1[:, :, :], -0.5, 1.5, ALU.mult, ALU.add))
            step(dve.tensor_tensor(sc[:, :, :], sc[:, :, :], t1[:, :, :], ALU.mult))
            step(dve.tensor_tensor(sc[:, :, :], sc[:, :, :], p[:, :, :, 1], ALU.mult))
            step(dve.tensor_tensor(t1[:, :, :], p[:, :, :, 0], p[:, :, :, 3], ALU.subtract))
            step(dve.tensor_tensor(t1[:, :, :], t1[:, :, :], sc[:, :, :], ALU.mult))
            dve.tensor_tensor(bi[:, :, :], t1[:, :, :], p[:, :, :, 2], ALU.add).then_inc(s_bn, 1)
            for j, (b, ot) in enumerate(tiles):
                dve.wait_ge(s_ev, NC * (j + 1))
                if j >= 2:
                    dve.wait_ge(s_t3, j - 1)
                dst = by_image(acc[:, j % 2, :])
                for i in range(TAPS):
                    dy, dx = divmod(i, 3)
                    src = pad[:, j % 2, dy:dy + H, dx:dx + W]
                    if i == 0:
                        ins = dve.tensor_scalar(dst, src, c2[:, ot, 0:1], None, ALU.mult)
                    else:
                        dve.wait_ge(s_tap, TAPS * j + i)
                        ins = dve.scalar_tensor_tensor(dst, src, c2[:, ot, i:i + 1], dst, ALU.mult, ALU.add)
                    ins.then_inc(s_tap, 1)
            dve.wait_ge(s_o, B * NC)
            step(dve.tensor_reduce(mean[:, :], m[:, :, :], AX.X, ALU.add))
            dve.tensor_scalar(mean[:, :], mean[:, :], 1.0 / L, None, ALU.mult).then_inc(s_m, 1)
            dve.wait_ge(s_e, 1)
            for b in range(B):
                step(dve.scalar_tensor_tensor(to[:, b, :], to[:, b, :], s2[:, b:b + 1], to[:, b, :], ALU.mult, ALU.add))
                step(dve.tensor_tensor(X[:, b, :], to[:, b, :], X[:, b, :], ALU.add))




def l1_pairs(nc, a, ps, X, pad, d):
    with ExitStack() as ctx:
        sb, sem = space(nc, ctx, "l1")
        wa = sb("wa", [128, PT, C])
        bias = sb("bias", [C, 1])
        rows, p = sb("rows", [C, B, PW, W]), sb("p", [C, B, L])
        base = sb("base", [128, 3, L])
        other = sb("other", [128, 3, L])
        prod = sb("prod", [128, 3, L])
        credit = sb("credit", [1, 3])
        s_w, s_edge, s_sum, s_sump, s_p, s_pd, s_prod, s_used, s_out = map(
            sem, "w edge sum sump p pd prod used out".split())
        s_base = [sem(f"base{i}") for i in range(3)]
        s_slot = [sem(f"slot{i}") for i in range(3)]
        reads = []
        for i in range(PT):
            lo, hi, part = 128 * i, min(128 * i + 128, PAIR_ROWS), []
            while lo < hi:
                end = min(hi, (lo // C + 1) * C)
                part.append((lo - 128 * i, end - lo, lo % C + lo // C))
                lo = end
            reads.append(part)
        last = [max(i for i in range(PT) if i % 3 == s) + 1 - PT for s in range(3)]
        height = [sum(n for _, n, _ in part) for part in reads]
        nslot = [sum(len(reads[i]) for i in range(s, PT, 3)) for s in range(3)]
        upto = [sum(len(reads[j]) for j in range(i % 3, i + 1, 3)) for i in range(PT)]
        block = ctx.enter_context(nc.Block())

        def box(step, eng, b):
            step(eng.tensor_tensor(rows[:, b, :, :], pad[:, b, :, 0:W], pad[:, b, :, 1:1 + W], ALU.add))
            step(eng.tensor_tensor(rows[:, b, :, :], rows[:, b, :, :], pad[:, b, :, 2:2 + W], ALU.add))
            step(eng.tensor_tensor(by_image(p[:, b, :]), rows[:, b, 0:H, :], rows[:, b, 1:1 + H, :], ALU.add))
            step(eng.tensor_tensor(by_image(p[:, b, :]), by_image(p[:, b, :]), rows[:, b, 2:2 + H, :], ALU.add))

        @block.sync
        def _(sp):
            sp.dma_start(wa[:, :, :], d["pairs"]).then_inc(s_w, 16)
            sp.dma_start(bias[:, :], a["l1b"]).then_inc(s_w, 16)
            with sp.Fori(0, B) as b:
                sp.wait_ge(s_pd, (b + 1) * 32)
                sp.wait_ge(s_prod, b * PT + 1)
                for i in range(PT):
                    if i < 3:
                        d0 = 128 * i % C
                        sp.dma_start(base[:, i, :], d["pd"][d0:d0 + 128, b, :]).then_inc(s_base[i], 16)
                    else:
                        sp.wait_ge(s_prod, b * PT + i - 1)
                    for lo, n, src in reads[i]:
                        sp.dma_start(other[lo:lo + n, i % 3, :], d["pd"][src:src + n, b, :]
                                     ).then_inc(s_slot[i % 3], 16)

        @block.gpsimd
        def _(pool):
            pool.wait_ge(s_edge, 1)
            box(Steps(pool, s_sump), pool, 1)

        @block.scalar
        def _(act):
            for b, s_box in enumerate((s_sum, s_sump)):
                act.wait_ge(s_box, 4)
                act.mul(p[:, b, :], p[:, b, :], 1.0 / 9.0).then_inc(s_p, 1)
                act.wait_ge(s_p, b + 1)
                if b:
                    act.wait_ge(s_pd, 32)
                for i in range(2):
                    act.dma_start(d["pd"][i * C:(i + 1) * C, b, :], p[:, b, :]).then_inc(s_pd, 16)
            act.wait_ge(s_pd, 64)

        @block.vector
        def _(dve):
            for b in range(B):
                dve.memset(pad[:, b, 0:PW:PW - 1, :], 0.0)
                ins = dve.memset(pad[:, b, 1:1 + H, 0:PW:PW - 1], 0.0)
            ins.then_inc(s_edge, 1)
            dve.memset(credit[:, 0:1], 0.0).then_inc(s_out, 1)
            dve.memset(credit[:, 1:2], 0.0).then_inc(s_prod, 1)
            dve.memset(credit[:, 2:3], 0.0).then_inc(s_used, 3)
            dve.wait_ge(s_edge, 1)
            box(Steps(dve, s_sum), dve, 0)
            dve.wait_ge(s_w, 32)
            with dve.Fori(0, B) as b:
                for i in range(PT):
                    s, n = i % 3, height[i]
                    if i < 3:
                        dve.wait_ge(s_base[i], (b + 1) * 16)
                    dve.wait_ge(s_slot[s], b * (16 * nslot[s]) + 16 * upto[i])
                    dve.wait_ge(s_used, b * PT + 3 + (i - 2 if i >= 3 else last[i]))
                    dve.tensor_tensor(prod[0:n, s, :], base[0:n, s, :], other[0:n, s, :], ALU.mult
                                      ).then_inc(s_prod, 1)
                dve.wait_ge(s_used, b * PT + PT + 3)
                xb = X[:, b, :].rearrange("p (c n) -> p c n", n=CH)
                dve.scalar_tensor_tensor(xb, banks(ps, 0, NC)[0:C], bias[:, :], xb, ALU.add, ALU.add
                                         ).then_inc(s_out, 1)
            dve.wait_ge(s_out, B + 1)

        @block.tensor
        def _(pe):
            pe.wait_ge(s_w, 32)
            with pe.Fori(0, B) as b:
                pe.wait_ge(s_out, b + 1)
                for i in range(PT):
                    pe.wait_ge(s_prod, b * PT + i + 2)
                    for c in range(NC):
                        mm = pe.matmul(ps[0:C, c * BANK:c * BANK + CH], wa[0:height[i], i, :],
                                       prod[0:height[i], i % 3, c * CH:(c + 1) * CH],
                                       start=(i == 0), stop=(i == PT - 1))
                    mm.then_inc(s_used, 1)



KS = 9
RAD = KS // 2
DW = W + 2 * RAD
HH = H // 2
HL = HH * W
DT = 2 * B * C // 128
DVE_TAPS, POOL_TAPS = 37, 19


def l2_diffuse(nc, a, ps, X, pad, ident):
    al = 0.65
    c1 = 1.0 / math.gamma(1.0 + 1.0 / al)
    c2 = math.sqrt(2.0 * c1)
    val = 3.0 * (-2.0 + (1.0 + 2.0 * al) * c2) / ((1.0 + 2.0 * al) * (-2.0 * c1 + 3.0 * c2))
    gauss_k = val / (4.0 * math.pi * c1)
    poi_k = (1.0 - val) * math.gamma(1.5) / math.pi ** 1.5 * c2
    NT = KS * KS
    NPE = NT - DVE_TAPS - POOL_TAPS
    dve_taps = list(range(DVE_TAPS))
    pool_taps = list(range(DVE_TAPS, DVE_TAPS + POOL_TAPS))
    pe_taps = list(range(DVE_TAPS + POOL_TAPS, NT))
    NPR = 4
    assert 2 * POOL_TAPS >= NPE
    NB = HL // CH
    pieces = []
    for g in range(2 * B):
        lo = g * C
        while lo < (g + 1) * C:
            hi = min((g + 1) * C, (lo // 128 + 1) * 128)
            pieces.append((lo // 128, lo % 128, lo - g * C, hi - lo, g // 2, g % 2))
            lo = hi
    npieces = [sum(p[0] == t for p in pieces) for t in range(DT)]
    with ExitStack() as ctx:
        sb, sem = space(nc, ctx, "l2")
        yg = sb("yg", [128, 2, NT])
        dm = sb("dm", [128, DT, 4])
        z, z2 = sb("z", [128, DT, 2, NT]), sb("z2", [128, DT, 2, NT])
        r2, q, ex, root, t = (sb(n, [128, DT, NT]) for n in ("r2", "q", "ex", "root", "t"))
        kern = sb("kern", [128, DT, NT])
        diag = sb("diag", [128, DT, NPE, 128])
        rows = sb("rows", [128, DT, HH + 2 * RAD, DW])
        acc, accp = sb("acc", [128, DT, HL]), sb("accp", [128, DT, HL])
        prod = sb("prod", [128, NPR, HL])
        back = sb("back", [C, B, L])
        s_in, s_edge, s_dve, s_r2, s_q, s_ex, s_root, s_kern, s_diag, s_tap, s_ptap, s_pe, s_sum, s_all, s_back = map(
            sem, "in edge dve r2 q ex root kern diag tap ptap pe sum all back".split())
        s_prod = sem("prod")
        s_rows = [sem(f"rows{i}") for i in range(DT)]
        block = ctx.enter_context(nc.Block())

        def half(tile, tl):
            return tile[:, tl, :].rearrange("p (h w) -> p h w", w=W)

        @block.sync
        def _(sp):
            sp.dma_start(yg[:, :, :], a["grid"]).then_inc(s_in, 16)
            sp.dma_start(dm[:, :, :], a["dm"]).then_inc(s_in, 16)
            for tl, p0, ch0, n, b, hf in pieces:
                sp.wait_ge(s_edge, b + 1)
                sp.dma_start(rows[p0:p0 + n, tl, :, :],
                             pad[ch0:ch0 + n, b, hf * HH:hf * HH + HH + 2 * RAD, :]).then_inc(s_rows[tl], 16)
            for tl, p0, ch0, n, b, hf in pieces:
                sp.wait_ge(s_all, tl + 1)
                sp.dma_start(back[ch0:ch0 + n, b, hf * HL:(hf + 1) * HL], acc[p0:p0 + n, tl, :]).then_inc(s_back, 16)
            sp.wait_ge(s_in, 32)

        @block.gpsimd
        def _(pool):
            for b in range(B):
                for lo, hi in ((0, RAD), (RAD + H, DW)):
                    pool.memset(pad[:, b, lo:hi, :], 0.0)
                    ins = pool.memset(pad[:, b, RAD:RAD + H, lo:hi], 0.0)
                ins.then_inc(s_edge, 1)
            for tl in range(DT):
                for i in range(1, POOL_TAPS):
                    g = tl * (POOL_TAPS - 1) + i - 1
                    pool.wait_ge(s_prod, tl * POOL_TAPS + i + 1)
                    if i > 1:
                        pool.wait_ge(s_ptap, g)
                    pool.tensor_tensor(accp[:, tl, :], accp[:, tl, :], prod[:, g % NPR, :], ALU.add
                                       ).then_inc(s_ptap, 1)

        @block.scalar
        def _(act):
            act.wait_ge(s_r2, 1)
            act.activation(ex[:, :, :], r2[:, :, :], ACT.Exp, scale=-1.0 / (4.0 * c1)).then_inc(s_ex, 1)
            act.wait_ge(s_q, 1)
            act.activation(root[:, :, :], q[:, :, :], ACT.Sqrt).then_inc(s_root, 1)
            act.wait_ge(s_kern, 1)

            def diagonal(tl, i):
                act.activation(diag[:, tl, i, :], ident[:, :], ACT.Copy, scale=kern[:, tl, pe_taps[i]:pe_taps[i] + 1]
                               ).then_inc(s_diag, 1)

            for i in range(NPE):
                diagonal(0, i)
            for tl in range(DT):
                act.wait_ge(s_rows[tl], 16 * npieces[tl])
                for i, tap in enumerate(pool_taps):
                    dy, dx = divmod(tap, KS)
                    g = tl * (POOL_TAPS - 1) + i - 1
                    if i and g >= NPR:
                        act.wait_ge(s_ptap, g - NPR + 1)
                    dst = half(prod, g % NPR) if i else half(accp, tl)
                    act.activation(dst, rows[:, tl, dy:dy + HH, dx:dx + W], ACT.Copy,
                                   scale=kern[:, tl, tap:tap + 1]).then_inc(s_prod, 1)
                    for e in range(2 * i, min(2 * i + 2, NPE)):
                        if tl + 1 < DT:
                            diagonal(tl + 1, e)

        @block.vector
        def _(dve):
            dve.wait_ge(s_in, 32)
            step = Steps(dve, s_dve)
            for i in range(2):
                for tl in range(DT):
                    dve.tensor_scalar(z[:, tl, i, :], yg[:, 0, :], dm[:, tl, 2 * i:2 * i + 1], None, ALU.mult
                                      ).then_inc(s_dve, 1)
                    step.n += 1
            dve.wait_ge(s_dve, step.n)
            for i in range(2):
                for tl in range(DT):
                    dve.scalar_tensor_tensor(z[:, tl, i, :], yg[:, 1, :], dm[:, tl, 2 * i + 1:2 * i + 2],
                                             z[:, tl, i, :], ALU.mult, ALU.add).then_inc(s_dve, 1)
                    step.n += 1
            dve.wait_ge(s_dve, step.n)
            step(dve.tensor_tensor(z2[:, :, :, :], z[:, :, :, :], z[:, :, :, :], ALU.mult))
            dve.tensor_tensor(r2[:, :, :], z2[:, :, 0, :], z2[:, :, 1, :], ALU.add).then_inc(s_r2, 1)
            dve.wait_ge(s_r2, 1)
            dve.tensor_scalar(q[:, :, :], r2[:, :, :], c2 * c2, None, ALU.add).then_inc(s_q, 1)
            dve.wait_ge(s_root, 1)
            step(dve.reciprocal(t[:, :, :], root[:, :, :]))
            step(dve.tensor_tensor(t[:, :, :], t[:, :, :], q[:, :, :], ALU.mult))
            step(dve.tensor_tensor(root[:, :, :], root[:, :, :], t[:, :, :], ALU.add))
            step(dve.tensor_tensor(t[:, :, :], root[:, :, :], q[:, :, :], ALU.mult))
            step(dve.reciprocal(root[:, :, :], t[:, :, :]))
            step(dve.tensor_scalar(root[:, :, :], root[:, :, :], 2.0 * poi_k, None, ALU.mult))
            dve.wait_ge(s_ex, 1)
            dve.scalar_tensor_tensor(kern[:, :, :], ex[:, :, :], gauss_k, root[:, :, :], ALU.mult, ALU.add
                                     ).then_inc(s_kern, 1)
            dve.wait_ge(s_kern, 1)

            def merge(tl):
                dve.wait_ge(s_pe, tl + 1)
                dve.tensor_tensor(acc[:, tl, :].rearrange("p (c n) -> p c n", n=CH), banks(ps, NB * (tl % 2), NB),
                                  acc[:, tl, :].rearrange("p (c n) -> p c n", n=CH), ALU.add).then_inc(s_sum, 1)
                dve.wait_ge(s_sum, tl + 1)
                dve.wait_ge(s_ptap, (POOL_TAPS - 1) * (tl + 1))
                dve.tensor_tensor(acc[:, tl, :], accp[:, tl, :], acc[:, tl, :], ALU.add).then_inc(s_all, 1)

            count = 0
            for tl in range(DT):
                dve.wait_ge(s_rows[tl], 16 * npieces[tl])
                for i, tap in enumerate(dve_taps):
                    dy, dx = divmod(tap, KS)
                    src = rows[:, tl, dy:dy + HH, dx:dx + W]
                    if i == 0:
                        ins = dve.tensor_scalar(half(acc, tl), src, kern[:, tl, tap:tap + 1], None, ALU.mult)
                    else:
                        dve.wait_ge(s_tap, count)
                        ins = dve.scalar_tensor_tensor(half(acc, tl), src, kern[:, tl, tap:tap + 1], half(acc, tl),
                                                       ALU.mult, ALU.add)
                    ins.then_inc(s_tap, 1)
                    count += 1
                    if tl and i == 5:
                        merge(tl - 1)
            dve.wait_ge(s_tap, count)
            merge(DT - 1)
            dve.wait_ge(s_back, 16 * len(pieces))
            for b in range(B):
                step(dve.tensor_tensor(X[:, b, :], back[:, b, :], X[:, b, :], ALU.add))

        @block.tensor
        def _(pe):
            for tl in range(DT):
                pe.wait_ge(s_rows[tl], 16 * npieces[tl])
                if tl >= 2:
                    pe.wait_ge(s_sum, tl - 1)
                for i, tap in enumerate(pe_taps):
                    pe.wait_ge(s_diag, tl * NPE + i + 1)
                    dy, dx = divmod(tap, KS)
                    for c in range(NB):
                        o = (NB * (tl % 2) + c) * BANK
                        mm = pe.matmul(ps[:, o:o + CH], diag[:, tl, i, :],
                                       rows[:, tl, dy + 8 * c:dy + 8 * c + 8, dx:dx + W],
                                       start=(i == 0), stop=(i == NPE - 1))
                mm.then_inc(s_pe, 1)



HC = 4 * HID
O_SP, O_AL, O_FR, O_FF = 0, 2 * C3, 2 * C3 + 1, 2 * C3 + 1 + 4 * C3
GO = O_FF + 4 * C3
BC = B * C3
FJ = 10
FCH = [(j, min(j + FJ, H)) for j in range(0, H, FJ)]


def l3_gates(nc, a, ps, st, wg, bw, w0g, cs, d, XG, G0, tr):
    with ExitStack() as ctx:
        sb, sem = space(nc, ctx, "l3g")
        gap = sb("gap", [C, B])
        w1, b1 = sb("w1", [C, HC]), sb("b1", [HC, 1])
        w2, b2 = sb("w2", [HC, GO]), sb("b2", [1, GO])
        one = sb("one", [1, C3])
        hid = sb("hid", [HC, B])
        row = sb("row", [1, B, GO])
        wt = sb("wt", [BC, 2, 2, 2 * C3])
        w0 = sb("w0", [3 * C3, B, 3, C3])
        gate = sb("gate", [BC, 2, 2, 2 * C3])
        gate0 = sb("gate0", [3 * C3, B, C3])
        lv = sb("lv", [BC, H])
        al = sb("al", [BC, 1])
        turns, fr = sb("turns", [BC, 2, H]), sb("fr", [BC, 2, H])
        whole = sb("whole", [BC, 2, H], I32)
        (s_in, s_dve, s_gap, s_hid, s_hs, s_row, s_rs, s_gate, s_gs, s_al, s_als, s_w, s_fr, s_cs, s_pool, s_x, s_ex
         ) = map(sem, "in dve gap hid hs row rs gate gs al als w fr cs pool x ex".split())
        s_tr, s_zero, s_spread = map(sem, "tr zero spread".split())
        NIN = 8
        block = ctx.enter_context(nc.Block())

        @block.sync
        def _(sp):
            sp.dma_start(d["g"].rearrange("c b l -> c (b l)"), XG[C3:C, :, :].rearrange("c b l -> c (b l)")
                         ).then_inc(s_x, 16)
            for dst, src in ((w1[:, :], "w1"), (b1[:, :], "b1"), (w2[:, :], "w2"), (b2[:, :], "b2"),
                             (wt[:, :, :, :], "wt"), (w0[:, :, :, :], "w0"), (lv[:, :], "lv"),
                             (bw[:, :, :, :], "bw")):
                sp.dma_start(dst, a[src]).then_inc(s_in, 16)
            for name in ("fh", "fw", "ef"):
                sp.dma_start(tr[name], a[name]).then_inc(s_tr, 16)
            sp.wait_ge(s_x, 16)
            for f in (1, 0):
                for b in range(B):
                    sp.dma_start(tr["xh"][:, f, C3 * b:C3 * b + C3, :],
                                 d["g"][C3 * f:C3 * f + C3, b, :].rearrange("c (h w) -> h c w", w=W)
                                 ).then_inc(s_tr, 16)
            sp.wait_ge(s_zero, 1)
            for i in range(3):
                lo, hi = max(0, i - 1), W + min(0, i - 1)
                for b in range(B):
                    sp.dma_start(G0[C3 * i:C3 * i + C3, b, 1:1 + H, lo + 1 - i:hi + 1 - i],
                                 by_image(XG[0:C3, b, :])[:, :, lo:hi]).then_inc(s_spread, 16)
            sp.wait_ge(s_in, 16 * NIN)
            sp.wait_ge(s_tr, 16 * (3 + 2 * B))
            sp.wait_ge(s_spread, 96)

        @block.gpsimd
        def _(pool):
            pool.memset(G0[:, :, :, :], 0.0).then_inc(s_zero, 1)

        @block.tensor
        def _(pe):
            pe.wait_ge(s_in, 16 * NIN)
            pe.wait_ge(s_gap, 1)
            pe.matmul(ps[0:HC, 0:B], w1[:, :], gap[:, :], start=True, stop=True).then_inc(s_hid, 1)
            pe.wait_ge(s_hs, 1)
            for b in range(B):
                pe.matmul(ps[0:1, (1 + b) * BANK:(1 + b) * BANK + GO], hid[:, b:b + 1], w2[:, :],
                          start=True, stop=False)
                mm = pe.matmul(ps[0:1, (1 + b) * BANK:(1 + b) * BANK + GO], one[:, 0:1], b2[:, :],
                               start=False, stop=True)
            mm.then_inc(s_row, 1)
            pe.wait_ge(s_rs, 1)
            for b in range(B):
                for f, o in enumerate((O_FR, O_FF)):
                    for p in range(2):
                        mm = pe.matmul(ps[C3 * b:C3 * b + C3, (3 + 2 * f + p) * BANK:(3 + 2 * f + p) * BANK + 2 * C3],
                                       row[:, b, o + 2 * C3 + p * C3:o + 2 * C3 + (p + 1) * C3],
                                       row[:, b, o:o + 2 * C3], start=True, stop=True)
            for b in range(B):
                for i in range(3):
                    pe.matmul(ps[C3 * i:C3 * i + C3, (7 * b) * BANK:(7 * b) * BANK + C3],
                              row[:, b, O_SP + C3:O_SP + 2 * C3], row[:, b, O_SP:O_SP + C3], start=True, stop=True)
            for b in range(B):
                mm = pe.matmul(ps[C3 * b:C3 * b + C3, BANK:BANK + 1], one[:, :], row[:, b, O_AL:O_AL + 1],
                               start=True, stop=True)
            mm.then_inc(s_gate, 1)

        @block.scalar
        def _(act):
            act.wait_ge(s_in, 16 * NIN)
            act.wait_ge(s_hid, 1)
            act.activation(hid[:, :], ps[0:HC, 0:B], ACT.Relu, bias=b1[:, :]).then_inc(s_hs, 1)
            act.wait_ge(s_row, 1)
            act.copy(row[:, :, :], ps[0:1, BANK:3 * BANK].rearrange("p (b n) -> p b n", b=B)[:, :, 0:GO]
                     ).then_inc(s_rs, 1)
            act.wait_ge(s_gate, 1)
            act.activation(al[:, :], ps[0:BC, BANK:BANK + 1], ACT.Sigmoid).then_inc(s_als, 1)
            act.activation(gate[:, :, :, :].rearrange("p f i o -> p (f i) o"),
                           ps[0:BC, 3 * BANK:7 * BANK].rearrange("p (q n) -> p q n", n=BANK)[:, :, 0:2 * C3],
                           ACT.Sigmoid).then_inc(s_gs, 1)
            for b in range(B):
                act.activation(gate0[:, b, :], ps[0:3 * C3, 7 * b * BANK:7 * b * BANK + C3], ACT.Sigmoid
                               ).then_inc(s_gs, 1)
            act.wait_ge(s_fr, 1)
            act.activation(cs[:, :, :], fr[:, :, :], ACT.Sin, scale=2.0 * math.pi * (1.0 - 1e-7)).then_inc(s_cs, 1)

        @block.vector
        def _(dve):
            step = Steps(dve, s_dve)
            step(dve.memset(one[:, :], 1.0))
            step(dve.tensor_tensor(gap[:, :], st["mv"][:, :, 0], st["rstd"][:, :], ALU.mult))
            dve.tensor_tensor(gap[:, :], gap[:, :], st["shift"][:, :], ALU.add).then_inc(s_gap, 1)
            step(dve.memset(wg[:, :, :, :, :], 0.0))
            dve.wait_ge(s_als, 1)
            step(dve.tensor_scalar(al[:, :], al[:, :], 0.8, 0.1, ALU.mult, ALU.add))
            step(dve.tensor_scalar(turns[:, 0, :], lv[:, :], al[:, 0:1], 0.25, ALU.mult, ALU.mult))
            step(dve.tensor_scalar(turns[:, 1, :], turns[:, 0, :], 0.25, None, ALU.add))
            step(dve.tensor_copy(whole[:, :, :], turns[:, :, :]))
            step(dve.tensor_copy(fr[:, :, :], whole[:, :, :]))
            step(dve.tensor_tensor(turns[:, :, :], turns[:, :, :], fr[:, :, :], ALU.subtract))
            step(dve.tensor_scalar(fr[:, :, :], turns[:, :, :], 0.5, None, ALU.is_gt))
            dve.tensor_tensor(fr[:, :, :], turns[:, :, :], fr[:, :, :], ALU.subtract).then_inc(s_fr, 1)
            dve.wait_ge(s_gs, 3)
            dve.wait_ge(s_in, 16 * NIN)
            for f in range(2):
                for b in range(B):
                    rows = slice(C3 * b, C3 * b + C3)
                    dst = wg[rows, f, :, :, rows]
                    step(dve.tensor_tensor(dst, gate[rows, f, :, :].rearrange("p i (q o) -> p i q o", q=2),
                                           wt[rows, f, :, :].rearrange("p i (q o) -> p i q o", q=2), ALU.mult))
            for b in range(B):
                for i in range(3):
                    ins = dve.tensor_tensor(w0g[:, b, i, :], gate0[:, b, :], w0[:, b, i, :], ALU.mult)
            step(ins)
            dve.wait_ge(s_cs, 1)


def l3_forward(nc, a, ps, wg, bw, cs, d, tr, xbuf):
    with ExitStack() as ctx:
        sb, sem = space(nc, ctx, "l3f")
        xh, ef, fh, fw = tr["xh"], tr["ef"], tr["fh"], tr["fw"]
        e11 = sb("e11", [1, H * H])
        ones = sb("ones", [1, BANK])
        A1 = sb("A1", [W, BC, H])
        Xh, Zr, Zi = (sb(n, [BC, H, H]) for n in ("Xh", "Zr", "Zi"))
        Fz = sb("Fz", [BC, H, 2, UH])
        Mz = sb("Mz", [BC, H, 2, UH])
        M = xbuf[:, 0:2 * H * H].rearrange("p (q j k) -> p q j k", q=2, j=H)
        A2 = sb("A2", [W, BC, 2, H])
        ph = sb("ph", [BC, 2, H, H])
        s_in, s_one, s_mm, s_ev, s_z, s_m, s_dve, s_v, s_out = map(sem, "in one mm ev z m dve v out".split())
        s_mst = sem("mst")
        block = ctx.enter_context(nc.Block())

        @block.sync
        def _(sp):
            sp.dma_start(e11[:, :], a["e11"]).then_inc(s_in, 16)
            for i in range(2):
                sp.wait_ge(s_v, i + 1)
                sp.dma_start(d["V"][:, i, :, :], M[:, i, :, :]).then_inc(s_out, 16)
            sp.wait_ge(s_m, 1)
            sp.dma_start(d["M"].rearrange("p u i k -> p (u i k)"), Mz[:, :, :, :].rearrange("p u i k -> p (u i k)")
                         ).then_inc(s_mst, 16)
            sp.wait_ge(s_mst, 16)
            sp.wait_ge(s_in, 16)
            sp.wait_ge(s_out, 32)

        def rows_jobs():
            n = BANK // H
            for c in range(0, BC, n):
                cc = range(c, min(c + n, BC))
                yield ([(xh[:, 0, i, :], ef[:, :], (i - c) * H, H, True, True) for i in cc], W,
                       A1[:, c:c + len(cc), :].rearrange("p c h -> p (c h)"), None)
            n = BANK // (2 * H)
            for c in range(0, BC, n):
                cc = range(c, min(c + n, BC))
                yield ([(xh[:, 1, i, :], fh[:, :], (i - c) * 2 * H, 2 * H, True, True) for i in cc], W,
                       A2[:, c:c + len(cc), :, :].rearrange("p c i h -> p (c i h)"), None)

        def cols_jobs():
            for lo, hi in FCH:
                yield ([(A1[:, :, j], ef[:, :], (j - lo) * H, H, True, True) for j in range(lo, hi)], BC,
                       Xh[:, lo:hi, :].rearrange("p j k -> p (j k)"), float(H))
            for lo, hi in FCH:
                mms = []
                for u in range(lo, hi):
                    mms.append((A2[:, :, 0, u], fw[:, 0, :], (u - lo) * 2 * UH, 2 * UH, True, False))
                    mms.append((A2[:, :, 1, u], fw[:, 1, :], (u - lo) * 2 * UH, 2 * UH, False, True))
                yield mms, BC, Fz[:, lo:hi, :, :].rearrange("p u i k -> p (u i k)"), None

        def mix_jobs():
            for lo, hi in FCH:
                for q in range(2):
                    o = (hi - lo) * UH
                    yield ([(wg[:, 1, 0, q, :], Fz[:, lo:hi, 0, :], 0, o, True, False),
                            (wg[:, 1, 1, q, :], Fz[:, lo:hi, 1, :], 0, o, False, False),
                            (bw[:, 1, q, :], ones[:, 0:o], 0, o, False, True)], BC, Mz[:, lo:hi, q, :], None)

        def frac_jobs():
            for lo, hi in FCH:
                for q in range(2):
                    o = (hi - lo) * H
                    yield ([(wg[:, 0, 0, q, :], Zr[:, lo:hi, :].rearrange("p j k -> p (j k)"), 0, o, True, False),
                            (wg[:, 0, 1, q, :], Zi[:, lo:hi, :].rearrange("p j k -> p (j k)"), 0, o, False, False),
                            (bw[:, 0, q, :], e11[:, lo * H:hi * H], 0, o, False, True)], BC,
                           M[:, q, lo:hi, :].rearrange("p j k -> p (j k)"), None)

        phases = [list(g()) for g in (rows_jobs, cols_jobs, frac_jobs, mix_jobs)]

        @block.tensor
        def _(pe):
            pe.wait_ge(s_one, 1)
            q = 0
            for i, jobs in enumerate(phases):
                if i:
                    pe.wait_ge(s_ev, q)
                if i == 2:
                    pe.wait_ge(s_z, 2)
                    pe.wait_ge(s_in, 16)
                for mms, rows, _, _ in jobs:
                    if q >= 8:
                        pe.wait_ge(s_ev, q - 7)
                    for lhsT, rhs, at, n, start, stop in mms:
                        mm = pe.matmul(ps[0:rows, (q % 8) * BANK + at:(q % 8) * BANK + at + n], lhsT, rhs,
                                       start=start, stop=stop)
                    mm.then_inc(s_mm, 1)
                    q += 1

        @block.scalar
        def _(act):
            q = 0
            for i, jobs in enumerate(phases):
                for mms, rows, dst, scale in jobs:
                    act.wait_ge(s_mm, q + 1)
                    n = mms[-1][2] + mms[-1][3]
                    src = ps[0:rows, (q % 8) * BANK:(q % 8) * BANK + n]
                    if len(dst.shape) == 3:
                        src = src.rearrange("p (u k) -> p u k", k=UH)
                    if scale:
                        act.mul(dst, src, scale).then_inc(s_ev, 1)
                    else:
                        act.copy(dst, src).then_inc(s_ev, 1)
                    q += 1
                if i == 3:
                    act.wait_ge(s_ev, q)
                    act.copy(ones[:, 0:1], ones[:, 0:1]).then_inc(s_m, 1)

        @block.vector
        def _(dve):
            step = Steps(dve, s_dve)
            dve.memset(ones[:, :], 1.0).then_inc(s_one, 1)
            sj = [cs[:, i, :].unsqueeze(2).to_broadcast([BC, H, H]) for i in range(2)]
            sk = [cs[:, i, :].unsqueeze(1).to_broadcast([BC, H, H]) for i in range(2)]
            step(dve.tensor_tensor(Zr[:, :, :], sj[1], sk[1], ALU.mult))
            step(dve.tensor_tensor(Zi[:, :, :], sj[0], sk[0], ALU.mult))
            step(dve.tensor_tensor(ph[:, 0, :, :], Zr[:, :, :], Zi[:, :, :], ALU.subtract))
            step(dve.tensor_tensor(Zr[:, :, :], sj[0], sk[1], ALU.mult))
            step(dve.tensor_tensor(Zi[:, :, :], sj[1], sk[0], ALU.mult))
            step(dve.tensor_tensor(ph[:, 1, :, :], Zr[:, :, :], Zi[:, :, :], ALU.add))
            dve.wait_ge(s_ev, len(phases[0]) + len(FCH))
            dve.tensor_tensor(Zr[:, :, :], Xh[:, :, :], ph[:, 0, :, :], ALU.mult).then_inc(s_z, 1)
            dve.scalar_tensor_tensor(Zi[:, :, :], Xh[:, :, :], -1.0, ph[:, 1, :, :], ALU.mult, ALU.mult
                                     ).then_inc(s_z, 1)
            dve.wait_ge(s_ev, sum(map(len, phases[0:3])))
            step(dve.tensor_tensor(Zr[:, :, :], M[:, 1, :, :], ph[:, 1, :, :], ALU.mult))
            step(dve.tensor_tensor(Zi[:, :, :], M[:, 0, :, :], ph[:, 1, :, :], ALU.mult))
            for q, (t, op) in enumerate(((Zr, ALU.subtract), (Zi, ALU.add))):
                step(dve.tensor_tensor(M[:, q, :, :], M[:, q, :, :], ph[:, 0, :, :], ALU.mult))
                dve.tensor_tensor(M[:, q, :, :], M[:, q, :, :], t[:, :, :], op).then_inc(s_v, 1)


def l3_inverse(nc, a, ps, X, G0, w0g, d):
    with ExitStack() as ctx:
        sb, sem = space(nc, ctx, "l3i")
        Vj = sb("Vj", [H, BC, 2, H])
        Mu = sb("Mu", [H, BC, 2 * UH])
        ei = sb("ei", [H, H])
        ih, iw = sb("ih", [H, 2 * H]), sb("iw", [2 * UH, 2, W])
        A3 = sb("A3", [W, BC, 2, H])
        A4 = sb("A4", [2 * UH, BC, 2, H])
        O = A4[0:H]
        P2, F = sb("P2", [H, BC, W]), sb("F", [H, BC, W])
        cat = sb("cat", [C, B, PW, PW])
        w2 = sb("w2", [C, TAPS, C])
        b0, b2 = sb("b0", [C3, 1]), sb("b2", [C, 1])
        s_b0, s_in, s_V, s_edge, s_mm, s_ev, s_sum, s_root, s_fst, s_cf, s_pst, s_c2, s_x = map(
            sem, "b0 in V edge mm ev sum root fst cf pst c2 x".split())
        s_cp = [sem(f"cp{b}") for b in range(B)]
        NIN = 6
        block = ctx.enter_context(nc.Block())

        def conv0_jobs():
            for b in range(B):
                for c in range(NC):
                    yield ([(w0g[:, b, i, :], G0[:, b, i + 8 * c:i + 8 * c + 8, 0:W], 0, CH, i == 0, i == 2)
                            for i in range(3)], C3, cat[0:C3, b, 1 + 8 * c:9 + 8 * c, 1:1 + W], ACT.Identity)

        def jobs(kind):
            n = BANK // (2 * H)
            m = BANK // H
            if kind == 1:
                for c in range(0, BC, n):
                    cc = range(c, min(c + n, BC))
                    yield ([(Mu[:, i, :], ih[:, :], (i - c) * 2 * H, 2 * H, True, True) for i in cc], 2 * UH,
                           A4[:, c:c + len(cc), :, :].rearrange("p c i h -> p (c i h)"), ACT.Copy)
            if kind == 2:
                for c in range(0, BC, m):
                    cc = range(c, min(c + m, BC))
                    mms = []
                    for i in cc:
                        for q in range(2):
                            mms.append((A4[:, i, q, :], iw[:, q, :], (i - c) * W, W, q == 0, q == 1))
                    yield mms, H, F[:, c:c + len(cc), :].rearrange("p c w -> p (c w)"), ACT.Copy
            if kind == 3:
                for c in range(0, 2 * BC, m):
                    cc = range(c, min(c + m, 2 * BC))
                    yield ([(Vj[:, i // 2, i % 2, :], ei[:, :], (i - c) * H, H, True, True) for i in cc], H,
                           A3[:, :, :, :].rearrange("p c i h -> p (c i) h")[:, c:c + len(cc), :]
                           .rearrange("p c h -> p (c h)"), ACT.Copy)
            if kind == 4:
                for c in range(0, 2 * BC, m):
                    cc = range(c, min(c + m, 2 * BC))
                    yield ([(A3[:, i // 2, i % 2, :], ei[:, :], (i - c) * H, H, True, True) for i in cc], H,
                           O[:, :, :, :].rearrange("p c i h -> p (c i) h")[:, c:c + len(cc), :]
                           .rearrange("p c h -> p (c h)"), ACT.Square)

        phases = [list(conv0_jobs())] + [list(jobs(i)) for i in range(1, 5)]
        first = [sum(map(len, phases[:i])) for i in range(len(phases) + 1)]
        n_act = first[-1]
        squares = [first[4] + -(-2 * C3 * (b + 1) // (BANK // H)) for b in range(B)]

        @block.sync
        def _(sp):
            sp.dma_start(b0[:, :], a["cb0"]).then_inc(s_b0, 16)
            sp.dma_start(Mu[:, :, :], d["M"].rearrange("p u i k -> u p (i k)")).then_inc(s_in, 16)
            for dst, src in ((ih[:, :], "ih"), (iw[:, :, :], "iw"), (ei[:, :], "ei"), (w2[:, :, :], "cw2"),
                             (b2[:, :], "cb2")):
                sp.dma_start(dst, a[src]).then_inc(s_in, 16)
            for i in range(2):
                sp.dma_start(Vj[:, :, i, :], d["V"][:, i, :, :].rearrange("p j k -> j p k")).then_inc(s_V, 16)
            sp.wait_ge(s_ev, first[3])
            sp.dma_start(d["o"][1], F[:, :, :]).then_inc(s_fst, 16)
            sp.wait_ge(s_edge, 1)
            sp.wait_ge(s_fst, 16)
            for b in range(B):
                sp.dma_start(interior(cat[2 * C3:C, b, :, :]),
                             d["o"][1, :, C3 * b:C3 * b + C3, :].rearrange("h c w -> c h w")).then_inc(s_cf, 16)
            for b in range(B):
                rows = slice(C3 * b, C3 * b + C3)
                sp.wait_ge(s_root, b + 1)
                sp.dma_start(d["o"][0][:, rows, :], P2[:, rows, :]).then_inc(s_pst, 16)
                sp.wait_ge(s_pst, 16 * (b + 1))
                sp.dma_start(interior(cat[C3:2 * C3, b, :, :]),
                             d["o"][0, :, rows, :].rearrange("h c w -> c h w")).then_inc(s_cp[b], 16)
            sp.wait_ge(s_b0, 16)
            sp.wait_ge(s_in, 16 * NIN)
            sp.wait_ge(s_V, 32)
            sp.wait_ge(s_cf, 16 * B)

        @block.gpsimd
        def _(pool):
            pool.memset(cat[:, :, :, :], 0.0).then_inc(s_edge, 1)

        @block.tensor
        def _(pe):
            def bank_free(q):
                if q >= 8 + n_act:
                    pe.wait_ge(s_x, q - 7 - n_act)
                elif q >= 8:
                    pe.wait_ge(s_ev, q - 7)

            q = 0
            for i, job in enumerate(phases):
                if i == 1:
                    pe.wait_ge(s_in, 16 * NIN)
                if i == 3:
                    pe.wait_ge(s_V, 32)
                if i in (2, 4):
                    pe.wait_ge(s_ev, q)
                for mms, rows, _, _ in job:
                    bank_free(q)
                    for lhsT, rhs, at, n, start, stop in mms:
                        mm = pe.matmul(ps[0:rows, (q % 8) * BANK + at:(q % 8) * BANK + at + n], lhsT, rhs,
                                       start=start, stop=stop)
                    mm.then_inc(s_mm, 1)
                    q += 1
            pe.wait_ge(s_cf, 16 * B)
            for b in range(B):
                pe.wait_ge(s_cp[b], 16)
                for c in range(NC):
                    bank_free(q)
                    for i in range(TAPS):
                        dy, dx = divmod(i, 3)
                        mm = pe.matmul(ps[0:C, (q % 8) * BANK:(q % 8) * BANK + CH], w2[:, i, :],
                                       cat[:, b, dy + 8 * c:dy + 8 * c + 8, dx:dx + W], start=(i == 0),
                                       stop=(i == TAPS - 1))
                    mm.then_inc(s_c2, 1)
                    q += 1

        @block.scalar
        def _(act):
            def root(b):
                rows = slice(C3 * b, C3 * b + C3)
                act.wait_ge(s_sum, b + 1)
                act.activation(P2[:, rows, :], P2[:, rows, :], ACT.Sqrt, scale=1.0 / (H * W)).then_inc(s_root, 1)

            act.wait_ge(s_edge, 1)
            act.wait_ge(s_b0, 16)
            q = 0
            for job in phases:
                for mms, rows, dst, fn in job:
                    act.wait_ge(s_mm, q + 1)
                    n = mms[-1][2] + mms[-1][3]
                    src = ps[0:rows, (q % 8) * BANK:(q % 8) * BANK + n]
                    if fn == ACT.Identity:
                        act.activation(dst, src.rearrange("p (h w) -> p h w", w=W), fn, bias=b0[:, :]
                                       ).then_inc(s_ev, 1)
                    else:
                        act.activation(dst, src, fn).then_inc(s_ev, 1)
                    q += 1
                    if q == squares[0] + 1:
                        root(0)
            root(1)

        @block.vector
        def _(dve):
            for b in range(B):
                rows = slice(C3 * b, C3 * b + C3)
                dve.wait_ge(s_ev, squares[b])
                dve.tensor_tensor(P2[:, rows, :], O[:, rows, 0, :], O[:, rows, 1, :], ALU.add).then_inc(s_sum, 1)
            dve.wait_ge(s_in, 16 * NIN)
            for q in range(B * NC):
                b, c = divmod(q, NC)
                dve.wait_ge(s_c2, q + 1)
                xs = X[:, b, c * CH:(c + 1) * CH]
                o = ((n_act + q) % 8) * BANK
                dve.scalar_tensor_tensor(xs, ps[0:C, o:o + CH], b2[:, :], xs, ALU.add, ALU.add).then_inc(s_x, 1)


def l3(nc, a, ps, X, gavg, ident, st):
    d = {"g": nc.dram_tensor("g3", (2 * C3, B, L), F32).ap(), "V": nc.dram_tensor("V", (BC, 2, H, H), F32).ap(),
         "M": nc.dram_tensor("M", (BC, H, 2, UH), F32).ap(), "o": nc.dram_tensor("o3", (2, H, BC, W), F32).ap()}
    with ExitStack() as ctx:
        sb, _ = space(nc, ctx, "l3")
        w0g = sb("w0g", [3 * C3, B, 3, C3])
        G0 = sb("G0", [3 * C3, B, PW, W])
        with ExitStack() as spectral:
            sb1, _ = space(nc, spectral, "l3w")
            wg = sb1("wg", [BC, 2, 2, 2, BC])
            bw = sb1("bw", [1, 2, 2, BC])
            cs = sb1("cs", [BC, 2, H])
            xbuf = sb1("xbuf", [BC, 2 * BC * W])
            ef = sb1("ef", [H, H])
            fh, fw = sb1("fh", [H, 2 * H]), sb1("fw", [H, 2, 2 * UH])
            tr = {"xh": xbuf[0:H, :].rearrange("p (f c w) -> p f c w", f=2, w=W), "ef": ef[:, :], "fh": fh[:, :],
                  "fw": fw[:, :, :]}
            with ExitStack() as early:
                XG = space(nc, early, "l3x")[0]("XG", [C, B, L])
                group_norm(nc, "gn3", X, ps, gavg, st, [by_image(XG[:, b, :]) for b in range(B)])
                l3_gates(nc, a, ps, st, wg, bw, w0g, cs, d, XG, G0, tr)
            l3_forward(nc, a, ps, wg, bw, cs, d, tr, xbuf)
        l3_inverse(nc, a, ps, X, G0, w0g, d)




def program(nc, a, x, out, layers=(0, 1, 2, 3)):
    with ExitStack() as ctx:
        sb, _ = space(nc, ctx, "net")
        ps = ctx.enter_context(nc.psum_tensor("ps", [128, 8 * BANK], F32))
        X = sb("X", [C, B, L])
        gavg = sb("gavg", [C, C])
        ident = sb("ident", [128, 128])
        st = {"mv": sb("mv", [C, B, 2]), "rstd": sb("rstd", [C, B]), "shift": sb("shift", [C, B])}
        load(nc, "x", [(X[:, :, :], x.rearrange("b c h w -> c b (h w)")), (gavg[:, :], a["gavg"]),
                       (ident[:, :], a["ident"])])
        pairs = nc.dram_tensor("pairs", (128, PT, C), F32).ap()
        if 0 in layers:
            d = {"dlt": nc.dram_tensor("dlt", (K * T, 128, L), F32).ap(), "v": nc.dram_tensor("v", (K * T, 128, L), F32).ap(),
                 "y": nc.dram_tensor("y", (K * T, 128, L), F32).ap(), "na": nc.dram_tensor("na", (K * T, 128, 2 * N), F32).ap(),
                 "pairs": pairs, "bc": nc.dram_tensor("bc", (K, 2, 3 * B * N, L), BF16).ap()}
            with ExitStack() as l0:
                sb0, _ = space(nc, l0, "l0")
                Z = sb0("Z", [128, T, L])
                with ExitStack() as early:
                    sb1, _ = space(nc, early, "l0e")
                    XI = sb1("XI", [128, T, L])
                    with ExitStack() as first:
                        XG = space(nc, first, "l0x")[0]("XG", [C, B, L])
                        group_norm(nc, "gn0", X, ps, gavg, st, [by_image(XG[:, b, :]) for b in range(B)])
                        l0_project(nc, a, X, XG, ps, XI, Z)
                    P = sb1("P", [K * B * R, L])
                    l0_rows(nc, a, ps, XI, P, d)
                    l0_steps(nc, a, ps, XI, P, d)
                l0_scan(nc, a, ps, ident, d)
                Y = sb0("Y", [128, T, L])
                l0_norm(nc, a, ps, Z, Y, d)
                l0_ffn(nc, a, ps, X, Y)
        if 1 in layers:
            with ExitStack() as l1:
                pad = space(nc, l1, "l1g")[0]("pad", [C, B, PW, PW])
                group_norm(nc, "gn1", X, ps, gavg, st, [interior(pad[:, b, :, :]) for b in range(B)])
                d = {"pairs": pairs, "pd": nc.dram_tensor("pd", (2 * C, B, L), F32).ap()}
                l1_pairs(nc, a, ps, X, pad, d)
        if 2 in layers:
            with ExitStack() as l2:
                pad = space(nc, l2, "l2g")[0]("pad", [C, B, DW, DW])
                group_norm(nc, "gn2", X, ps, gavg, st, [interior(pad[:, b, :, :], RAD) for b in range(B)])
                l2_diffuse(nc, a, ps, X, pad, ident)
        if 3 in layers:
            l3(nc, a, ps, X, gavg, ident, st)
        load(nc, "out", [(out.rearrange("b c h w -> c b (h w)"), X[:, :, :])])


def row_tiles(x):
    x = np.concatenate([x] * B, axis=0)
    return np.ascontiguousarray(np.moveaxis(x.reshape(T, 128, *x.shape[1:]), 0, 1))


def layout(v):
    f = np.float32
    a = {}
    c = np.arange(C)
    a["gavg"] = ((c[:, None] // 3 == c[None, :] // 3) / 3).astype(f)
    a["ident"] = np.eye(128, dtype=f)
    p = "L0_conv_"
    a["w_in"] = np.ascontiguousarray(v[p + "in_proj_w"].T)
    a["cw"] = row_tiles(v[p + "conv_w"].reshape(E, TAPS))
    a["cb"] = row_tiles(v[p + "conv_b"])
    image = (np.arange(B * E) // E).reshape(T, 128)
    xp, dp = v[p + "x_proj_w"], v[p + "dt_proj_w"]
    w_bc = np.zeros((128, 2, T, 128), f)
    w_dt = np.zeros((128, T, K, B, R), f)
    w_up = np.zeros((K, B, R, T, K, 128), f)
    xe = row_tiles(np.ascontiguousarray(np.transpose(xp, (2, 0, 1))))
    de = row_tiles(np.ascontiguousarray(np.transpose(dp, (1, 0, 2))))
    for t in range(T):
        for b in range(B):
            rows = image[t] == b
            for k in range(K):
                w_dt[rows, t, k, b] = xe[rows, t, k, 0:R]
                w_up[k, b][:, t, k, rows] = de[rows, t, k].T
                for s in range(2):
                    o = 64 * (k % 2) + 32 * s + N * b
                    w_bc[rows, k // 2, t, o:o + N] = xe[rows, t, k, R + N * s:R + N * (s + 1)]
    a["w_bc"], a["w_dt"] = w_bc, w_dt.reshape(128, T, K * B * R)
    a["w_up"] = w_up.reshape(K * B * R, T * K, 128)
    a["dtb"] = row_tiles(np.ascontiguousarray(v[p + "dt_proj_b"].T))
    a["A"] = row_tiles(np.ascontiguousarray(np.transpose(v[p + "A_log"], (1, 0, 2)))).reshape(128, T * K, N)
    sel = np.zeros((T, 3, B, N, N, 128), f)
    for t in range(T):
        for b in range(B):
            for n in range(N):
                sel[t, :, b, n, n, image[t] == b] = 1
    a["sel"] = sel.reshape(T, 3 * B * N, N * 128).astype(mybir.dt.np(BF16))
    a["Ds"] = row_tiles(np.ascontiguousarray(v[p + "Ds"].T))
    a["gb"] = row_tiles(np.stack([v[p + "ln_g"], v[p + "ln_b"]], 1))
    avg = np.zeros((128, 7, 128), f)
    for i, (src, dst) in enumerate(((0, 0), (1, 0), (0, 1), (1, 1), (2, 1), (1, 2), (2, 2))):
        avg[:, i] = (image[src][:, None] == image[dst][None, :]) / E
    a["avg"] = avg
    a["c1"] = row_tiles(np.ascontiguousarray(v[p + "c1_w"].reshape(2 * E, E).T))
    per = lambda x: np.ascontiguousarray(np.moveaxis(x.reshape(2 * E // 128, 128, -1), 0, 1))
    a["c3"] = per(v[p + "c3_w"].reshape(C, 2 * E).T)
    a["c2"] = per(v[p + "c2_w"].reshape(2 * E, TAPS))
    a["ffn"] = per(np.stack([v[p + n] for n in ("c1_b", "bn1_g", "bn1_b", "bn1_m", "bn1_v",
                                                "c2_b", "bn2_g", "bn2_b", "bn2_m", "bn2_v")], 1))
    a["c3b"] = v[p + "c3_b"].reshape(C, 1)
    a["se1"] = np.ascontiguousarray(v[p + "se1_w"].T)
    a["se2"] = np.ascontiguousarray(v[p + "se2_w"].T)
    seb = np.zeros((C, 2), f)
    seb[0:C // 2, 0], seb[:, 1] = v[p + "se1_b"], v[p + "se2_b"]
    a["seb"] = seb
    i = np.arange(PT * 128)
    ci, cj = i % C, (i % C + i // C) % C
    keep = i < PAIR_ROWS
    for name, key in (("w", "weight"), ("m", "mask")):
        src = v["L1_conv_" + key]
        for n, (p0, p1) in (("a", (ci, cj)), ("b", (cj, ci))):
            g = np.where(keep[:, None], src[:, p0, p1].T, f(0))
            a[name + n] = np.ascontiguousarray(np.moveaxis(g.reshape(PT, 128, C), 0, 1))
    a["l1b"] = v["L1_conv_bias"].reshape(C, 1)
    yy = np.stack(np.divmod(np.arange(KS * KS), KS)) - RAD
    a["grid"] = np.ascontiguousarray(np.broadcast_to(yy.astype(f), (128, 2, KS * KS)))
    a["dm"] = np.moveaxis(np.tile(v["L2_conv_diff_metric"].reshape(C, 4), (2 * B, 1)).reshape(DT, 128, 4), 0, 1)
    layout3(v, a)
    return {k: np.ascontiguousarray(x) for k, x in a.items()}


def transform_basis(n):
    s = np.zeros(n)
    s[1] = s[n - 1] = 1.0
    idx = (np.arange(n)[:, None] - np.arange(n)[None, :]) % n
    S = s[idx] + np.diag(np.fft.fft(s).real)
    r, even = n // 2, 1 - n % 2
    P = np.zeros((n, n))
    P[0, 0] = 1.0
    for i in range(1, r - even + 1):
        P[i, i] = P[i, n - i] = 1 / math.sqrt(2)
    if even:
        P[r, r] = 1.0
    for i in range(r + 1, n):
        P[i, i], P[i, n - i] = -1 / math.sqrt(2), 1 / math.sqrt(2)
    CS = P @ S @ P.T
    h = n // 2 + 1
    ec, vc = np.linalg.eigh(CS[:h, :h])
    es, vs = np.linalg.eigh(CS[h:, h:])
    vc, vs = vc[:, np.argsort(-ec)], vs[:, np.argsort(-es)]
    c2, s2 = P @ np.vstack([vc, np.zeros((n - h, h))]), P @ np.vstack([np.zeros((h, n - h)), vs])
    e = np.zeros((n, n + 1))
    e[:, 0:n + 1:2] = c2
    e[:, 1:n:2] = np.hstack([s2, np.zeros((n, 1))])[:, 0:len(range(1, n, 2))]
    return np.delete(e, n - 1, axis=1)


def layout3(v, a):
    f = np.float32
    p = "L3_conv_"
    w1, b1 = np.zeros((C, HC), f), np.zeros((HC, 1), f)
    w2, b2 = np.zeros((HC, GO), f), np.zeros((1, GO), f)
    for i, (name, c0, o, n) in enumerate((("gsp", 0, O_SP, 2 * C3), ("alpha", C3, O_AL, 1),
                                          ("gfreq", C3, O_FR, 4 * C3), ("gfft", 2 * C3, O_FF, 4 * C3))):
        h = slice(i * HID, (i + 1) * HID)
        w1[c0:c0 + C3, h] = v[p + name + "_w1"].T
        b1[h, 0] = v[p + name + "_b1"]
        w2[h, o:o + n] = v[p + name + "_w2"].T
        b2[0, o:o + n] = v[p + name + "_b2"]
    a["w1"], a["b1"], a["w2"], a["b2"] = w1, b1, w2, b2
    wt = np.zeros((B, C3, 2, 2, 2 * C3), f)
    bw = np.zeros((1, 2, 2, B, C3), f)
    for i, name in enumerate(("conv05", "conv1")):
        wt[:, :, i] = v[p + name + "_w"].reshape(2 * C3, 2, C3).transpose(2, 1, 0)
        bw[:, i] = v[p + name + "_b"].reshape(2, 1, C3)
    a["wt"], a["bw"] = wt.reshape(BC, 2, 2, 2 * C3), bw.reshape(1, 2, 2, BC)
    w0 = v[p + "conv0_w"].transpose(3, 1, 2, 0).reshape(3 * C3, 1, 3, C3)
    a["w0"] = np.repeat(w0, B, axis=1)
    a["cw2"] = v[p + "conv2_w"].transpose(1, 2, 3, 0).reshape(C, TAPS, C)
    a["cb0"], a["cb2"] = v[p + "conv0_b"].reshape(C3, 1), v[p + "conv2_b"].reshape(C, 1)
    lv = np.arange(H)
    lv[-1] = H
    a["lv"] = np.broadcast_to(lv.astype(f), (BC, H))
    e = np.roll(transform_basis(H).astype(f).astype(np.float64), H // 2, axis=1)
    a["ef"], a["ei"] = e.T.astype(f), e.astype(f)
    a["e11"] = np.outer(e.sum(1), e.sum(1)).reshape(1, H * H).astype(f)
    i, k = np.arange(H), np.arange(UH)
    full, half = 2 * np.pi * np.outer(i, i) / H, 2 * np.pi * np.outer(i, k) / W
    a["fh"] = np.concatenate([np.cos(full), -np.sin(full)], 1).astype(f)
    a["fw"] = np.stack([np.concatenate([np.cos(half), -np.sin(half)], 1),
                        np.concatenate([np.sin(half), np.cos(half)], 1)], 1).astype(f)
    a["ih"] = np.concatenate([np.cos(full), np.sin(full)], 1).astype(f)
    wk = np.where((k == 0) | (k == W // 2), 1.0, 2.0)[:, None] / (H * W)
    c, s = wk * np.cos(half.T), wk * np.sin(half.T)
    a["iw"] = np.stack([np.concatenate([c, -s]), np.concatenate([-s, -c])], 1).astype(f)


_OUT = (B, C, H, W)


def kernel(**inputs):
    import concourse.bacc as bacc
    from concourse.bass_utils import run_bass_kernel_spmd

    v = {k: np.asarray(x) for k, x in inputs.items()}
    arrays = layout(v)
    nc = bacc.Bacc("TRN2", target_bir_lowering=False, num_devices=1)
    a, sent = {}, {}
    for name, arr in arrays.items():
        sent[f"in_{name}"] = arr
        a[name] = nc.dram_tensor(f"in_{name}", arr.shape, mybir.dt.from_np(arr.dtype), kind="ExternalInput").ap()
    sent["in_x"] = np.ascontiguousarray(v["x"])
    x = nc.dram_tensor("in_x", _OUT, F32, kind="ExternalInput").ap()
    out = nc.dram_tensor("out_0", _OUT, F32, kind="ExternalOutput").ap()
    program(nc, a, x, out)
    r = run_bass_kernel_spmd(nc, [sent], core_ids=[0])
    return r.results[0]["out_0"]
```

```python
from contextlib import ExitStack
import math

import numpy as np

import concourse.bass as bass
from concourse import mybir

F32 = mybir.dt.float32
BF16 = mybir.dt.bfloat16
I32 = mybir.dt.int32
ALU = mybir.AluOpType
ACT = mybir.ActivationFunctionType
AX = mybir.AxisListType

B, C, H, W = 2, 96, 48, 48
L = H * W
E = 2 * C
T = B * E // 128
R, N = 6, 16
K = 4
CH = 8 * W
NC = L // CH
BANK = 512
SEG = 2 * CH
NSEG = L // SEG
PW = W + 2
LOG_FLOOR = math.log(1e12)
PAIR_ROWS = (C // 2) * C + C // 2
PT = -(-PAIR_ROWS // 128)
TAPS = 9
C3 = C // 3
HID = 8
UH = W // 2 + 1


class Steps:

    def __init__(self, eng, sem):
        self.eng, self.sem, self.n = eng, sem, 0

    def __call__(self, ins):
        self.n += 1
        ins.then_inc(self.sem, 1)
        self.eng.wait_ge(self.sem, self.n)


def space(nc, ctx, tag):
    numbers = []

    def sb(name, shape, dt=F32):
        return ctx.enter_context(nc.sbuf_tensor(f"{tag}_{name}", shape, dt))

    def sem(name):
        s = ctx.enter_context(nc.semaphore(f"{tag}_{name}"))
        numbers.append(s.num)
        return s

    def clear():
        run = []
        for n in sorted(numbers) + [None]:
            if run and n != run[-1] + 1:
                nc.gpsimd.sem_clear(range(run[0], run[-1] + 1))
                run = []
            run.append(n)

    ctx.callback(clear)
    return sb, sem


def whole(tile):
    return tile[tuple(slice(None) for _ in tile.shape)]


def by_image(ap):
    return ap.rearrange("p (h w) -> p h w", w=W)


def interior(pad, border=1):
    return pad[:, border:border + H, border:border + W]


def scan_order(ap, k):
    v = ap[:, ::-1] if k % 2 else ap
    return v.rearrange("p (w h) -> p h w", h=H) if k >= 2 else v.rearrange("p (h w) -> p h w", w=W)


def banks(ps, first, count):
    return ps[:, first * BANK:(first + count) * BANK].rearrange("p (c n) -> p c n", n=BANK)[:, :, 0:CH]


def rsqrt_newton(step, dve, out, v, t1, t2):
    step(dve.tensor_tensor(t1, out, out, ALU.mult))
    step(dve.tensor_tensor(t2, t1, v, ALU.mult))
    step(dve.tensor_scalar(t1, t2, -0.5, 1.5, ALU.mult, ALU.add))


def group_norm(nc, tag, X, ps, gavg, st, outs, eps=1e-5):
    with ExitStack() as ctx:
        sb, sem = space(nc, ctx, tag)
        bn = sb("bn", [C, B, NC, 6])
        d, sq, var, t1, t2 = (sb(n, [C, B]) for n in ("d", "sq", "var", "t1", "t2"))
        s_dve, s_stat, s_mean, s_spread, s_var, s_inv, s_root = map(
            sem, ("dve", "stat", "mean", "spread", "var", "inv", "root"))
        mv, rstd, shift = st["mv"], st["rstd"], st["shift"]
        block = ctx.enter_context(nc.Block())

        @block.vector
        def _(dve):
            step = Steps(dve, s_dve)
            for b in range(B):
                for c in range(NC):
                    last = dve.bn_stats(bn[:, b, c, :], X[:, b, c * CH:(c + 1) * CH])
                step(last)
                ins = dve.bn_aggr(mv[:, b, :], bn[:, b, :, :].rearrange("p c s -> p (c s)"))
                ins.then_inc(s_stat, 1)
            dve.wait_ge(s_stat, B)
            dve.wait_ge(s_mean, 1)
            step(dve.tensor_tensor(d[:, :], mv[:, :, 0], ps[0:C, 0:B], ALU.subtract))
            step(dve.tensor_tensor(sq[:, :], d[:, :], d[:, :], ALU.mult))
            dve.tensor_tensor(sq[:, :], sq[:, :], mv[:, :, 1], ALU.add).then_inc(s_spread, 1)
            dve.wait_ge(s_var, 1)
            step(dve.tensor_scalar(var[:, :], ps[0:C, BANK:BANK + B], eps, None, ALU.add))
            dve.reciprocal(t1[:, :], var[:, :]).then_inc(s_inv, 1)
            dve.wait_ge(s_root, 1)
            rsqrt_newton(step, dve, rstd[:, :], var[:, :], t1[:, :], t2[:, :])
            step(dve.tensor_tensor(rstd[:, :], rstd[:, :], t1[:, :], ALU.mult))
            step(dve.tensor_scalar(t2[:, :], ps[0:C, 0:B], -1.0, None, ALU.mult))
            step(dve.tensor_tensor(shift[:, :], t2[:, :], rstd[:, :], ALU.mult))
            for b in range(B):
                ins = dve.tensor_scalar(outs[b], by_image(X[:, b, :]), rstd[:, b:b + 1], shift[:, b:b + 1],
                                        ALU.mult, ALU.add)
            step(ins)

        @block.tensor
        def _(pe):
            pe.wait_ge(s_stat, B)
            pe.matmul(ps[0:C, 0:B], gavg[:, :], mv[:, :, 0], start=True, stop=True).then_inc(s_mean, 1)
            pe.wait_ge(s_spread, 1)
            pe.matmul(ps[0:C, BANK:BANK + B], gavg[:, :], sq[:, :], start=True, stop=True).then_inc(s_var, 1)

        @block.scalar
        def _(act):
            act.wait_ge(s_inv, 1)
            act.activation(rstd[:, :], t1[:, :], ACT.Sqrt).then_inc(s_root, 1)


def load(nc, tag, pairs):
    with ExitStack() as ctx:
        _, sem = space(nc, ctx, tag)
        s_in = sem("in")
        block = ctx.enter_context(nc.Block())

        @block.sync
        def _(sp):
            for dst, src in pairs:
                sp.dma_start(dst, src).then_inc(s_in, 16)
            sp.wait_ge(s_in, 16 * len(pairs))




def l0_project(nc, a, XG, ps, XI, Z, ahead):
    with ExitStack() as ctx:
        sb, sem = space(nc, ctx, "l0p")
        w_in = sb("w_in", [C, 2 * E])
        cw = sb("cw", [128, T, TAPS])
        cb = sb("cb", [128, T])
        pad = sb("pad", [128, T, PW, PW])
        acc = sb("acc", [128, T, L])
        prod = sb("prod", [128, 2, L])
        s_in, s_pad, s_mm, s_ev, s_silu, s_tap, s_first, s_prod, s_sum = map(
            sem, "in pad mm ev silu tap first prod sum".split())
        s_ahead = sem("ahead")
        SUMS = [0, 2, 3]
        own = [TAPS - 1 - n for n in SUMS]
        block = ctx.enter_context(nc.Block())
        parts = [[(0, 128, 0, 0)], [(0, 64, 128, 0), (64, 128, 0, 1)], [(0, 128, 64, 1)]]

        @block.sync
        def _(sp):
            sp.dma_start(w_in[:, :], a["w_in"]).then_inc(s_in, 16)
            sp.dma_start(cw[:, :, :], a["cw"]).then_inc(s_in, 16)
            sp.dma_start(cb[:, :], a["cb"]).then_inc(s_in, 16)
            for dst, src in ahead:
                sp.dma_start(dst, src).then_inc(s_ahead, 16)
            sp.wait_ge(s_in, 48)
            sp.wait_ge(s_ahead, 16 * len(ahead))

        @block.tensor
        def _(pe):
            pe.wait_ge(s_in, 48)
            for j in range(2 * T):
                half, t = divmod(j, T)
                for c in range(NC):
                    q = j * NC + c
                    if q >= 8:
                        pe.wait_ge(s_ev, q - 7)
                    for lo, hi, w0, b in parts[t]:
                        mm = pe.matmul(ps[lo:hi, (q % 8) * BANK:(q % 8) * BANK + CH],
                                       w_in[:, half * E + w0:half * E + w0 + hi - lo],
                                       XG[:, b, c * CH:(c + 1) * CH], start=True, stop=True)
                    mm.then_inc(s_mm, 1)

        @block.scalar
        def _(act):
            act.wait_ge(s_pad, T)
            act.wait_ge(s_in, 48)
            for j in range(2 * T):
                half, t = divmod(j, T)
                for c in range(NC):
                    q = j * NC + c
                    act.wait_ge(s_mm, q + 1)
                    src = ps[:, (q % 8) * BANK:(q % 8) * BANK + CH]
                    if half:
                        act.copy(Z[:, t, c * CH:(c + 1) * CH], src).then_inc(s_ev, 1)
                    else:
                        act.copy(pad[:, t, 1 + 8 * c:9 + 8 * c, 1:1 + W],
                                 src.rearrange("p (h w) -> p h w", w=W)).then_inc(s_ev, 1)
                if not half:
                    act.wait_ge(s_ev, NC * (j + 1))
                    for i in range(SUMS[t] + 1):
                        dy, dx = divmod(i, 3)
                        g = sum(SUMS[:t]) + i - 1
                        if i and g >= 2:
                            act.wait_ge(s_sum, g - 1)
                        dst = prod[:, g % 2, :] if i else acc[:, t, :]
                        act.activation(by_image(dst), pad[:, t, dy:dy + H, dx:dx + W], ACT.Copy,
                                       scale=cw[:, t, i:i + 1]).then_inc(s_prod if i else s_first, 1)
            for t in range(T):
                act.wait_ge(s_tap, sum(own[:t + 1]))
                act.activation(XI[:, t, :], acc[:, t, :], ACT.Silu, bias=cb[:, t:t + 1]).then_inc(s_silu, 1)
            act.wait_ge(s_silu, T)

        @block.vector
        def _(dve):
            for t in range(T):
                dve.memset(pad[:, t, :, :], 0.0).then_inc(s_pad, 1)
            dve.wait_ge(s_in, 48)
            for t in range(T):
                dve.wait_ge(s_first, t + 1)
                if SUMS[t]:
                    dve.wait_ge(s_sum, sum(SUMS[:t + 1]))
                dst = by_image(acc[:, t, :])
                for n, i in enumerate(range(SUMS[t] + 1, TAPS)):
                    dy, dx = divmod(i, 3)
                    if n:
                        dve.wait_ge(s_tap, sum(own[:t]) + n)
                    dve.scalar_tensor_tensor(dst, pad[:, t, dy:dy + H, dx:dx + W], cw[:, t, i:i + 1], dst,
                                             ALU.mult, ALU.add).then_inc(s_tap, 1)

        @block.gpsimd
        def _(pool):
            for t in range(T):
                for n in range(SUMS[t]):
                    g = sum(SUMS[:t]) + n
                    if not n:
                        pool.wait_ge(s_first, t + 1)
                    else:
                        pool.wait_ge(s_sum, g)
                    pool.wait_ge(s_prod, g + 1)
                    pool.tensor_tensor(acc[:, t, :], acc[:, t, :], prod[:, g % 2, :], ALU.add).then_inc(s_sum, 1)


def l0_rows(nc, a, ps, XI, P, d, w_bc, w_dt, al):
    with ExitStack() as ctx:
        sb, sem = space(nc, ctx, "l0r")
        na = sb("na", [128, K * T, 2 * N])
        bc = sb("bc", [128, 2, L])
        rest = sb("rest", [128, L])
        parts = sb("parts", [128, 2, 3, L], BF16)
        wa, wb, mask = (sb(n, [128, PT, C]) for n in ("wa", "wb", "mask"))
        s_wa, s_wb, s_ma, s_mb, s_pair, s_wout = map(sem, "wa wb ma mb pair wout".split())
        s_bc, s_bce, s_hi, s_mid, s_lo, s_rest, s_na, s_out = map(
            sem, "bc bce hi mid lo rest na out".split())
        block = ctx.enter_context(nc.Block())

        @block.sync
        def _(sp):
            for dst, src, s_done in ((wa, "wa", s_wa), (mask, "ma", s_ma), (wb, "wb", s_wb)):
                sp.dma_start(dst[:, :, :], a[src]).then_inc(s_done, 16)
            sp.wait_ge(s_na, 2)
            sp.dma_start(d["na"].rearrange("g p n -> p g n"), na[:, :, :]).then_inc(s_out, 16)
            sp.wait_ge(s_pair, 1)
            sp.dma_start(mask[:, :, :], a["mb"]).then_inc(s_mb, 16)
            for m in range(2):
                for i, s_part in enumerate((s_hi, s_mid, s_lo)):
                    sp.wait_ge(s_part, m + 1)
                    for r in range(4):
                        k, s = 2 * m + r // 2, r % 2
                        sp.dma_start(d["bc"][k, s, i * B * N:(i + 1) * B * N, :],
                                     parts[32 * r:32 * r + 32, m, i, :]).then_inc(s_out, 16)
            sp.wait_ge(s_pair, 4)
            sp.dma_start(d["pairs"], wa[:, :, :]).then_inc(s_wout, 16)
            sp.wait_ge(s_out, 16 * 25)
            sp.wait_ge(s_wout, 16)

        @block.gpsimd
        def _(pool):
            pool.wait_ge(s_wa, 16)
            pool.wait_ge(s_ma, 16)
            pool.tensor_tensor(wa[:, :, :], wa[:, :, :], mask[:, :, :], ALU.mult).then_inc(s_pair, 1)
            pool.wait_ge(s_wb, 16)
            pool.wait_ge(s_mb, 16)
            pool.tensor_tensor(wb[:, :, :], wb[:, :, :], mask[:, :, :], ALU.mult).then_inc(s_pair, 1)
            pool.wait_ge(s_pair, 2)
            pool.tensor_tensor(wa[:, 1:, :], wa[:, 1:, :], wb[:, 1:, :], ALU.add).then_inc(s_pair, 1)
            pool.wait_ge(s_pair, 3)
            pool.tensor_tensor(wa[C:128, 0, :], wa[C:128, 0, :], wb[C:128, 0, :], ALU.add).then_inc(s_pair, 1)

        @block.tensor
        def _(pe):
            for q in range(3 * NC):
                m, c = divmod(q, NC)
                if q >= 8:
                    pe.wait_ge(s_bce, q - 7)
                o = (q % 8) * BANK
                for t in range(T):
                    w = w_bc[:, m, t, :] if m < 2 else w_dt[:, t, :]
                    mm = pe.matmul(ps[0:128 if m < 2 else K * B * R, o:o + CH], w, XI[:, t, c * CH:(c + 1) * CH],
                                   start=(t == 0), stop=(t == T - 1))
                mm.then_inc(s_bc, 1)

        @block.scalar
        def _(act):
            act.mul(na[:, :, 0:N], al[:, :, :], -1.0).then_inc(s_na, 1)
            act.mul(na[:, :, N:2 * N], al[:, :, :], -0.5).then_inc(s_na, 1)
            for m in range(2):
                for c in range(NC):
                    q = m * NC + c
                    act.wait_ge(s_bc, q + 1)
                    for r in range(2):
                        ins = act.copy(scan_order(bc[:, m, :], 2 * m + r)[64 * r:64 * r + 64, 8 * c:8 * c + 8, :],
                                       ps[64 * r:64 * r + 64, (q % 8) * BANK:(q % 8) * BANK + CH]
                                       .rearrange("p (h w) -> p h w", w=W))
                    ins.then_inc(s_bce, 1)
                act.wait_ge(s_bce, NC * (m + 1))
                act.copy(parts[:, m, 0, :], bc[:, m, :]).then_inc(s_hi, 1)
                act.wait_ge(s_rest, m + 1)
                act.copy(parts[:, m, 1, :], rest[:, :]).then_inc(s_mid, 1)
            for c in range(NC):
                q = 2 * NC + c
                act.wait_ge(s_bc, q + 1)
                act.copy(P[:, c * CH:(c + 1) * CH], ps[0:K * B * R, (q % 8) * BANK:(q % 8) * BANK + CH]
                         ).then_inc(s_bce, 1)

        @block.vector
        def _(dve):
            for m in range(2):
                dve.wait_ge(s_hi, m + 1)
                if m:
                    dve.wait_ge(s_lo, m)
                dve.tensor_tensor(rest[:, :], bc[:, m, :], parts[:, m, 0, :], ALU.subtract).then_inc(s_rest, 1)
                dve.wait_ge(s_mid, m + 1)
                dve.wait_ge(s_rest, m + 1)
                dve.tensor_tensor(parts[:, m, 2, :], rest[:, :], parts[:, m, 1, :], ALU.subtract).then_inc(s_lo, 1)


def l0_steps(nc, ps, XI, P, d, w_up, dtb):
    with ExitStack() as ctx:
        sb, sem = space(nc, ctx, "l0s")
        NS = 4
        HI = L // 2
        x0, e, ln, wm = (sb(n, [128, NS, HI]) for n in ("x0", "e", "ln", "wm"))
        dl, vv = (sb(n, [128, 2, L]) for n in ("dl", "vv"))
        s_up, s_x0, s_ab, s_e, s_ln, s_wm, s_c, s_sumv, s_sump, s_min, s_dl, s_vv = map(
            sem, "up x0 ab e ln wm c sumv sump min dl vv".split())
        s_store = [sem(f"store{i}") for i in range(2)]
        G = K * T
        Q = 2 * G
        by_dve = lambda q: q % 4 == 3
        block = ctx.enter_context(nc.Block())

        def rows(tile, q):
            g, half = q // 2, q % 2
            return scan_order(tile[:, g % 2, :], g % K)[:, half * (H // 2):(half + 1) * (H // 2), :]

        @block.sync
        def _(sp):
            for g in range(G):
                sp.wait_ge(s_dl, 2 * g + 2)
                sp.dma_start(d["dlt"][g], dl[:, g % 2, :]).then_inc(s_store[g % 2], 16)
                sp.wait_ge(s_vv, 2 * g + 2)
                sp.dma_start(d["v"][g], vv[:, g % 2, :]).then_inc(s_store[g % 2], 16)
            for i in range(2):
                sp.wait_ge(s_store[i], 32 * (G // 2))

        @block.tensor
        def _(pe):
            for q in range(Q):
                g, half = q // 2, q % 2
                if q >= 2:
                    pe.wait_ge(s_ab, q - 1)
                for c in range(3 * half, 3 * half + 3):
                    mm = pe.matmul(ps[:, c * BANK:c * BANK + CH], w_up[:, g, :],
                                   P[:, c * CH:(c + 1) * CH], start=True, stop=True)
                mm.then_inc(s_up, 1)

        @block.scalar
        def _(act):
            act.preload_act_table_set("natural_log_exp_and_others")
            for i in range(Q + 1):
                q = i
                if q < Q:
                    g, half, s = q // 2, q % 2, q % NS
                    b = dtb[:, g // K, g % K:g % K + 1]
                    act.wait_ge(s_up, q + 1)
                    if q >= NS:
                        act.wait_ge(s_dl, q - NS + 1)
                    act.activation(x0[:, s, :].rearrange("p (c n) -> p c n", n=CH), banks(ps, 3 * half, 3),
                                   ACT.Identity, bias=b).then_inc(s_x0, 1)
                    act.activation(e[:, s, :].rearrange("p (c n) -> p c n", n=CH), banks(ps, 3 * half, 3),
                                   ACT.Abs, bias=b).then_inc(s_ab, 1)
                q = i - 1
                if 0 <= q < Q:
                    act.wait_ge(s_ab, q + 1)
                    act.activation(e[:, q % NS, :], e[:, q % NS, :], ACT.Exp, scale=-1.0).then_inc(s_e, 1)
                    act.wait_ge(s_e, q + 1)
                    act.activation(ln[:, q % NS, :], e[:, q % NS, :], ACT.Ln, bias=1.0).then_inc(s_ln, 1)

        @block.vector
        def _(dve):
            n_own = 0
            for i in range(Q + 2):
                q = i
                if q < Q:
                    dve.wait_ge(s_e, q + 1)
                    dve.tensor_scalar(wm[:, q % NS, :], e[:, q % NS, :], 1.0, -1.0, ALU.add, ALU.add).then_inc(s_wm, 1)
                q = i - 1
                if 0 <= q < Q:
                    s = q % NS
                    if by_dve(q):
                        dve.wait_ge(s_c, q + 1)
                        dve.wait_ge(s_ln, q + 1)
                        dve.tensor_tensor(ln[:, s, :], ln[:, s, :], wm[:, s, :], ALU.add).then_inc(s_sumv, 1)
                        n_own += 1
                        dve.wait_ge(s_sumv, n_own)
                    else:
                        dve.wait_ge(s_sump, q + 1 - n_own)
                    dve.tensor_tensor(ln[:, s, :], ln[:, s, :], e[:, s, :], ALU.min).then_inc(s_min, 1)
                q = i - 2
                if q >= 0:
                    dve.wait_ge(s_dl, q + 1)
                    half = q % 2
                    dve.tensor_tensor(rows(vv, q), by_image(XI[:, q // 2 // K, half * HI:(half + 1) * HI]),
                                      rows(dl, q), ALU.mult).then_inc(s_vv, 1)
                q = i - 1
                if 0 <= q < Q:
                    s = q % NS
                    dve.wait_ge(s_min, q + 1)
                    if q >= 4:
                        dve.wait_ge(s_store[q // 2 % 2], 32 * (q // 4))
                    dve.scalar_tensor_tensor(rows(dl, q), by_image(x0[:, s, :]), 0.0, by_image(ln[:, s, :]),
                                             ALU.max, ALU.add).then_inc(s_dl, 1)

        @block.gpsimd
        def _(pool):
            for q in range(Q):
                s = q % NS
                pool.wait_ge(s_wm, q + 1)
                pool.tensor_tensor(wm[:, s, :], e[:, s, :], wm[:, s, :], ALU.subtract).then_inc(s_c, 1)
                if not by_dve(q):
                    pool.wait_ge(s_c, q + 1)
                    pool.wait_ge(s_ln, q + 1)
                    pool.tensor_tensor(ln[:, s, :], ln[:, s, :], wm[:, s, :], ALU.add).then_inc(s_sump, 1)


def l0_scan(nc, a, ps, ident, d):
    with ExitStack() as ctx:
        sb, sem = space(nc, ctx, "l0c")
        NR, NDA, NHV, NHP = 6, 4, 4, 2
        SPAN = 6
        AHEAD = 3
        dlt, v, S, y = (sb(n, [128, 2, SEG]) for n in ("dlt", "v", "S", "y"))
        Bp, Cp = (sb(n, [3 * B * N, 2, SEG], BF16) for n in ("Bp", "Cp"))
        sel = sb("sel", [3 * B * N, 2, N * 128], BF16)
        na = sb("na", [128, 2, 2 * N])
        da = sb("da", [128, NDA, SEG])
        r = sb("r", [128, NR, SEG])
        h = sb("h", [128, N, SEG])
        hcv = sb("hcv", [128, NHV, SEG])
        hcp = sb("hcp", [128, NHP, SEG])
        cs = sb("cs", [128, NHP, SEG])
        credit = sb("credit", [128, 8])
        floor = sb("floor", [128, 1])
        s_in = [sem(f"in{i}") for i in range(2)]
        s_sel = [sem(f"sel{i}") for i in range(2)]
        s_yout = [sem(f"yout{i}") for i in range(2)]
        s_scan, s_ub, s_hv, s_hp, s_cc, s_y, s_evac = map(sem, ("scan", "ub", "hv", "hp", "cc", "y", "evac"))
        s_a, s_tanh, s_w, s_b, s_c, s_S, s_init = map(sem, ("a", "tanh", "w", "b", "c", "S", "init"))
        HP0 = 6
        PB, PC, PY = 0, 2, 4
        block = ctx.enter_context(nc.Block())
        U = 2 * NSEG
        J = U * N
        NLOAD = 5

        def nest(eng):
            return eng.Fori(0, T), eng.Fori(0, K // 2)

        def by_pool(j):
            return j % 3 == 2

        def dve_steps(j):
            return 2 * (j // 3) + j % 3

        def chunks(ap):
            return ap.rearrange("p (c n) -> p c n", n=CH)

        @block.sync
        def _(sp):
            lt, lq = nest(sp)
            with lt as t, lq as q:
                for u in range(U):
                    g = t * (2 * U) + q * U + u
                    kt = t * K + q * 2 + u // NSEG
                    c0 = (u % NSEG) * SEG
                    i = u % 2
                    sp.wait_ge(s_evac, g + 1)
                    sp.dma_start(dlt[:, i, :], d["dlt"][kt, :, c0:c0 + SEG]).then_inc(s_in[i], 16)
                    sp.dma_start(na[:, i, :], d["na"][kt]).then_inc(s_in[i], 16)
                    sp.dma_start(Bp[:, i, :], d["bc"][q * 2 + u // NSEG, 0, :, c0:c0 + SEG]).then_inc(s_in[i], 16)
                    if u < 2:
                        sp.dma_start(sel[:, i, :], a["sel"][t]).then_inc(s_sel[i], 16)
                    sp.dma_start(v[:, i, :], d["v"][kt, :, c0:c0 + SEG]).then_inc(s_in[i], 16)
                    sp.dma_start(Cp[:, i, :], d["bc"][q * 2 + u // NSEG, 1, :, c0:c0 + SEG]).then_inc(s_in[i], 16)
            for i in range(2):
                sp.wait_ge(s_in[i], 16 * NLOAD * K * T * NSEG // 2)
                sp.wait_ge(s_sel[i], 16 * 2 * T)

        @block.tensor
        def _(pe):
            lt, lq = nest(pe)
            with lt as t, lq as q:
                base = t * (2 * J) + q * J
                vbase = t * (2 * dve_steps(J)) + q * dve_steps(J)
                pbase = t * (2 * J // 3) + q * (J // 3)
                segs = t * (2 * U) + q * U

                def spread(rows, first, j, done):
                    i, n = (j // N) % 2, j % N
                    for c in range(2):
                        mm = pe.matmul(ps[:, (first + c) * BANK:(first + c) * BANK + CH],
                                       sel[:, i, n * 128:(n + 1) * 128], rows[:, i, c * CH:(c + 1) * CH],
                                       start=True, stop=True)
                    mm.then_inc(done, 1)

                def b_rows(j):
                    u = j // N
                    if j % N == 0:
                        pe.wait_ge(s_in[u % 2], (t * U + q * (U // 2) + u // 2 + 1) * (16 * NLOAD))
                        if u < 2:
                            pe.wait_ge(s_sel[u], (t * 2 + q + 1) * 16)
                    pe.wait_ge(s_ub, base + j + 1)
                    spread(Bp, PB, j, s_b)

                def c_rows(j):
                    if j % 3 == 0:
                        pe.wait_ge(s_cc, pbase + j // 3 + 1)
                    else:
                        pe.wait_ge(s_hv, vbase + dve_steps(j))
                    spread(Cp, PC, j, s_c)

                def add_y(j):
                    u, n = j // N, j % N
                    if n == 0:
                        pe.wait_ge(s_evac, segs + u + 1)
                    if by_pool(j):
                        pe.wait_ge(s_hp, pbase + j // 3 + 1 + HP0)
                        hc = hcp[:, (j // 3) % NHP, :]
                    else:
                        pe.wait_ge(s_hv, vbase + dve_steps(j) + 1)
                        hc = hcv[:, dve_steps(j) % NHV, :]
                    for c in range(2):
                        o = (PY + 2 * (u % 2) + c) * BANK
                        mm = pe.matmul(ps[:, o:o + CH], ident[:, :], hc[:, c * CH:(c + 1) * CH],
                                       start=(n == 0), stop=(n == N - 1))
                    mm.then_inc(s_y, 1)

                for j in range(AHEAD + 1):
                    b_rows(j)
                for j in range(J + 3):
                    if j + AHEAD + 1 < J:
                        b_rows(j + AHEAD + 1)
                    if j < J:
                        c_rows(j)
                    if j >= 3:
                        add_y(j - 3)

        @block.vector
        def _(dve):
            dve.memset(floor[:, :], 0.5 * LOG_FLOOR).then_inc(s_init, 1)
            for i, (s, n) in enumerate(((s_scan, NR), (s_ub, 1), (s_cc, 1), (s_hp, HP0), (s_y, SPAN), (s_evac, 2),
                                        (s_yout[0], 16), (s_yout[1], 16))):
                dve.memset(credit[:, i:i + 1], 0.0).then_inc(s, n)
            lt, lq = nest(dve)
            with lt as t, lq as q:
                base = t * (2 * J) + q * J
                segs = t * (2 * U) + q * U
                loads = t * U + q * (U // 2)

                def cumsum(u):
                    i = u % 2
                    dve.wait_ge(s_in[i], (loads + u // 2 + 1) * (16 * NLOAD))
                    if u % NSEG:
                        dve.wait_ge(s_S, segs + u)
                        init = S[:, 1 - i, SEG - 1:SEG]
                    else:
                        init = 0.0
                    dve.tensor_tensor_scan(S[:, i, :], dlt[:, i, :], dlt[:, i, :], init, ALU.add, ALU.bypass
                                           ).then_inc(s_S, 1)

                def b_r(j):
                    dve.wait_ge(s_tanh, base + j + 1)
                    dve.wait_ge(s_b, base + j + 1)
                    rj = chunks(r[:, j % NR, :])
                    dve.scalar_tensor_tensor(rj, rj, 1.0, banks(ps, PB, 2), ALU.add, ALU.mult).then_inc(s_ub, 1)

                def times_c(j):
                    dve.wait_ge(s_scan, base + j + NR + 1)
                    dve.wait_ge(s_c, base + j + 1)
                    dve.wait_ge(s_y, base + j + 1)
                    dve.tensor_tensor(chunks(hcv[:, dve_steps(j) % NHV, :]), banks(ps, PC, 2), chunks(h[:, j % N, :]),
                                      ALU.mult).then_inc(s_hv, 1)

                cumsum(0)
                for j in range(AHEAD):
                    b_r(j)
                for j in range(J):
                    u, n = j // N, j % N
                    if j + AHEAD < J:
                        b_r(j + AHEAD)
                    if j and not by_pool(j - 1):
                        times_c(j - 1)
                    if n == 10 and u + 1 < U:
                        cumsum(u + 1)
                    dve.wait_ge(s_a, base + j + 1)
                    dve.wait_ge(s_w, base + j + 1)
                    if u % NSEG:
                        init = h[:, n, SEG - 1:SEG]
                    else:
                        init = 0.0
                    dve.tensor_tensor_scan(h[:, n, :], da[:, j % NDA, :], r[:, j % NR, :], init, ALU.mult, ALU.add
                                           ).then_inc(s_scan, 1)
                assert by_pool(J - 1)

        @block.gpsimd
        def _(pool):
            lt, lq = nest(pool)
            with lt as t, lq as q:
                base = t * (2 * J) + q * J
                pbase = t * (2 * J // 3) + q * (J // 3)
                for j in range(J + AHEAD + 1):
                    if j < J:
                        if j % N == 0:
                            pool.wait_ge(s_in[(j // N) % 2], (t * U + q * (U // 2) + j // N // 2 + 1) * (16 * NLOAD))
                        pool.wait_ge(s_ub, base + j + 2)
                        pool.tensor_tensor(r[:, j % NR, :], r[:, j % NR, :], v[:, (j // N) % 2, :], ALU.mult
                                           ).then_inc(s_w, 1)
                    e = j - AHEAD - 1
                    if e >= 0 and by_pool(e):
                        pool.wait_ge(s_scan, base + e + NR + 1)
                        pool.wait_ge(s_cc, pbase + e // 3 + 2)
                        pool.wait_ge(s_y, base + e + 1)
                        pool.tensor_tensor(hcp[:, (e // 3) % NHP, :], cs[:, (e // 3) % NHP, :], h[:, e % N, :],
                                           ALU.mult).then_inc(s_hp, 1)

        @block.scalar
        def _(act):
            act.wait_ge(s_init, 1)
            lt, lq = nest(act)
            with lt as t, lq as q:
                base = t * (2 * J) + q * J
                pbase = t * (2 * J // 3) + q * (J // 3)
                segs = t * (2 * U) + q * U

                def store(u):
                    i = u % 2
                    act.wait_ge(s_y, base + (u + 1) * N + SPAN)
                    act.wait_ge(s_yout[i], (t * U + q * (U // 2) + u // 2 + 1) * 16)
                    act.activation(chunks(y[:, i, :]), banks(ps, PY + 2 * i, 2), ACT.Copy, scale=0.5
                                   ).then_inc(s_evac, 1)
                    act.wait_ge(s_evac, segs + u + 3)
                    kt = t * K + q * 2 + u // NSEG
                    c0 = (u % NSEG) * SEG
                    act.dma_start(d["y"][kt, :, c0:c0 + SEG], y[:, i, :]).then_inc(s_yout[i], 16)

                for j in range(J + 6):
                    u, n, i = j // N, j % N, (j // N) % 2
                    if j < J:
                        if n == 0:
                            act.wait_ge(s_in[i], (t * U + q * (U // 2) + u // 2 + 1) * (16 * NLOAD))
                            act.wait_ge(s_S, segs + u + 1)
                        act.wait_ge(s_scan, base + j + 1)
                        act.activation(r[:, j % NR, :], S[:, i, :], ACT.Tanh, bias=floor[:, :],
                                       scale=na[:, i, N + n:N + n + 1]).then_inc(s_tanh, 1)
                    e = j - 2
                    if 0 <= e < J:
                        ie, ne = (e // N) % 2, e % N
                        act.wait_ge(s_scan, base + e + 1 + NR - NDA)
                        act.activation(da[:, e % NDA, :], dlt[:, ie, :], ACT.Exp,
                                       scale=na[:, ie, ne:ne + 1]).then_inc(s_a, 1)
                    e = j - 5
                    if 0 <= e < J and by_pool(e):
                        act.wait_ge(s_c, base + e + 1)
                        act.wait_ge(s_hp, pbase + e // 3 + 1 + HP0 - NHP)
                        act.copy(chunks(cs[:, (e // 3) % NHP, :]), banks(ps, PC, 2)).then_inc(s_cc, 1)
                    if n == 8 and 0 < u < U:
                        store(u - 1)
                store(U - 1)
            for i in range(2):
                act.wait_ge(s_yout[i], 16 * (K * T * NSEG // 2 + 1))


def l0_norm(nc, a, ps, Z, Y, d, ahead):
    with ExitStack() as ctx:
        sb, sem = space(nc, ctx, "l0n")
        yk = sb("yk", [128, 3, L])
        Ds = sb("Ds", [128, T, K])
        dsum = sb("dsum", [128, T])
        gb = sb("gb", [128, T, 2])
        avg = sb("avg", [128, 7, 128])
        sq = sb("sq", [128, T, L])
        iv = sb("iv", [128, T, L])
        avgv, selv = sb("avgv", [128, T, B]), sb("selv", [B, T, 128])
        var, root = sb("var", [B, L]), sb("root", [B, L])
        s_in, s_dve, s_mean, s_yc, s_sq, s_var, s_eps, s_inv, s_root, s_rep, s_n, s_aff, s_add = map(
            sem, "in dve mean yc sq var eps inv root rep n aff add".split())
        s_ds, s_ahead = sem("ds"), sem("ahead")
        s_y = [sem(f"y{t}") for t in range(T)]
        s_k = [sem(f"k{i}") for i in range(3)]
        mix = [[(0, 0), (1, 1)], [(0, 2), (1, 3), (2, 4)], [(1, 5), (2, 6)]]
        adds = [(t, k) for t in range(T) for k in range(1, K)]
        block = ctx.enter_context(nc.Block())

        @block.sync
        def _(sp):
            sp.dma_start(Ds[:, :, :], a["Ds"]).then_inc(s_ds, 16)
            for j, (t, k) in enumerate(adds):
                if k == 1:
                    sp.dma_start(Y[:, t, :], d["y"][t * K]).then_inc(s_y[t], 16)
                if j == 3:
                    for dst, src in ((gb[:, :, :], a["gb"]), (avg[:, :, :], a["avg"]), (avgv[:, :, :], a["avgv"]),
                                     (selv[:, :, :], a["selv"])):
                        sp.dma_start(dst, src).then_inc(s_in, 16)
                if j == 8:
                    for dst, src in ahead:
                        sp.dma_start(dst, src).then_inc(s_ahead, 16)
                if j >= 3:
                    sp.wait_ge(s_add, j - 2)
                sp.dma_start(yk[:, j % 3, :], d["y"][t * K + k]).then_inc(s_k[j % 3], 16)

            sp.wait_ge(s_ahead, 16 * len(ahead))

        @block.tensor
        def _(pe):
            pe.wait_ge(s_in, 64)
            for q in range(T * NC):
                t, c = divmod(q, NC)
                if not c:
                    pe.wait_ge(s_add, min(t + 2, T) * (K - 1))
                if q >= 8:
                    pe.wait_ge(s_yc, q - 7)
                o = (q % 8) * BANK
                for m, (f, blk) in enumerate(mix[t]):
                    mm = pe.matmul(ps[:, o:o + CH], avg[:, blk, :], Y[:, f, c * CH:(c + 1) * CH],
                                   start=(m == 0), stop=(m == len(mix[t]) - 1))
                mm.then_inc(s_mean, 1)
            pe.wait_ge(s_sq, T)
            for c in range(NC):
                for t in range(T):
                    mm = pe.matmul(ps[0:B, c * BANK:c * BANK + CH], avgv[:, t, :], sq[:, t, c * CH:(c + 1) * CH],
                                   start=(t == 0), stop=(t == T - 1))
                mm.then_inc(s_var, 1)
            pe.wait_ge(s_eps, NC)
            for q in range(NC * T):
                c, t = divmod(q, T)
                pe.wait_ge(s_root, c + 1)
                if q >= 8:
                    pe.wait_ge(s_n, q - 7)
                pe.matmul(ps[:, (q % 8) * BANK:(q % 8) * BANK + CH], selv[:, t, :], root[:, c * CH:(c + 1) * CH],
                          start=True, stop=True).then_inc(s_rep, 1)

        @block.scalar
        def _(act):
            for t in range(T):
                act.wait_ge(s_yc, NC * (t + 1))
                act.activation(sq[:, t, :], iv[:, t, :], ACT.Square).then_inc(s_sq, 1)
            act.wait_ge(s_in, 64)
            for c in range(NC):
                act.wait_ge(s_inv, c + 1)
                act.activation(root[:, c * CH:(c + 1) * CH], root[:, c * CH:(c + 1) * CH], ACT.Sqrt).then_inc(s_root, 1)
            for q in range(NC * T):
                c, t = divmod(q, T)
                act.wait_ge(s_n, q + 1)
                ch = yk[:, t, c * CH:(c + 1) * CH]
                act.activation(ch, ch, ACT.Identity, scale=gb[:, t, 0:1], bias=gb[:, t, 1:2]).then_inc(s_aff, 1)

        @block.vector
        def _(dve):
            step = Steps(dve, s_dve)
            dve.wait_ge(s_ds, 16)
            step(dve.tensor_reduce(dsum[:, :], Ds[:, :, :], AX.X, ALU.add))
            for j, (t, k) in enumerate(adds):
                dve.wait_ge(s_k[j % 3], 16 * (j // 3 + 1))
                if k == 1:
                    dve.wait_ge(s_y[t], 16)
                if j:
                    dve.wait_ge(s_add, j)
                dst = by_image(Y[:, t, :])
                src = scan_order(yk[:, j % 3, :], k)
                if k == 1:
                    ins = dve.scalar_tensor_tensor(dst, src, dsum[:, t:t + 1], dst, ALU.add, ALU.add)
                else:
                    ins = dve.tensor_tensor(dst, src, dst, ALU.add)
                ins.then_inc(s_add, 1)
            for q in range(T * NC):
                t, c = divmod(q, NC)
                dve.wait_ge(s_mean, q + 1)
                o = (q % 8) * BANK
                cs = slice(c * CH, (c + 1) * CH)
                dve.tensor_tensor(iv[:, t, cs], Y[:, t, cs], ps[:, o:o + CH], ALU.subtract).then_inc(s_yc, 1)
            for c in range(NC):
                cs = slice(c * CH, (c + 1) * CH)
                dve.wait_ge(s_var, c + 1)
                dve.tensor_scalar(var[:, cs], ps[0:B, c * BANK:c * BANK + CH], 1e-5, None, ALU.add).then_inc(s_eps, 1)
            for c in range(NC):
                cs = slice(c * CH, (c + 1) * CH)
                dve.wait_ge(s_eps, c + 1)
                dve.reciprocal(root[:, cs], var[:, cs]).then_inc(s_inv, 1)

            def normalise(c):
                for t in range(T):
                    q = c * T + t
                    dve.wait_ge(s_rep, q + 1)
                    cs = slice(c * CH, (c + 1) * CH)
                    dve.tensor_tensor(yk[:, t, cs], ps[:, (q % 8) * BANK:(q % 8) * BANK + CH], iv[:, t, cs], ALU.mult
                                      ).then_inc(s_n, 1)

            for c in range(NC + 1):
                if c < NC:
                    normalise(c)
                if c:
                    cs = slice((c - 1) * CH, c * CH)
                    dve.wait_ge(s_aff, T * c)
                    last = dve.tensor_tensor(Y[:, :, cs], yk[:, :, cs], Z[:, :, cs], ALU.mult)
            step(last)


def l0_ffn(nc, ps, X, U, acc, w):
    OT = 2 * E // 128
    SUMS = [0 if j == 0 else 3 if j % 2 else 2 for j in range(B * OT)]
    own = [TAPS - 1 - n for n in SUMS]
    pool_before = [sum(SUMS[:j]) for j in range(B * OT + 1)]
    own_before = [sum(own[:j]) for j in range(B * OT + 1)]
    with ExitStack() as ctx:
        sb, sem = space(nc, ctx, "l0f")
        c1, c3, pr, c2, c3b, se1, se2, seb = (w[n] for n in ("c1", "c3", "ffn", "c2", "c3b", "se1", "se2", "seb"))
        sc = sb("sc", [128, 2, OT])
        bi = sb("bi", [128, 2, OT])
        t1, t2 = sb("t1", [128, 2, OT]), sb("t2", [128, 2, OT])
        pad = sb("pad", [128, 3, PW, PW])
        prod = sb("prod", [128, 2, L])
        t3 = sb("t3", [128, OT, L])
        to = sb("to", [C, B, L])
        m, s1, s2 = sb("m", [C, B, NC]), sb("s1", [C // 2, B]), sb("s2", [C, B])
        mean = sb("mean", [C, B])
        (s_dve, s_inv, s_root, s_bn, s_pad, s_c1, s_ev, s_tap, s_t3, s_c3, s_o, s_m, s_h, s_s1, s_g, s_e
         ) = map(sem, "dve inv root bn pad c1 ev tap t3 c3 o m h s1 g e".split())
        s_first, s_prod, s_sum = map(sem, "first prod sum".split())
        block = ctx.enter_context(nc.Block())

        feeds = [[(0, 128, 0), (0, 64, 1)], [(64, 128, 1), (0, 128, 2)]]
        tiles = [(b, ot) for b in range(B) for ot in range(OT)]

        @block.tensor
        def _(pe):
            def c1_tile(j):
                b, ot = tiles[j]
                for c in range(NC):
                    if j:
                        pe.wait_ge(s_ev, NC * (j - 1) + c + 1)
                    for f, (lo, hi, t) in enumerate(feeds[b]):
                        mm = pe.matmul(ps[:, c * BANK:c * BANK + CH], c1[lo:hi, t, ot * 128:(ot + 1) * 128],
                                       U[lo:hi, t, c * CH:(c + 1) * CH], start=(f == 0), stop=(f == 1))
                    mm.then_inc(s_c1, 1)

            def c3_first():
                pe.wait_ge(s_t3, OT)
                for c in range(NC):
                    if c >= 2:
                        pe.wait_ge(s_o, c - 1)
                    o = (6 + c % 2) * BANK
                    for ot in range(OT):
                        mm = pe.matmul(ps[0:C, o:o + CH], c3[:, ot, :], t3[:, ot, c * CH:(c + 1) * CH],
                                       start=(ot == 0), stop=(ot == OT - 1))
                    mm.then_inc(s_c3, 1)

            def c3_second():
                pe.wait_ge(s_ev, 2 * OT * NC)
                for ot in range(OT):
                    pe.wait_ge(s_t3, OT + ot + 1)
                    for c in range(NC):
                        mm = pe.matmul(ps[0:C, c * BANK:c * BANK + CH], c3[:, ot, :], t3[:, ot, c * CH:(c + 1) * CH],
                                       start=(ot == 0), stop=(ot == OT - 1))
                        if ot == OT - 1:
                            mm.then_inc(s_c3, 1)

            for j in range(OT + 3):
                c1_tile(j)
            c3_first()
            for j in range(OT + 3, 2 * OT):
                c1_tile(j)
            c3_second()
            pe.wait_ge(s_m, 1)
            pe.matmul(ps[0:C // 2, 6 * BANK:6 * BANK + B], se1[:, :], mean[:, :], start=True, stop=True).then_inc(s_h, 1)
            pe.wait_ge(s_s1, 1)
            pe.matmul(ps[0:C, 7 * BANK:7 * BANK + B], se2[:, :], s1[:, :], start=True, stop=True).then_inc(s_g, 1)

        @block.scalar
        def _(act):
            act.wait_ge(s_inv, 1)
            act.activation(sc[:, :, :], t1[:, :, :], ACT.Sqrt).then_inc(s_root, 1)
            act.wait_ge(s_bn, 1)
            act.wait_ge(s_pad, 3)

            def stage(j):
                b, ot = tiles[j]
                if j >= 3:
                    act.wait_ge(s_tap, own_before[j - 2])
                for c in range(NC):
                    act.wait_ge(s_c1, NC * j + c + 1)
                    act.activation(pad[:, j % 3, 1 + 8 * c:9 + 8 * c, 1:1 + W],
                                   ps[:, c * BANK:c * BANK + CH].rearrange("p (h w) -> p h w", w=W), ACT.Relu,
                                   scale=sc[:, 0, ot:ot + 1], bias=bi[:, 0, ot:ot + 1]).then_inc(s_ev, 1)
                act.wait_ge(s_ev, NC * (j + 1))
                for i in range(SUMS[j] + 1):
                    dy, dx = divmod(i, 3)
                    g = pool_before[j] + i - 1
                    if i and g >= 2:
                        act.wait_ge(s_sum, g - 1)
                    dst = prod[:, g % 2, :] if i else acc[:, j % 3, :]
                    act.activation(by_image(dst), pad[:, j % 3, dy:dy + H, dx:dx + W], ACT.Copy,
                                   scale=c2[:, ot, i:i + 1]).then_inc(s_prod if i else s_first, 1)

            def finish(j):
                b, ot = tiles[j]
                act.wait_ge(s_tap, own_before[j + 1])
                if b:
                    act.wait_ge(s_c3, NC)
                act.activation(t3[:, ot, :], acc[:, j % 3, :], ACT.Relu, scale=sc[:, 1, ot:ot + 1],
                               bias=bi[:, 1, ot:ot + 1]).then_inc(s_t3, 1)

            def out(b):
                for c in range(NC):
                    q = b * NC + c
                    act.wait_ge(s_c3, q + 1)
                    o = (c if b else 6 + c % 2) * BANK
                    act.activation(to[:, b, c * CH:(c + 1) * CH], ps[0:C, o:o + CH], ACT.Identity,
                                   bias=c3b[:, :], accum_out=m[:, b, c:c + 1]).then_inc(s_o, 1)

            for j in range(3):
                stage(j)
            for j in range(2 * OT):
                finish(j)
                if j + 3 < 2 * OT:
                    stage(j + 3)
                if j == OT - 1:
                    out(0)
            out(1)
            act.wait_ge(s_h, 1)
            act.activation(s1[:, :], ps[0:C // 2, 6 * BANK:6 * BANK + B], ACT.Relu, bias=seb[0:C // 2, 0:1]).then_inc(s_s1, 1)
            act.wait_ge(s_g, 1)
            act.activation(s2[:, :], ps[0:C, 7 * BANK:7 * BANK + B], ACT.Sigmoid, bias=seb[:, 1:2]).then_inc(s_e, 1)

        @block.vector
        def _(dve):
            step = Steps(dve, s_dve)
            for i in range(3):
                dve.memset(pad[:, i, :, :], 0.0).then_inc(s_pad, 1)
            p = pr[:, :, :].rearrange("p o (h q) -> p h o q", h=2)
            step(dve.tensor_scalar(t2[:, :, :], p[:, :, :, 4], 1e-5, None, ALU.add))
            dve.reciprocal(t1[:, :, :], t2[:, :, :]).then_inc(s_inv, 1)
            dve.wait_ge(s_root, 1)
            step(dve.tensor_tensor(t1[:, :, :], sc[:, :, :], sc[:, :, :], ALU.mult))
            step(dve.tensor_tensor(t1[:, :, :], t1[:, :, :], t2[:, :, :], ALU.mult))
            step(dve.tensor_scalar(t1[:, :, :], t1[:, :, :], -0.5, 1.5, ALU.mult, ALU.add))
            step(dve.tensor_tensor(sc[:, :, :], sc[:, :, :], t1[:, :, :], ALU.mult))
            step(dve.tensor_tensor(sc[:, :, :], sc[:, :, :], p[:, :, :, 1], ALU.mult))
            step(dve.tensor_tensor(t1[:, :, :], p[:, :, :, 0], p[:, :, :, 3], ALU.subtract))
            step(dve.tensor_tensor(t1[:, :, :], t1[:, :, :], sc[:, :, :], ALU.mult))
            dve.tensor_tensor(bi[:, :, :], t1[:, :, :], p[:, :, :, 2], ALU.add).then_inc(s_bn, 1)
            for j, (b, ot) in enumerate(tiles):
                dve.wait_ge(s_first, j + 1)
                if SUMS[j]:
                    dve.wait_ge(s_sum, pool_before[j + 1])
                dst = by_image(acc[:, j % 3, :])
                for n, i in enumerate(range(SUMS[j] + 1, TAPS)):
                    dy, dx = divmod(i, 3)
                    if n:
                        dve.wait_ge(s_tap, own_before[j] + n)
                    dve.scalar_tensor_tensor(dst, pad[:, j % 3, dy:dy + H, dx:dx + W], c2[:, ot, i:i + 1], dst,
                                             ALU.mult, ALU.add).then_inc(s_tap, 1)
            dve.wait_ge(s_o, B * NC)
            step(dve.tensor_reduce(mean[:, :], m[:, :, :], AX.X, ALU.add))
            dve.tensor_scalar(mean[:, :], mean[:, :], 1.0 / L, None, ALU.mult).then_inc(s_m, 1)
            dve.wait_ge(s_e, 1)
            step(dve.tensor_scalar(s2[:, :], s2[:, :], 1.0, None, ALU.add))
            for b in range(B):
                step(dve.scalar_tensor_tensor(X[:, b, :], to[:, b, :], s2[:, b:b + 1], X[:, b, :], ALU.mult, ALU.add))

        @block.gpsimd
        def _(pool):
            for j in range(B * OT):
                for n in range(SUMS[j]):
                    g = pool_before[j] + n
                    if not n:
                        pool.wait_ge(s_first, j + 1)
                    else:
                        pool.wait_ge(s_sum, g)
                    pool.wait_ge(s_prod, g + 1)
                    pool.tensor_tensor(acc[:, j % 3, :], acc[:, j % 3, :], prod[:, g % 2, :], ALU.add
                                       ).then_inc(s_sum, 1)




def l1_pairs(nc, a, ps, X, pad, d):
    with ExitStack() as ctx:
        sb, sem = space(nc, ctx, "l1")
        wa = sb("wa", [128, PT, C])
        bias = sb("bias", [C, 1])
        rows, p = sb("rows", [C, B, PW, W]), sb("p", [C, B, L])
        base = sb("base", [128, 3, L])
        other = sb("other", [128, 3, L])
        prod = sb("prod", [128, 3, L])
        credit = sb("credit", [1, 3])
        s_w, s_edge, s_sum, s_sump, s_p, s_pd, s_prod, s_used, s_out = map(
            sem, "w edge sum sump p pd prod used out".split())
        s_base = [sem(f"base{i}") for i in range(3)]
        s_slot = [sem(f"slot{i}") for i in range(3)]
        reads = []
        for i in range(PT):
            lo, hi, part = 128 * i, min(128 * i + 128, PAIR_ROWS), []
            while lo < hi:
                end = min(hi, (lo // C + 1) * C)
                part.append((lo - 128 * i, end - lo, lo % C + lo // C))
                lo = end
            reads.append(part)
        last = [max(i for i in range(PT) if i % 3 == s) + 1 - PT for s in range(3)]
        height = [sum(n for _, n, _ in part) for part in reads]
        nslot = [sum(len(reads[i]) for i in range(s, PT, 3)) for s in range(3)]
        upto = [sum(len(reads[j]) for j in range(i % 3, i + 1, 3)) for i in range(PT)]
        block = ctx.enter_context(nc.Block())

        def box(step, eng, b):
            step(eng.tensor_tensor(rows[:, b, :, :], pad[:, b, :, 0:W], pad[:, b, :, 1:1 + W], ALU.add))
            step(eng.tensor_tensor(rows[:, b, :, :], rows[:, b, :, :], pad[:, b, :, 2:2 + W], ALU.add))
            step(eng.tensor_tensor(by_image(p[:, b, :]), rows[:, b, 0:H, :], rows[:, b, 1:1 + H, :], ALU.add))
            step(eng.tensor_tensor(by_image(p[:, b, :]), by_image(p[:, b, :]), rows[:, b, 2:2 + H, :], ALU.add))

        @block.sync
        def _(sp):
            sp.dma_start(wa[:, :, :], d["pairs"]).then_inc(s_w, 16)
            sp.dma_start(bias[:, :], a["l1b"]).then_inc(s_w, 16)
            with sp.Fori(0, B) as b:
                sp.wait_ge(s_pd, (b + 1) * 32)
                sp.wait_ge(s_prod, b * PT + 1)
                for i in range(PT):
                    if i < 3:
                        d0 = 128 * i % C
                        sp.dma_start(base[:, i, :], d["pd"][d0:d0 + 128, b, :]).then_inc(s_base[i], 16)
                    else:
                        sp.wait_ge(s_prod, b * PT + i - 1)
                    for lo, n, src in reads[i]:
                        sp.dma_start(other[lo:lo + n, i % 3, :], d["pd"][src:src + n, b, :]
                                     ).then_inc(s_slot[i % 3], 16)

        @block.gpsimd
        def _(pool):
            pool.wait_ge(s_edge, 1)
            box(Steps(pool, s_sump), pool, 1)

        @block.scalar
        def _(act):
            for b, s_box in enumerate((s_sum, s_sump)):
                act.wait_ge(s_box, 4)
                act.mul(p[:, b, :], p[:, b, :], 1.0 / 9.0).then_inc(s_p, 1)
                act.wait_ge(s_p, b + 1)
                if b:
                    act.wait_ge(s_pd, 32)
                for i in range(2):
                    act.dma_start(d["pd"][i * C:(i + 1) * C, b, :], p[:, b, :]).then_inc(s_pd, 16)
            act.wait_ge(s_pd, 64)

        @block.vector
        def _(dve):
            for b in range(B):
                dve.memset(pad[:, b, 0:PW:PW - 1, :], 0.0)
                ins = dve.memset(pad[:, b, 1:1 + H, 0:PW:PW - 1], 0.0)
            ins.then_inc(s_edge, 1)
            dve.memset(credit[:, 0:1], 0.0).then_inc(s_out, 1)
            dve.memset(credit[:, 1:2], 0.0).then_inc(s_prod, 1)
            dve.memset(credit[:, 2:3], 0.0).then_inc(s_used, 3)
            dve.wait_ge(s_edge, 1)
            box(Steps(dve, s_sum), dve, 0)
            dve.wait_ge(s_w, 32)
            with dve.Fori(0, B) as b:
                for i in range(PT):
                    s, n = i % 3, height[i]
                    if i < 3:
                        dve.wait_ge(s_base[i], (b + 1) * 16)
                    dve.wait_ge(s_slot[s], b * (16 * nslot[s]) + 16 * upto[i])
                    dve.wait_ge(s_used, b * PT + 3 + (i - 2 if i >= 3 else last[i]))
                    dve.tensor_tensor(prod[0:n, s, :], base[0:n, s, :], other[0:n, s, :], ALU.mult
                                      ).then_inc(s_prod, 1)
                dve.wait_ge(s_used, b * PT + PT + 3)
                xb = X[:, b, :].rearrange("p (c n) -> p c n", n=CH)
                dve.scalar_tensor_tensor(xb, banks(ps, 0, NC)[0:C], bias[:, :], xb, ALU.add, ALU.add
                                         ).then_inc(s_out, 1)
            dve.wait_ge(s_out, B + 1)

        @block.tensor
        def _(pe):
            pe.wait_ge(s_w, 32)
            with pe.Fori(0, B) as b:
                pe.wait_ge(s_out, b + 1)
                for i in range(PT):
                    pe.wait_ge(s_prod, b * PT + i + 2)
                    for c in range(NC):
                        mm = pe.matmul(ps[0:C, c * BANK:c * BANK + CH], wa[0:height[i], i, :],
                                       prod[0:height[i], i % 3, c * CH:(c + 1) * CH],
                                       start=(i == 0), stop=(i == PT - 1))
                    mm.then_inc(s_used, 1)



KS = 9
RAD = KS // 2
DW = W + 2 * RAD
HH = H // 2
HL = HH * W
DT = 2 * B * C // 128
DVE_TAPS, POOL_TAPS = 36, 19


def l2_diffuse(nc, a, ps, X, pad, ident):
    al = 0.65
    c1 = 1.0 / math.gamma(1.0 + 1.0 / al)
    c2 = math.sqrt(2.0 * c1)
    val = 3.0 * (-2.0 + (1.0 + 2.0 * al) * c2) / ((1.0 + 2.0 * al) * (-2.0 * c1 + 3.0 * c2))
    gauss_k = val / (4.0 * math.pi * c1)
    poi_k = (1.0 - val) * math.gamma(1.5) / math.pi ** 1.5 * c2
    NT = KS * KS
    NPE = NT - DVE_TAPS - POOL_TAPS
    dve_taps = list(range(DVE_TAPS))
    pool_taps = list(range(DVE_TAPS, DVE_TAPS + POOL_TAPS))
    pe_taps = list(range(DVE_TAPS + POOL_TAPS, NT))
    NPR = 4
    assert 2 * POOL_TAPS >= NPE
    NB = HL // CH
    pieces = []
    for g in range(2 * B):
        lo = g * C
        while lo < (g + 1) * C:
            hi = min((g + 1) * C, (lo // 128 + 1) * 128)
            pieces.append((lo // 128, lo % 128, lo - g * C, hi - lo, g // 2, g % 2))
            lo = hi
    npieces = [sum(p[0] == t for p in pieces) for t in range(DT)]
    with ExitStack() as ctx:
        sb, sem = space(nc, ctx, "l2")
        yg = sb("yg", [128, 2, NT])
        dm = sb("dm", [128, DT, 4])
        z, z2 = sb("z", [128, DT, 2, NT]), sb("z2", [128, DT, 2, NT])
        r2, q, ex, root, t = (sb(n, [128, DT, NT]) for n in ("r2", "q", "ex", "root", "t"))
        kern = sb("kern", [128, DT, NT])
        diag = sb("diag", [128, DT, NPE, 128])
        rows = sb("rows", [128, DT, HH + 2 * RAD, DW])
        acc, accp = sb("acc", [128, DT, HL]), sb("accp", [128, DT, HL])
        prod = sb("prod", [128, NPR, HL])
        back = sb("back", [C, B, L])
        s_in, s_edge, s_dve, s_r2, s_q, s_ex, s_root, s_kern, s_diag, s_tap, s_ptap, s_pe, s_sum, s_all, s_back = map(
            sem, "in edge dve r2 q ex root kern diag tap ptap pe sum all back".split())
        s_prod = sem("prod")
        s_rows = [sem(f"rows{i}") for i in range(DT)]
        block = ctx.enter_context(nc.Block())

        def half(tile, tl):
            return tile[:, tl, :].rearrange("p (h w) -> p h w", w=W)

        @block.sync
        def _(sp):
            sp.dma_start(yg[:, :, :], a["grid"]).then_inc(s_in, 16)
            sp.dma_start(dm[:, :, :], a["dm"]).then_inc(s_in, 16)
            for tl, p0, ch0, n, b, hf in pieces:
                sp.wait_ge(s_edge, b + 1)
                sp.dma_start(rows[p0:p0 + n, tl, :, :],
                             pad[ch0:ch0 + n, b, hf * HH:hf * HH + HH + 2 * RAD, :]).then_inc(s_rows[tl], 16)
            for tl, p0, ch0, n, b, hf in pieces:
                sp.wait_ge(s_all, tl + 1)
                sp.dma_start(back[ch0:ch0 + n, b, hf * HL:(hf + 1) * HL], acc[p0:p0 + n, tl, :]).then_inc(s_back, 16)
            sp.wait_ge(s_in, 32)

        @block.gpsimd
        def _(pool):
            for b in range(B):
                for lo, hi in ((0, RAD), (RAD + H, DW)):
                    pool.memset(pad[:, b, lo:hi, :], 0.0)
                    ins = pool.memset(pad[:, b, RAD:RAD + H, lo:hi], 0.0)
                ins.then_inc(s_edge, 1)
            for tl in range(DT):
                for i in range(1, POOL_TAPS):
                    g = tl * (POOL_TAPS - 1) + i - 1
                    pool.wait_ge(s_prod, tl * POOL_TAPS + i + 1)
                    if i > 1:
                        pool.wait_ge(s_ptap, g)
                    pool.tensor_tensor(accp[:, tl, :], accp[:, tl, :], prod[:, g % NPR, :], ALU.add
                                       ).then_inc(s_ptap, 1)

        @block.scalar
        def _(act):
            act.wait_ge(s_r2, 1)
            act.activation(ex[:, :, :], r2[:, :, :], ACT.Exp, scale=-1.0 / (4.0 * c1)).then_inc(s_ex, 1)
            act.wait_ge(s_q, 1)
            act.activation(root[:, :, :], q[:, :, :], ACT.Sqrt).then_inc(s_root, 1)
            act.wait_ge(s_kern, 1)

            def diagonal(tl, i):
                act.activation(diag[:, tl, i, :], ident[:, :], ACT.Copy, scale=kern[:, tl, pe_taps[i]:pe_taps[i] + 1]
                               ).then_inc(s_diag, 1)

            for i in range(NPE):
                diagonal(0, i)
            for tl in range(DT):
                act.wait_ge(s_rows[tl], 16 * npieces[tl])
                for i, tap in enumerate(pool_taps):
                    dy, dx = divmod(tap, KS)
                    g = tl * (POOL_TAPS - 1) + i - 1
                    if i and g >= NPR:
                        act.wait_ge(s_ptap, g - NPR + 1)
                    dst = half(prod, g % NPR) if i else half(accp, tl)
                    act.activation(dst, rows[:, tl, dy:dy + HH, dx:dx + W], ACT.Copy,
                                   scale=kern[:, tl, tap:tap + 1]).then_inc(s_prod, 1)
                    for e in range(2 * i, min(2 * i + 2, NPE)):
                        if tl + 1 < DT:
                            diagonal(tl + 1, e)

        @block.vector
        def _(dve):
            dve.wait_ge(s_in, 32)
            step = Steps(dve, s_dve)
            for i in range(2):
                for tl in range(DT):
                    dve.tensor_scalar(z[:, tl, i, :], yg[:, 0, :], dm[:, tl, 2 * i:2 * i + 1], None, ALU.mult
                                      ).then_inc(s_dve, 1)
                    step.n += 1
            dve.wait_ge(s_dve, step.n)
            for i in range(2):
                for tl in range(DT):
                    dve.scalar_tensor_tensor(z[:, tl, i, :], yg[:, 1, :], dm[:, tl, 2 * i + 1:2 * i + 2],
                                             z[:, tl, i, :], ALU.mult, ALU.add).then_inc(s_dve, 1)
                    step.n += 1
            dve.wait_ge(s_dve, step.n)
            step(dve.tensor_tensor(z2[:, :, :, :], z[:, :, :, :], z[:, :, :, :], ALU.mult))
            dve.tensor_tensor(r2[:, :, :], z2[:, :, 0, :], z2[:, :, 1, :], ALU.add).then_inc(s_r2, 1)
            dve.wait_ge(s_r2, 1)
            dve.tensor_scalar(q[:, :, :], r2[:, :, :], c2 * c2, None, ALU.add).then_inc(s_q, 1)
            dve.wait_ge(s_root, 1)
            step(dve.reciprocal(t[:, :, :], root[:, :, :]))
            step(dve.tensor_tensor(t[:, :, :], t[:, :, :], q[:, :, :], ALU.mult))
            step(dve.tensor_tensor(root[:, :, :], root[:, :, :], t[:, :, :], ALU.add))
            step(dve.tensor_tensor(t[:, :, :], root[:, :, :], q[:, :, :], ALU.mult))
            step(dve.reciprocal(root[:, :, :], t[:, :, :]))
            step(dve.tensor_scalar(root[:, :, :], root[:, :, :], 2.0 * poi_k, None, ALU.mult))
            dve.wait_ge(s_ex, 1)
            dve.scalar_tensor_tensor(kern[:, :, :], ex[:, :, :], gauss_k, root[:, :, :], ALU.mult, ALU.add
                                     ).then_inc(s_kern, 1)
            dve.wait_ge(s_kern, 1)

            def merge(tl):
                dve.wait_ge(s_pe, tl + 1)
                dve.tensor_tensor(acc[:, tl, :].rearrange("p (c n) -> p c n", n=CH), banks(ps, NB * (tl % 2), NB),
                                  acc[:, tl, :].rearrange("p (c n) -> p c n", n=CH), ALU.add).then_inc(s_sum, 1)
                dve.wait_ge(s_sum, tl + 1)
                dve.wait_ge(s_ptap, (POOL_TAPS - 1) * (tl + 1))
                dve.tensor_tensor(acc[:, tl, :], accp[:, tl, :], acc[:, tl, :], ALU.add).then_inc(s_all, 1)

            count = 0
            for tl in range(DT):
                dve.wait_ge(s_rows[tl], 16 * npieces[tl])
                for i, tap in enumerate(dve_taps):
                    dy, dx = divmod(tap, KS)
                    src = rows[:, tl, dy:dy + HH, dx:dx + W]
                    if i == 0:
                        ins = dve.tensor_scalar(half(acc, tl), src, kern[:, tl, tap:tap + 1], None, ALU.mult)
                    else:
                        dve.wait_ge(s_tap, count)
                        ins = dve.scalar_tensor_tensor(half(acc, tl), src, kern[:, tl, tap:tap + 1], half(acc, tl),
                                                       ALU.mult, ALU.add)
                    ins.then_inc(s_tap, 1)
                    count += 1
                    if tl and i == 5:
                        merge(tl - 1)
            dve.wait_ge(s_tap, count)
            merge(DT - 1)
            dve.wait_ge(s_back, 16 * len(pieces))
            for b in range(B):
                step(dve.tensor_tensor(X[:, b, :], back[:, b, :], X[:, b, :], ALU.add))

        @block.tensor
        def _(pe):
            for tl in range(DT):
                pe.wait_ge(s_rows[tl], 16 * npieces[tl])
                if tl >= 2:
                    pe.wait_ge(s_sum, tl - 1)
                for i, tap in enumerate(pe_taps):
                    pe.wait_ge(s_diag, tl * NPE + i + 1)
                    dy, dx = divmod(tap, KS)
                    for c in range(NB):
                        o = (NB * (tl % 2) + c) * BANK
                        mm = pe.matmul(ps[:, o:o + CH], diag[:, tl, i, :],
                                       rows[:, tl, dy + 8 * c:dy + 8 * c + 8, dx:dx + W],
                                       start=(i == 0), stop=(i == NPE - 1))
                mm.then_inc(s_pe, 1)



HC = 4 * HID
O_SP, O_AL, O_FR, O_FF = 0, 2 * C3, 2 * C3 + 1, 2 * C3 + 1 + 4 * C3
GO = O_FF + 4 * C3
BC = B * C3
FJ = 10
FCH = [(j, min(j + FJ, H)) for j in range(0, H, FJ)]


def l3_gates(nc, a, ps, st, wg, bw, w0g, cs, d, XG, G0, tr):
    with ExitStack() as ctx:
        sb, sem = space(nc, ctx, "l3g")
        gap = sb("gap", [C, B])
        w1, b1 = sb("w1", [C, HC]), sb("b1", [HC, 1])
        w2, b2 = sb("w2", [HC, GO]), sb("b2", [1, GO])
        one = sb("one", [1, C3])
        hid = sb("hid", [HC, B])
        row = sb("row", [1, B, GO])
        wt = sb("wt", [BC, 2, 2, 2 * C3])
        w0 = sb("w0", [3 * C3, B, 3, C3])
        gate = sb("gate", [BC, 2, 2, 2 * C3])
        gate0 = sb("gate0", [3 * C3, B, C3])
        lv = sb("lv", [BC, H])
        al = sb("al", [BC, 1])
        turns, fr = sb("turns", [BC, 2, H]), sb("fr", [BC, 2, H])
        whole = sb("whole", [BC, 2, H], I32)
        (s_in, s_dve, s_gap, s_hid, s_hs, s_row, s_rs, s_gate, s_gs, s_als, s_fr, s_cs, s_x
         ) = map(sem, "in dve gap hid hs row rs gate gs als fr cs x".split())
        s_tr, s_zero, s_spread = map(sem, "tr zero spread".split())
        NIN = 8
        block = ctx.enter_context(nc.Block())

        @block.sync
        def _(sp):
            sp.dma_start(d["g"].rearrange("c b l -> c (b l)"), XG[C3:C, :, :].rearrange("c b l -> c (b l)")
                         ).then_inc(s_x, 16)
            for dst, src in ((w1[:, :], "w1"), (b1[:, :], "b1"), (w2[:, :], "w2"), (b2[:, :], "b2"),
                             (wt[:, :, :, :], "wt"), (w0[:, :, :, :], "w0"), (lv[:, :], "lv"),
                             (bw[:, :, :, :], "bw")):
                sp.dma_start(dst, a[src]).then_inc(s_in, 16)
            for name in ("fh", "fw", "ef"):
                sp.dma_start(tr[name], a[name]).then_inc(s_tr, 16)
            sp.wait_ge(s_x, 16)
            for f in (1, 0):
                for b in range(B):
                    sp.dma_start(tr["xh"][:, f, C3 * b:C3 * b + C3, :],
                                 d["g"][C3 * f:C3 * f + C3, b, :].rearrange("c (h w) -> h c w", w=W)
                                 ).then_inc(s_tr, 16)
            sp.wait_ge(s_zero, 1)
            for i in range(3):
                lo, hi = max(0, i - 1), W + min(0, i - 1)
                for b in range(B):
                    sp.dma_start(G0[C3 * i:C3 * i + C3, b, 1:1 + H, lo + 1 - i:hi + 1 - i],
                                 by_image(XG[0:C3, b, :])[:, :, lo:hi]).then_inc(s_spread, 16)
            sp.wait_ge(s_in, 16 * NIN)
            sp.wait_ge(s_tr, 16 * (3 + 2 * B))
            sp.wait_ge(s_spread, 96)

        @block.gpsimd
        def _(pool):
            pool.memset(G0[:, :, :, :], 0.0).then_inc(s_zero, 1)

        @block.tensor
        def _(pe):
            pe.wait_ge(s_in, 16 * NIN)
            pe.wait_ge(s_gap, 1)
            pe.matmul(ps[0:HC, 0:B], w1[:, :], gap[:, :], start=True, stop=True).then_inc(s_hid, 1)
            pe.wait_ge(s_hs, 1)
            for b in range(B):
                pe.matmul(ps[0:1, (1 + b) * BANK:(1 + b) * BANK + GO], hid[:, b:b + 1], w2[:, :],
                          start=True, stop=False)
                mm = pe.matmul(ps[0:1, (1 + b) * BANK:(1 + b) * BANK + GO], one[:, 0:1], b2[:, :],
                               start=False, stop=True)
            mm.then_inc(s_row, 1)
            pe.wait_ge(s_rs, 1)
            for b in range(B):
                for f, o in enumerate((O_FR, O_FF)):
                    for p in range(2):
                        mm = pe.matmul(ps[C3 * b:C3 * b + C3, (3 + 2 * f + p) * BANK:(3 + 2 * f + p) * BANK + 2 * C3],
                                       row[:, b, o + 2 * C3 + p * C3:o + 2 * C3 + (p + 1) * C3],
                                       row[:, b, o:o + 2 * C3], start=True, stop=True)
            for b in range(B):
                for i in range(3):
                    pe.matmul(ps[C3 * i:C3 * i + C3, (7 * b) * BANK:(7 * b) * BANK + C3],
                              row[:, b, O_SP + C3:O_SP + 2 * C3], row[:, b, O_SP:O_SP + C3], start=True, stop=True)
            for b in range(B):
                mm = pe.matmul(ps[C3 * b:C3 * b + C3, BANK:BANK + 1], one[:, :], row[:, b, O_AL:O_AL + 1],
                               start=True, stop=True)
            mm.then_inc(s_gate, 1)

        @block.scalar
        def _(act):
            act.wait_ge(s_in, 16 * NIN)
            act.wait_ge(s_hid, 1)
            act.activation(hid[:, :], ps[0:HC, 0:B], ACT.Relu, bias=b1[:, :]).then_inc(s_hs, 1)
            act.wait_ge(s_row, 1)
            act.copy(row[:, :, :], ps[0:1, BANK:3 * BANK].rearrange("p (b n) -> p b n", b=B)[:, :, 0:GO]
                     ).then_inc(s_rs, 1)
            act.wait_ge(s_gate, 1)
            act.activation(al[:, :], ps[0:BC, BANK:BANK + 1], ACT.Sigmoid).then_inc(s_als, 1)
            act.activation(gate[:, :, :, :].rearrange("p f i o -> p (f i) o"),
                           ps[0:BC, 3 * BANK:7 * BANK].rearrange("p (q n) -> p q n", n=BANK)[:, :, 0:2 * C3],
                           ACT.Sigmoid).then_inc(s_gs, 1)
            for b in range(B):
                act.activation(gate0[:, b, :], ps[0:3 * C3, 7 * b * BANK:7 * b * BANK + C3], ACT.Sigmoid
                               ).then_inc(s_gs, 1)
            act.wait_ge(s_fr, 1)
            act.activation(cs[:, :, :], fr[:, :, :], ACT.Sin, scale=2.0 * math.pi * (1.0 - 1e-7)).then_inc(s_cs, 1)

        @block.vector
        def _(dve):
            step = Steps(dve, s_dve)
            step(dve.memset(one[:, :], 1.0))
            step(dve.tensor_tensor(gap[:, :], st["mv"][:, :, 0], st["rstd"][:, :], ALU.mult))
            dve.tensor_tensor(gap[:, :], gap[:, :], st["shift"][:, :], ALU.add).then_inc(s_gap, 1)
            step(dve.memset(wg[:, :, :, :, :], 0.0))
            dve.wait_ge(s_als, 1)
            step(dve.tensor_scalar(al[:, :], al[:, :], 0.8, 0.1, ALU.mult, ALU.add))
            step(dve.tensor_scalar(turns[:, 0, :], lv[:, :], al[:, 0:1], 0.25, ALU.mult, ALU.mult))
            step(dve.tensor_scalar(turns[:, 1, :], turns[:, 0, :], 0.25, None, ALU.add))
            step(dve.tensor_copy(whole[:, :, :], turns[:, :, :]))
            step(dve.tensor_copy(fr[:, :, :], whole[:, :, :]))
            step(dve.tensor_tensor(turns[:, :, :], turns[:, :, :], fr[:, :, :], ALU.subtract))
            step(dve.tensor_scalar(fr[:, :, :], turns[:, :, :], 0.5, None, ALU.is_gt))
            dve.tensor_tensor(fr[:, :, :], turns[:, :, :], fr[:, :, :], ALU.subtract).then_inc(s_fr, 1)
            dve.wait_ge(s_gs, 3)
            dve.wait_ge(s_in, 16 * NIN)
            for f in range(2):
                for b in range(B):
                    rows = slice(C3 * b, C3 * b + C3)
                    dst = wg[rows, f, :, :, rows]
                    step(dve.tensor_tensor(dst, gate[rows, f, :, :].rearrange("p i (q o) -> p i q o", q=2),
                                           wt[rows, f, :, :].rearrange("p i (q o) -> p i q o", q=2), ALU.mult))
            for b in range(B):
                for i in range(3):
                    ins = dve.tensor_tensor(w0g[:, b, i, :], gate0[:, b, :], w0[:, b, i, :], ALU.mult)
            step(ins)
            dve.wait_ge(s_cs, 1)


def l3_forward(nc, a, ps, wg, bw, cs, d, tr, xbuf):
    with ExitStack() as ctx:
        sb, sem = space(nc, ctx, "l3f")
        xh, ef, fh, fw = tr["xh"], tr["ef"], tr["fh"], tr["fw"]
        e11 = sb("e11", [1, H * H])
        ones = sb("ones", [1, BANK])
        A1 = sb("A1", [W, BC, H])
        Xh, Zr, Zi = (sb(n, [BC, H, H]) for n in ("Xh", "Zr", "Zi"))
        Fz = sb("Fz", [BC, H, 2, UH])
        Mz = sb("Mz", [BC, H, 2, UH])
        M = xbuf[:, 0:2 * H * H].rearrange("p (q j k) -> p q j k", q=2, j=H)
        A2 = sb("A2", [W, BC, 2, H])
        ph = sb("ph", [BC, 2, H, H])
        s_in, s_one, s_mm, s_ev, s_z, s_m, s_dve, s_v, s_out = map(sem, "in one mm ev z m dve v out".split())
        s_mst = sem("mst")
        block = ctx.enter_context(nc.Block())

        @block.sync
        def _(sp):
            sp.dma_start(e11[:, :], a["e11"]).then_inc(s_in, 16)
            for i in range(2):
                sp.wait_ge(s_v, i + 1)
                sp.dma_start(d["V"][:, i, :, :], M[:, i, :, :]).then_inc(s_out, 16)
            sp.wait_ge(s_m, 1)
            sp.dma_start(d["M"].rearrange("p u i k -> p (u i k)"), Mz[:, :, :, :].rearrange("p u i k -> p (u i k)")
                         ).then_inc(s_mst, 16)
            sp.wait_ge(s_mst, 16)
            sp.wait_ge(s_in, 16)
            sp.wait_ge(s_out, 32)

        def rows_jobs():
            n = BANK // H
            for c in range(0, BC, n):
                cc = range(c, min(c + n, BC))
                yield ([(xh[:, 0, i, :], ef[:, :], (i - c) * H, H, True, True) for i in cc], W,
                       A1[:, c:c + len(cc), :].rearrange("p c h -> p (c h)"), None)
            n = BANK // (2 * H)
            for c in range(0, BC, n):
                cc = range(c, min(c + n, BC))
                yield ([(xh[:, 1, i, :], fh[:, :], (i - c) * 2 * H, 2 * H, True, True) for i in cc], W,
                       A2[:, c:c + len(cc), :, :].rearrange("p c i h -> p (c i h)"), None)

        def cols_jobs():
            for lo, hi in FCH:
                yield ([(A1[:, :, j], ef[:, :], (j - lo) * H, H, True, True) for j in range(lo, hi)], BC,
                       Xh[:, lo:hi, :].rearrange("p j k -> p (j k)"), float(H))
            for lo, hi in FCH:
                mms = []
                for u in range(lo, hi):
                    mms.append((A2[:, :, 0, u], fw[:, 0, :], (u - lo) * 2 * UH, 2 * UH, True, False))
                    mms.append((A2[:, :, 1, u], fw[:, 1, :], (u - lo) * 2 * UH, 2 * UH, False, True))
                yield mms, BC, Fz[:, lo:hi, :, :].rearrange("p u i k -> p (u i k)"), None

        def mix_jobs():
            for lo, hi in FCH:
                for q in range(2):
                    o = (hi - lo) * UH
                    yield ([(wg[:, 1, 0, q, :], Fz[:, lo:hi, 0, :], 0, o, True, False),
                            (wg[:, 1, 1, q, :], Fz[:, lo:hi, 1, :], 0, o, False, False),
                            (bw[:, 1, q, :], ones[:, 0:o], 0, o, False, True)], BC, Mz[:, lo:hi, q, :], None)

        def frac_jobs():
            for lo, hi in FCH:
                for q in range(2):
                    o = (hi - lo) * H
                    yield ([(wg[:, 0, 0, q, :], Zr[:, lo:hi, :].rearrange("p j k -> p (j k)"), 0, o, True, False),
                            (wg[:, 0, 1, q, :], Zi[:, lo:hi, :].rearrange("p j k -> p (j k)"), 0, o, False, False),
                            (bw[:, 0, q, :], e11[:, lo * H:hi * H], 0, o, False, True)], BC,
                           M[:, q, lo:hi, :].rearrange("p j k -> p (j k)"), None)

        phases = [list(g()) for g in (rows_jobs, cols_jobs, frac_jobs, mix_jobs)]

        @block.tensor
        def _(pe):
            pe.wait_ge(s_one, 1)
            q = 0
            for i, jobs in enumerate(phases):
                if i:
                    pe.wait_ge(s_ev, q)
                if i == 2:
                    pe.wait_ge(s_z, 2)
                    pe.wait_ge(s_in, 16)
                for mms, rows, _, _ in jobs:
                    if q >= 8:
                        pe.wait_ge(s_ev, q - 7)
                    for lhsT, rhs, at, n, start, stop in mms:
                        mm = pe.matmul(ps[0:rows, (q % 8) * BANK + at:(q % 8) * BANK + at + n], lhsT, rhs,
                                       start=start, stop=stop)
                    mm.then_inc(s_mm, 1)
                    q += 1

        @block.scalar
        def _(act):
            q = 0
            for i, jobs in enumerate(phases):
                for mms, rows, dst, scale in jobs:
                    act.wait_ge(s_mm, q + 1)
                    n = mms[-1][2] + mms[-1][3]
                    src = ps[0:rows, (q % 8) * BANK:(q % 8) * BANK + n]
                    if len(dst.shape) == 3:
                        src = src.rearrange("p (u k) -> p u k", k=UH)
                    if scale:
                        act.mul(dst, src, scale).then_inc(s_ev, 1)
                    else:
                        act.copy(dst, src).then_inc(s_ev, 1)
                    q += 1
                if i == 3:
                    act.wait_ge(s_ev, q)
                    act.copy(ones[:, 0:1], ones[:, 0:1]).then_inc(s_m, 1)

        @block.vector
        def _(dve):
            step = Steps(dve, s_dve)
            dve.memset(ones[:, :], 1.0).then_inc(s_one, 1)
            sj = [cs[:, i, :].unsqueeze(2).to_broadcast([BC, H, H]) for i in range(2)]
            sk = [cs[:, i, :].unsqueeze(1).to_broadcast([BC, H, H]) for i in range(2)]
            step(dve.tensor_tensor(Zr[:, :, :], sj[1], sk[1], ALU.mult))
            step(dve.tensor_tensor(Zi[:, :, :], sj[0], sk[0], ALU.mult))
            step(dve.tensor_tensor(ph[:, 0, :, :], Zr[:, :, :], Zi[:, :, :], ALU.subtract))
            step(dve.tensor_tensor(Zr[:, :, :], sj[0], sk[1], ALU.mult))
            step(dve.tensor_tensor(Zi[:, :, :], sj[1], sk[0], ALU.mult))
            step(dve.tensor_tensor(ph[:, 1, :, :], Zr[:, :, :], Zi[:, :, :], ALU.add))
            dve.wait_ge(s_ev, len(phases[0]) + len(FCH))
            dve.tensor_tensor(Zr[:, :, :], Xh[:, :, :], ph[:, 0, :, :], ALU.mult).then_inc(s_z, 1)
            dve.scalar_tensor_tensor(Zi[:, :, :], Xh[:, :, :], -1.0, ph[:, 1, :, :], ALU.mult, ALU.mult
                                     ).then_inc(s_z, 1)
            dve.wait_ge(s_ev, sum(map(len, phases[0:3])))
            step(dve.tensor_tensor(Zr[:, :, :], M[:, 1, :, :], ph[:, 1, :, :], ALU.mult))
            step(dve.tensor_tensor(Zi[:, :, :], M[:, 0, :, :], ph[:, 1, :, :], ALU.mult))
            for q, (t, op) in enumerate(((Zr, ALU.subtract), (Zi, ALU.add))):
                step(dve.tensor_tensor(M[:, q, :, :], M[:, q, :, :], ph[:, 0, :, :], ALU.mult))
                dve.tensor_tensor(M[:, q, :, :], M[:, q, :, :], t[:, :, :], op).then_inc(s_v, 1)


def l3_inverse(nc, a, ps, X, G0, w0g, d):
    with ExitStack() as ctx:
        sb, sem = space(nc, ctx, "l3i")
        Vj = sb("Vj", [H, BC, 2, H])
        Mu = sb("Mu", [H, BC, 2 * UH])
        ei = sb("ei", [H, H])
        ih, iw = sb("ih", [H, 2 * H]), sb("iw", [2 * UH, 2, W])
        A3 = sb("A3", [W, BC, 2, H])
        A4 = sb("A4", [2 * UH, BC, 2, H])
        O = A4[0:H]
        P2, F = sb("P2", [H, BC, W]), sb("F", [H, BC, W])
        cat = sb("cat", [C, B, PW, PW])
        w2 = sb("w2", [C, TAPS, C])
        b0, b2 = sb("b0", [C3, 1]), sb("b2", [C, 1])
        s_b0, s_in, s_V, s_edge, s_mm, s_ev, s_sum, s_root, s_fst, s_cf, s_pst, s_c2, s_x = map(
            sem, "b0 in V edge mm ev sum root fst cf pst c2 x".split())
        s_cp = [sem(f"cp{b}") for b in range(B)]
        NIN = 6
        block = ctx.enter_context(nc.Block())

        def conv0_jobs():
            for b in range(B):
                for c in range(NC):
                    yield ([(w0g[:, b, i, :], G0[:, b, i + 8 * c:i + 8 * c + 8, 0:W], 0, CH, i == 0, i == 2)
                            for i in range(3)], C3, cat[0:C3, b, 1 + 8 * c:9 + 8 * c, 1:1 + W], ACT.Identity)

        def jobs(kind):
            n = BANK // (2 * H)
            m = BANK // H
            if kind == 1:
                for c in range(0, BC, n):
                    cc = range(c, min(c + n, BC))
                    yield ([(Mu[:, i, :], ih[:, :], (i - c) * 2 * H, 2 * H, True, True) for i in cc], 2 * UH,
                           A4[:, c:c + len(cc), :, :].rearrange("p c i h -> p (c i h)"), ACT.Copy)
            if kind == 2:
                for c in range(0, BC, m):
                    cc = range(c, min(c + m, BC))
                    mms = []
                    for i in cc:
                        for q in range(2):
                            mms.append((A4[:, i, q, :], iw[:, q, :], (i - c) * W, W, q == 0, q == 1))
                    yield mms, H, F[:, c:c + len(cc), :].rearrange("p c w -> p (c w)"), ACT.Copy
            if kind == 3:
                for c in range(0, 2 * BC, m):
                    cc = range(c, min(c + m, 2 * BC))
                    yield ([(Vj[:, i // 2, i % 2, :], ei[:, :], (i - c) * H, H, True, True) for i in cc], H,
                           A3[:, :, :, :].rearrange("p c i h -> p (c i) h")[:, c:c + len(cc), :]
                           .rearrange("p c h -> p (c h)"), ACT.Copy)
            if kind == 4:
                for c in range(0, 2 * BC, m):
                    cc = range(c, min(c + m, 2 * BC))
                    yield ([(A3[:, i // 2, i % 2, :], ei[:, :], (i - c) * H, H, True, True) for i in cc], H,
                           O[:, :, :, :].rearrange("p c i h -> p (c i) h")[:, c:c + len(cc), :]
                           .rearrange("p c h -> p (c h)"), ACT.Square)

        phases = [list(conv0_jobs())] + [list(jobs(i)) for i in range(1, 5)]
        first = [sum(map(len, phases[:i])) for i in range(len(phases) + 1)]
        n_act = first[-1]
        squares = [first[4] + -(-2 * C3 * (b + 1) // (BANK // H)) for b in range(B)]

        @block.sync
        def _(sp):
            sp.dma_start(b0[:, :], a["cb0"]).then_inc(s_b0, 16)
            sp.dma_start(Mu[:, :, :], d["M"].rearrange("p u i k -> u p (i k)")).then_inc(s_in, 16)
            for dst, src in ((ih[:, :], "ih"), (iw[:, :, :], "iw"), (ei[:, :], "ei"), (w2[:, :, :], "cw2"),
                             (b2[:, :], "cb2")):
                sp.dma_start(dst, a[src]).then_inc(s_in, 16)
            for i in range(2):
                sp.dma_start(Vj[:, :, i, :], d["V"][:, i, :, :].rearrange("p j k -> j p k")).then_inc(s_V, 16)
            sp.wait_ge(s_ev, first[3])
            sp.dma_start(d["o"][1], F[:, :, :]).then_inc(s_fst, 16)
            sp.wait_ge(s_edge, 1)
            sp.wait_ge(s_fst, 16)
            for b in range(B):
                sp.dma_start(interior(cat[2 * C3:C, b, :, :]),
                             d["o"][1, :, C3 * b:C3 * b + C3, :].rearrange("h c w -> c h w")).then_inc(s_cf, 16)
            for b in range(B):
                rows = slice(C3 * b, C3 * b + C3)
                sp.wait_ge(s_root, b + 1)
                sp.dma_start(d["o"][0][:, rows, :], P2[:, rows, :]).then_inc(s_pst, 16)
                sp.wait_ge(s_pst, 16 * (b + 1))
                sp.dma_start(interior(cat[C3:2 * C3, b, :, :]),
                             d["o"][0, :, rows, :].rearrange("h c w -> c h w")).then_inc(s_cp[b], 16)
            sp.wait_ge(s_b0, 16)
            sp.wait_ge(s_in, 16 * NIN)
            sp.wait_ge(s_V, 32)
            sp.wait_ge(s_cf, 16 * B)

        @block.gpsimd
        def _(pool):
            pool.memset(cat[:, :, :, :], 0.0).then_inc(s_edge, 1)

        @block.tensor
        def _(pe):
            def bank_free(q):
                if q >= 8 + n_act:
                    pe.wait_ge(s_x, q - 7 - n_act)
                elif q >= 8:
                    pe.wait_ge(s_ev, q - 7)

            q = 0
            for i, job in enumerate(phases):
                if i == 1:
                    pe.wait_ge(s_in, 16 * NIN)
                if i == 3:
                    pe.wait_ge(s_V, 32)
                if i in (2, 4):
                    pe.wait_ge(s_ev, q)
                for mms, rows, _, _ in job:
                    bank_free(q)
                    for lhsT, rhs, at, n, start, stop in mms:
                        mm = pe.matmul(ps[0:rows, (q % 8) * BANK + at:(q % 8) * BANK + at + n], lhsT, rhs,
                                       start=start, stop=stop)
                    mm.then_inc(s_mm, 1)
                    q += 1
            pe.wait_ge(s_cf, 16 * B)
            for b in range(B):
                pe.wait_ge(s_cp[b], 16)
                for c in range(NC):
                    bank_free(q)
                    for i in range(TAPS):
                        dy, dx = divmod(i, 3)
                        mm = pe.matmul(ps[0:C, (q % 8) * BANK:(q % 8) * BANK + CH], w2[:, i, :],
                                       cat[:, b, dy + 8 * c:dy + 8 * c + 8, dx:dx + W], start=(i == 0),
                                       stop=(i == TAPS - 1))
                    mm.then_inc(s_c2, 1)
                    q += 1

        @block.scalar
        def _(act):
            def root(b):
                rows = slice(C3 * b, C3 * b + C3)
                act.wait_ge(s_sum, b + 1)
                act.activation(P2[:, rows, :], P2[:, rows, :], ACT.Sqrt, scale=1.0 / (H * W)).then_inc(s_root, 1)

            act.wait_ge(s_edge, 1)
            act.wait_ge(s_b0, 16)
            q = 0
            for job in phases:
                for mms, rows, dst, fn in job:
                    act.wait_ge(s_mm, q + 1)
                    n = mms[-1][2] + mms[-1][3]
                    src = ps[0:rows, (q % 8) * BANK:(q % 8) * BANK + n]
                    if fn == ACT.Identity:
                        act.activation(dst, src.rearrange("p (h w) -> p h w", w=W), fn, bias=b0[:, :]
                                       ).then_inc(s_ev, 1)
                    else:
                        act.activation(dst, src, fn).then_inc(s_ev, 1)
                    q += 1
                    if q == squares[0] + 1:
                        root(0)
            root(1)

        @block.vector
        def _(dve):
            for b in range(B):
                rows = slice(C3 * b, C3 * b + C3)
                dve.wait_ge(s_ev, squares[b])
                dve.tensor_tensor(P2[:, rows, :], O[:, rows, 0, :], O[:, rows, 1, :], ALU.add).then_inc(s_sum, 1)
            dve.wait_ge(s_in, 16 * NIN)
            for q in range(B * NC):
                b, c = divmod(q, NC)
                dve.wait_ge(s_c2, q + 1)
                xs = X[:, b, c * CH:(c + 1) * CH]
                o = ((n_act + q) % 8) * BANK
                dve.scalar_tensor_tensor(xs, ps[0:C, o:o + CH], b2[:, :], xs, ALU.add, ALU.add).then_inc(s_x, 1)


def l3(nc, a, ps, X, gavg, st):
    d = {"g": nc.dram_tensor("g3", (2 * C3, B, L), F32).ap(), "V": nc.dram_tensor("V", (BC, 2, H, H), F32).ap(),
         "M": nc.dram_tensor("M", (BC, H, 2, UH), F32).ap(), "o": nc.dram_tensor("o3", (2, H, BC, W), F32).ap()}
    with ExitStack() as ctx:
        sb, _ = space(nc, ctx, "l3")
        w0g = sb("w0g", [3 * C3, B, 3, C3])
        G0 = sb("G0", [3 * C3, B, PW, W])
        with ExitStack() as spectral:
            sb1, _ = space(nc, spectral, "l3w")
            wg = sb1("wg", [BC, 2, 2, 2, BC])
            bw = sb1("bw", [1, 2, 2, BC])
            cs = sb1("cs", [BC, 2, H])
            xbuf = sb1("xbuf", [BC, 2 * BC * W])
            ef = sb1("ef", [H, H])
            fh, fw = sb1("fh", [H, 2 * H]), sb1("fw", [H, 2, 2 * UH])
            tr = {"xh": xbuf[0:H, :].rearrange("p (f c w) -> p f c w", f=2, w=W), "ef": ef[:, :], "fh": fh[:, :],
                  "fw": fw[:, :, :]}
            with ExitStack() as early:
                XG = space(nc, early, "l3x")[0]("XG", [C, B, L])
                group_norm(nc, "gn3", X, ps, gavg, st, [by_image(XG[:, b, :]) for b in range(B)])
                l3_gates(nc, a, ps, st, wg, bw, w0g, cs, d, XG, G0, tr)
            l3_forward(nc, a, ps, wg, bw, cs, d, tr, xbuf)
        l3_inverse(nc, a, ps, X, G0, w0g, d)




def program(nc, a, x, out, layers=(0, 1, 2, 3)):
    with ExitStack() as ctx:
        sb, _ = space(nc, ctx, "net")
        ps = ctx.enter_context(nc.psum_tensor("ps", [128, 8 * BANK], F32))
        X = sb("X", [C, B, L])
        gavg = sb("gavg", [C, C])
        ident = sb("ident", [128, 128])
        st = {"mv": sb("mv", [C, B, 2]), "rstd": sb("rstd", [C, B]), "shift": sb("shift", [C, B])}
        load(nc, "x", [(X[:, :, :], x.rearrange("b c h w -> c b (h w)")), (gavg[:, :], a["gavg"]),
                       (ident[:, :], a["ident"])])
        pairs = nc.dram_tensor("pairs", (128, PT, C), F32).ap()
        if 0 in layers:
            d = {"dlt": nc.dram_tensor("dlt", (K * T, 128, L), F32).ap(),
                 "v": nc.dram_tensor("v", (K * T, 128, L), F32).ap(),
                 "y": nc.dram_tensor("y", (K * T, 128, L), F32).ap(),
                 "na": nc.dram_tensor("na", (K * T, 128, 2 * N), F32).ap(),
                 "pairs": pairs, "bc": nc.dram_tensor("bc", (K, 2, 3 * B * N, L), BF16).ap()}
            with ExitStack() as l0:
                sb0, _ = space(nc, l0, "l0")
                Z = sb0("Z", [128, T, L])
                with ExitStack() as early:
                    sb1, _ = space(nc, early, "l0e")
                    XI = sb1("XI", [128, T, L])
                    w = {n: sb1(n, a[n].shape) for n in ("w_bc", "w_dt", "A", "w_up", "dtb")}
                    with ExitStack() as first:
                        XG = space(nc, first, "l0x")[0]("XG", [C, B, L])
                        group_norm(nc, "gn0", X, ps, gavg, st, [by_image(XG[:, b, :]) for b in range(B)])
                        l0_project(nc, a, XG, ps, XI, Z, [(whole(w[n]), a[n]) for n in w])
                    P = sb1("P", [K * B * R, L])
                    l0_rows(nc, a, ps, XI, P, d, w["w_bc"], w["w_dt"], w["A"])
                    l0_steps(nc, ps, XI, P, d, w["w_up"], w["dtb"])
                l0_scan(nc, a, ps, ident, d)
                Y = sb0("Y", [128, T, L])
                w = {n: sb0(n, a[n].shape) for n in ("c1", "c3", "ffn", "c2", "c3b", "se1", "se2", "seb")}
                l0_norm(nc, a, ps, Z, Y, d, [(whole(w[n]), a[n]) for n in w])
                l0_ffn(nc, ps, X, Y, Z, w)
        if 1 in layers:
            with ExitStack() as l1:
                pad = space(nc, l1, "l1g")[0]("pad", [C, B, PW, PW])
                group_norm(nc, "gn1", X, ps, gavg, st, [interior(pad[:, b, :, :]) for b in range(B)])
                d = {"pairs": pairs, "pd": nc.dram_tensor("pd", (2 * C, B, L), F32).ap()}
                l1_pairs(nc, a, ps, X, pad, d)
        if 2 in layers:
            with ExitStack() as l2:
                pad = space(nc, l2, "l2g")[0]("pad", [C, B, DW, DW])
                group_norm(nc, "gn2", X, ps, gavg, st, [interior(pad[:, b, :, :], RAD) for b in range(B)])
                l2_diffuse(nc, a, ps, X, pad, ident)
        if 3 in layers:
            l3(nc, a, ps, X, gavg, st)
        load(nc, "out", [(out.rearrange("b c h w -> c b (h w)"), X[:, :, :])])


def row_tiles(x):
    x = np.concatenate([x] * B, axis=0)
    return np.ascontiguousarray(np.moveaxis(x.reshape(T, 128, *x.shape[1:]), 0, 1))


def layout(v):
    f = np.float32
    a = {}
    c = np.arange(C)
    a["gavg"] = ((c[:, None] // 3 == c[None, :] // 3) / 3).astype(f)
    a["ident"] = np.eye(128, dtype=f)
    p = "L0_conv_"
    a["w_in"] = np.ascontiguousarray(v[p + "in_proj_w"].T)
    a["cw"] = row_tiles(v[p + "conv_w"].reshape(E, TAPS))
    a["cb"] = row_tiles(v[p + "conv_b"])
    image = (np.arange(B * E) // E).reshape(T, 128)
    xp, dp = v[p + "x_proj_w"], v[p + "dt_proj_w"]
    w_bc = np.zeros((128, 2, T, 128), f)
    w_dt = np.zeros((128, T, K, B, R), f)
    w_up = np.zeros((K, B, R, T, K, 128), f)
    xe = row_tiles(np.ascontiguousarray(np.transpose(xp, (2, 0, 1))))
    de = row_tiles(np.ascontiguousarray(np.transpose(dp, (1, 0, 2))))
    for t in range(T):
        for b in range(B):
            rows = image[t] == b
            for k in range(K):
                w_dt[rows, t, k, b] = xe[rows, t, k, 0:R]
                w_up[k, b][:, t, k, rows] = de[rows, t, k].T
                for s in range(2):
                    o = 64 * (k % 2) + 32 * s + N * b
                    w_bc[rows, k // 2, t, o:o + N] = xe[rows, t, k, R + N * s:R + N * (s + 1)]
    a["w_bc"], a["w_dt"] = w_bc, w_dt.reshape(128, T, K * B * R)
    a["w_up"] = w_up.reshape(K * B * R, T * K, 128)
    a["dtb"] = row_tiles(np.ascontiguousarray(v[p + "dt_proj_b"].T))
    a["A"] = row_tiles(np.ascontiguousarray(np.transpose(v[p + "A_log"], (1, 0, 2)))).reshape(128, T * K, N)
    sel = np.zeros((T, 3, B, N, N, 128), f)
    for t in range(T):
        for b in range(B):
            for n in range(N):
                sel[t, :, b, n, n, image[t] == b] = 1
    a["sel"] = sel.reshape(T, 3 * B * N, N * 128).astype(mybir.dt.np(BF16))
    a["Ds"] = row_tiles(np.ascontiguousarray(v[p + "Ds"].T))
    a["gb"] = row_tiles(np.stack([v[p + "ln_g"], v[p + "ln_b"]], 1))
    avg = np.zeros((128, 7, 128), f)
    for i, (src, dst) in enumerate(((0, 0), (1, 0), (0, 1), (1, 1), (2, 1), (1, 2), (2, 2))):
        avg[:, i] = (image[src][:, None] == image[dst][None, :]) / E
    a["avg"] = avg
    of_image = (image[:, :, None] == np.arange(B)).astype(f)
    a["avgv"] = np.moveaxis(of_image / f(E), 0, 1)
    a["selv"] = np.moveaxis(of_image, 2, 0)
    a["c1"] = row_tiles(np.ascontiguousarray(v[p + "c1_w"].reshape(2 * E, E).T))
    per = lambda x: np.ascontiguousarray(np.moveaxis(x.reshape(2 * E // 128, 128, -1), 0, 1))
    a["c3"] = per(v[p + "c3_w"].reshape(C, 2 * E).T)
    a["c2"] = per(v[p + "c2_w"].reshape(2 * E, TAPS))
    a["ffn"] = per(np.stack([v[p + n] for n in ("c1_b", "bn1_g", "bn1_b", "bn1_m", "bn1_v",
                                                "c2_b", "bn2_g", "bn2_b", "bn2_m", "bn2_v")], 1))
    a["c3b"] = v[p + "c3_b"].reshape(C, 1)
    a["se1"] = np.ascontiguousarray(v[p + "se1_w"].T)
    a["se2"] = np.ascontiguousarray(v[p + "se2_w"].T)
    seb = np.zeros((C, 2), f)
    seb[0:C // 2, 0], seb[:, 1] = v[p + "se1_b"], v[p + "se2_b"]
    a["seb"] = seb
    i = np.arange(PT * 128)
    ci, cj = i % C, (i % C + i // C) % C
    keep = i < PAIR_ROWS
    for name, key in (("w", "weight"), ("m", "mask")):
        src = v["L1_conv_" + key]
        for n, (p0, p1) in (("a", (ci, cj)), ("b", (cj, ci))):
            g = np.where(keep[:, None], src[:, p0, p1].T, f(0))
            a[name + n] = np.ascontiguousarray(np.moveaxis(g.reshape(PT, 128, C), 0, 1))
    a["l1b"] = v["L1_conv_bias"].reshape(C, 1)
    yy = np.stack(np.divmod(np.arange(KS * KS), KS)) - RAD
    a["grid"] = np.ascontiguousarray(np.broadcast_to(yy.astype(f), (128, 2, KS * KS)))
    a["dm"] = np.moveaxis(np.tile(v["L2_conv_diff_metric"].reshape(C, 4), (2 * B, 1)).reshape(DT, 128, 4), 0, 1)
    layout3(v, a)
    return {k: np.ascontiguousarray(x) for k, x in a.items()}


def transform_basis(n):
    s = np.zeros(n)
    s[1] = s[n - 1] = 1.0
    idx = (np.arange(n)[:, None] - np.arange(n)[None, :]) % n
    S = s[idx] + np.diag(np.fft.fft(s).real)
    r, even = n // 2, 1 - n % 2
    P = np.zeros((n, n))
    P[0, 0] = 1.0
    for i in range(1, r - even + 1):
        P[i, i] = P[i, n - i] = 1 / math.sqrt(2)
    if even:
        P[r, r] = 1.0
    for i in range(r + 1, n):
        P[i, i], P[i, n - i] = -1 / math.sqrt(2), 1 / math.sqrt(2)
    CS = P @ S @ P.T
    h = n // 2 + 1
    ec, vc = np.linalg.eigh(CS[:h, :h])
    es, vs = np.linalg.eigh(CS[h:, h:])
    vc, vs = vc[:, np.argsort(-ec)], vs[:, np.argsort(-es)]
    c2, s2 = P @ np.vstack([vc, np.zeros((n - h, h))]), P @ np.vstack([np.zeros((h, n - h)), vs])
    e = np.zeros((n, n + 1))
    e[:, 0:n + 1:2] = c2
    e[:, 1:n:2] = np.hstack([s2, np.zeros((n, 1))])[:, 0:len(range(1, n, 2))]
    return np.delete(e, n - 1, axis=1)


def layout3(v, a):
    f = np.float32
    p = "L3_conv_"
    w1, b1 = np.zeros((C, HC), f), np.zeros((HC, 1), f)
    w2, b2 = np.zeros((HC, GO), f), np.zeros((1, GO), f)
    for i, (name, c0, o, n) in enumerate((("gsp", 0, O_SP, 2 * C3), ("alpha", C3, O_AL, 1),
                                          ("gfreq", C3, O_FR, 4 * C3), ("gfft", 2 * C3, O_FF, 4 * C3))):
        h = slice(i * HID, (i + 1) * HID)
        w1[c0:c0 + C3, h] = v[p + name + "_w1"].T
        b1[h, 0] = v[p + name + "_b1"]
        w2[h, o:o + n] = v[p + name + "_w2"].T
        b2[0, o:o + n] = v[p + name + "_b2"]
    a["w1"], a["b1"], a["w2"], a["b2"] = w1, b1, w2, b2
    wt = np.zeros((B, C3, 2, 2, 2 * C3), f)
    bw = np.zeros((1, 2, 2, B, C3), f)
    for i, name in enumerate(("conv05", "conv1")):
        wt[:, :, i] = v[p + name + "_w"].reshape(2 * C3, 2, C3).transpose(2, 1, 0)
        bw[:, i] = v[p + name + "_b"].reshape(2, 1, C3)
    a["wt"], a["bw"] = wt.reshape(BC, 2, 2, 2 * C3), bw.reshape(1, 2, 2, BC)
    w0 = v[p + "conv0_w"].transpose(3, 1, 2, 0).reshape(3 * C3, 1, 3, C3)
    a["w0"] = np.repeat(w0, B, axis=1)
    a["cw2"] = v[p + "conv2_w"].transpose(1, 2, 3, 0).reshape(C, TAPS, C)
    a["cb0"], a["cb2"] = v[p + "conv0_b"].reshape(C3, 1), v[p + "conv2_b"].reshape(C, 1)
    lv = np.arange(H)
    lv[-1] = H
    a["lv"] = np.broadcast_to(lv.astype(f), (BC, H))
    e = np.roll(transform_basis(H).astype(f).astype(np.float64), H // 2, axis=1)
    a["ef"], a["ei"] = e.T.astype(f), e.astype(f)
    a["e11"] = np.outer(e.sum(1), e.sum(1)).reshape(1, H * H).astype(f)
    i, k = np.arange(H), np.arange(UH)
    full, half = 2 * np.pi * np.outer(i, i) / H, 2 * np.pi * np.outer(i, k) / W
    a["fh"] = np.concatenate([np.cos(full), -np.sin(full)], 1).astype(f)
    a["fw"] = np.stack([np.concatenate([np.cos(half), -np.sin(half)], 1),
                        np.concatenate([np.sin(half), np.cos(half)], 1)], 1).astype(f)
    a["ih"] = np.concatenate([np.cos(full), np.sin(full)], 1).astype(f)
    wk = np.where((k == 0) | (k == W // 2), 1.0, 2.0)[:, None] / (H * W)
    c, s = wk * np.cos(half.T), wk * np.sin(half.T)
    a["iw"] = np.stack([np.concatenate([c, -s]), np.concatenate([-s, -c])], 1).astype(f)


_OUT = (B, C, H, W)


def kernel(**inputs):
    import concourse.bacc as bacc
    from concourse.bass_utils import run_bass_kernel_spmd

    v = {k: np.asarray(x) for k, x in inputs.items()}
    arrays = layout(v)
    nc = bacc.Bacc("TRN2", target_bir_lowering=False, num_devices=1)
    a, sent = {}, {}
    for name, arr in arrays.items():
        sent[f"in_{name}"] = arr
        a[name] = nc.dram_tensor(f"in_{name}", arr.shape, mybir.dt.from_np(arr.dtype), kind="ExternalInput").ap()
    sent["in_x"] = np.ascontiguousarray(v["x"])
    x = nc.dram_tensor("in_x", _OUT, F32, kind="ExternalInput").ap()
    out = nc.dram_tensor("out_0", _OUT, F32, kind="ExternalOutput").ap()
    program(nc, a, x, out)
    r = run_bass_kernel_spmd(nc, [sent], core_ids=[0])
    return r.results[0]["out_0"]
```
